# Optimizing a Trainium2 kernel written in Bass

```python
import numpy as np
import jax
import jax.numpy as jnp

def _softmax(x, axis=-1):
    return jax.nn.softmax(x, axis=axis)

def _gelu(x):
    return jax.nn.gelu(x, approximate=True)

def _silu(x):
    return jax.nn.silu(x)

def _sigmoid(x):
    return jax.nn.sigmoid(x)

def _layernorm(x, axis=-1, eps=1e-05):
    m = jnp.mean(x, axis=axis, keepdims=True)
    v = jnp.var(x, axis=axis, keepdims=True)
    return (x - m) / jnp.sqrt(v + eps)

def _scatter_add(tgt, idx, src, axis=0):
    return tgt.at[idx].add(src)

def _segment_sum(src, seg, n):
    return jax.ops.segment_sum(src, seg, n)
kernel_name = 'mk_flamingo_gated_d4_seqx_r4_88680c'

def setup_inputs(seed: int=0):
    np.random.seed(seed)
    _w = jnp.asarray

    def _rec_inputs():
        import jax
        import jax.numpy as jnp
        _rk = jax.random.key(seed)
        x = -0.0002928 + 1 * jax.random.normal(jax.random.fold_in(_rk, 1), (16, 128, 256), jnp.float32)
        _lenS = 128 - jax.random.randint(jax.random.fold_in(_rk, 7), (16,), 0, max(1, 128 // 4) + 1, jnp.int32)
        _lenS2 = 128 - jax.random.randint(jax.random.fold_in(_rk, 8), (16,), 0, max(1, 128 // 4) + 1, jnp.int32)
        _ctx_1024P = jax.random.normal(jax.random.fold_in(_rk, 11), (16, 16, 256), jnp.float32)
        _ctx_1024c = jax.random.dirichlet(jax.random.fold_in(_rk, 511), 0.3 * jnp.ones((16,), jnp.float32), (16, 128))
        _ctx_1024t = jnp.einsum('bsk,bkd->bsd', _ctx_1024c, _ctx_1024P)
        _ctx_1024t = _ctx_1024t * jax.lax.rsqrt(jnp.mean(jnp.square(_ctx_1024t)) + 1e-12) * 0.953939
        ctx_1024 = -1.39393e-06 + 0.999914 * (_ctx_1024t + 0.3 * jax.random.normal(jax.random.fold_in(_rk, 611), (16, 128, 256), jnp.float32))
        _validS = jnp.arange(128)[None, :] < _lenS[:, None]
        _validS2 = jnp.arange(128)[None, :] < _lenS2[:, None]
        _causal = jnp.tril(jnp.ones((128, 128), dtype=bool))
        mask_Bx1xSxS2_ik1 = jnp.where(jnp.broadcast_to(_validS2[:, None, None, :], (16, 1, 128, 128)), 1, 0).astype(jnp.int32)
        mask_BxSxS2_ik0 = jnp.where(jnp.broadcast_to(_validS2[:, None, :], (16, 128, 128)), 0, 1).astype(jnp.int32)
        _g = jax.random.normal(jax.random.fold_in(_rk, 9001), (2, 4), jnp.float32)
        _g = jnp.sign(_g) * jnp.maximum(jnp.abs(_g), 1.0) + (_g == 0) * 1.0
        g_xattn = _g[0]
        g_ffn = _g[1]
        return (x, ctx_1024, mask_Bx1xSxS2_ik1, mask_BxSxS2_ik0, g_xattn, g_ffn)
    x, ctx_1024, mask_Bx1xSxS2_ik1, mask_BxSxS2_ik0, g_xattn, g_ffn = _rec_inputs()

    def _L0_xattn_setup():
        import jax, jax.numpy as jnp
        import numpy as np
        import math
        HEAD = 16
        D_MODEL = 256
        HEAD_DIM = D_MODEL // HEAD
        B, S = (2, 512)
        key = jax.random.key(seed)
        ks = jax.random.split(key, 9)
        sc = 1.0 / math.sqrt(D_MODEL)
        return {'q': jax.random.normal(ks[0], (B, S, D_MODEL), dtype=jnp.float32), 'k': jax.random.normal(ks[1], (B, S, D_MODEL), dtype=jnp.float32), 'v': jax.random.normal(ks[2], (B, S, D_MODEL), dtype=jnp.float32), 'mask': jax.random.randint(ks[3], (B, 1, S, S), 0, 2, dtype=jnp.int32), 'wq': jax.random.normal(ks[4], (D_MODEL, D_MODEL), dtype=jnp.float32) * sc, 'wk': jax.random.normal(ks[5], (D_MODEL, D_MODEL), dtype=jnp.float32) * sc, 'wv': jax.random.normal(ks[6], (D_MODEL, D_MODEL), dtype=jnp.float32) * sc, 'wo': jax.random.normal(ks[7], (D_MODEL, D_MODEL), dtype=jnp.float32) * sc, 'bo': jax.random.normal(ks[8], (D_MODEL,), dtype=jnp.float32) * 0.01}
    _L0_xattn_all = _L0_xattn_setup()
    _L0_xattn_in = {k: v for k, v in _L0_xattn_all.items() if k in ('wq', 'wk', 'wv', 'wo', 'bo')}
    del _L0_xattn_all

    def _L0_ffn_setup():
        import jax, jax.numpy as jnp
        import numpy as np
        B, S, D, H, F = (4, 1024, 256, 16, 1024)
        CAP = 0.125
        ROPE_BASE = 10000.0

        def rmsnorm(x, g):
            return x * jax.lax.rsqrt(jnp.mean(x * x, -1, keepdims=True) + 1e-06) * g

        def rope(t, pos):
            hd = t.shape[-1]
            inv = 1.0 / ROPE_BASE ** (jnp.arange(0, hd, 2, dtype=jnp.float32) / hd)
            f = pos[:, None, :, None].astype(jnp.float32) * inv
            emb = jnp.concatenate([f, f], axis=-1)
            cos, sin = (jnp.cos(emb), jnp.sin(emb))
            rot = jnp.concatenate([-t[..., hd // 2:], t[..., :hd // 2]], axis=-1)
            return t * cos + rot * sin
        key = jax.random.key(seed)
        ks = jax.random.split(key, 9)
        scale = 0.02
        x = jax.random.normal(ks[0], (B, S, D), jnp.float32)
        causal = jnp.where(jnp.tril(jnp.ones((S, S), bool)), 0.0, -1000000000.0).astype(jnp.float32)
        attention_mask = jnp.broadcast_to(causal[None, None], (B, 1, S, S))
        position_ids = jnp.broadcast_to(jnp.arange(S, dtype=jnp.int32), (B, S))
        return {'x': x, 'attention_mask': attention_mask, 'position_ids': position_ids, 'router_w': jax.random.normal(ks[1], (D, 1), jnp.float32) * scale, 'router_b': jnp.zeros((1,), jnp.float32), 'wq': jax.random.normal(ks[2], (D, D), jnp.float32) * scale, 'wk': jax.random.normal(ks[3], (D, D), jnp.float32) * scale, 'wv': jax.random.normal(ks[4], (D, D), jnp.float32) * scale, 'wo': jax.random.normal(ks[5], (D, D), jnp.float32) * scale, 'w1': jax.random.normal(ks[6], (D, F), jnp.float32) * scale, 'w2': jax.random.normal(ks[7], (F, D), jnp.float32) * scale, 'ln1': jnp.ones((D,), jnp.float32), 'ln2': jnp.ones((D,), jnp.float32)}
    _L0_ffn_all = _L0_ffn_setup()
    _L0_ffn_in = {k: v for k, v in _L0_ffn_all.items() if k in ('attention_mask', 'position_ids', 'router_w', 'router_b', 'wq', 'wk', 'wv', 'wo', 'w1', 'w2', 'ln1', 'ln2')}
    del _L0_ffn_all

    def _L1_xattn_setup():
        import jax, jax.numpy as jnp
        import numpy as np
        B, L_ENC, L_DEC, D = (16, 128, 128, 256)
        key = jax.random.key(seed)
        k1, k2, k3, k4, k5, k6 = jax.random.split(key, 6)
        encoder_hc = jax.random.normal(k1, (B, L_ENC, D), dtype=jnp.float32)
        decoder_hq = jax.random.normal(k2, (B, L_DEC, D), dtype=jnp.float32)
        w_sim = jax.random.normal(k3, (3 * D,), dtype=jnp.float32) * 0.02
        b_sim = jax.random.normal(k4, (1,), dtype=jnp.float32) * 0.02
        W_qv = jax.random.normal(k5, (4 * D, D), dtype=jnp.float32) * 0.02
        b_qv = jax.random.normal(k6, (D,), dtype=jnp.float32) * 0.02
        return {'encoder_hc': encoder_hc, 'decoder_hq': decoder_hq, 'w_sim': w_sim, 'b_sim': b_sim, 'W_qv': W_qv, 'b_qv': b_qv}
    _L1_xattn_all = _L1_xattn_setup()
    _L1_xattn_in = {k: v for k, v in _L1_xattn_all.items() if k in ('w_sim', 'b_sim', 'W_qv', 'b_qv')}
    del _L1_xattn_all

    def _L1_ffn_setup():
        import jax, jax.numpy as jnp
        import numpy as np
        B, S, H, E, DFF = (4, 1024, 256, 8, 1024)
        key = jax.random.key(seed)
        k0, k1, k2, k3 = jax.random.split(key, 4)
        hidden_states = jax.random.normal(k0, (B, S, H), dtype=jnp.float32)
        gate_w = jax.random.normal(k1, (E, H), dtype=jnp.float32) * 0.02
        w1 = jax.random.normal(k2, (E, H, DFF), dtype=jnp.float32) * 0.02
        b1 = jnp.zeros((E, DFF), dtype=jnp.float32)
        w2 = jax.random.normal(k3, (E, DFF, H), dtype=jnp.float32) * 0.02
        b2 = jnp.zeros((E, H), dtype=jnp.float32)
        return {'hidden_states': hidden_states, 'gate_w': gate_w, 'w1': w1, 'b1': b1, 'w2': w2, 'b2': b2}
    _L1_ffn_all = _L1_ffn_setup()
    _L1_ffn_in = {k: v for k, v in _L1_ffn_all.items() if k in ('gate_w', 'w1', 'b1', 'w2', 'b2')}
    del _L1_ffn_all

    def _L2_xattn_setup():
        import jax, jax.numpy as jnp
        import numpy as np
        import math
        B, T, S, D, N, H = (2, 512, 512, 256, 16, 64)
        key = jax.random.key(seed)
        ks = jax.random.split(key, 8)
        scale = 0.02
        return {'query': jax.random.normal(ks[0], (B, T, D), jnp.float32), 'value': jax.random.normal(ks[1], (B, S, D), jnp.float32), 'attention_mask': jax.random.randint(ks[2], (B, T, S), 0, 2, jnp.int32), 'Wq': jax.random.normal(ks[3], (D, N, H), jnp.float32) * scale, 'bq': jnp.zeros((N, H), jnp.float32), 'Wk': jax.random.normal(ks[4], (D, N, H), jnp.float32) * scale, 'bk': jnp.zeros((N, H), jnp.float32), 'Wv': jax.random.normal(ks[5], (D, N, H), jnp.float32) * scale, 'bv': jnp.zeros((N, H), jnp.float32), 'Wo': jax.random.normal(ks[6], (N, H, D), jnp.float32) * scale, 'bo': jnp.zeros((D,), jnp.float32)}
    _L2_xattn_all = _L2_xattn_setup()
    _L2_xattn_in = {k: v for k, v in _L2_xattn_all.items() if k in ('Wq', 'bq', 'Wk', 'bk', 'Wv', 'bv', 'Wo', 'bo')}
    del _L2_xattn_all

    def _L2_ffn_setup():
        import jax, jax.numpy as jnp
        import numpy as np
        B, S, D = (1, 512, 256)
        E, F = (16, 256)
        NG, TKG, K = (4, 2, 4)
        NSH = 2
        SCALE = 2.5
        STD = 0.02
        EPG = E // NG

        def _route(x_flat, router_w, bias):
            logits = x_flat.astype(jnp.float32) @ router_w.T
            scores = jax.nn.sigmoid(logits)
            s = scores + bias[None, :]
            sg = s.reshape(-1, NG, EPG)
            group_score = jax.lax.top_k(sg, 2)[0].sum(-1)
            gidx = jax.lax.top_k(group_score, TKG)[1]
            gmask = jnp.sum(jax.nn.one_hot(gidx, NG, dtype=jnp.float32), axis=1) > 0
            emask = jnp.repeat(gmask, EPG, axis=1)
            masked = jnp.where(emask, s, -1.0)
            topk_idx = jax.lax.top_k(masked, K)[1]
            tw = jnp.take_along_axis(scores, topk_idx, axis=1)
            tw = tw / (tw.sum(-1, keepdims=True) + 1e-20)
            tw = tw * SCALE
            return (topk_idx, tw)
        key = jax.random.key(seed)
        ks = jax.random.split(key, 8)
        return {'hidden_states': jax.random.normal(ks[0], (B, S, D), jnp.float32), 'router_w': jax.random.normal(ks[1], (E, D), jnp.float32) * STD, 'bias': jnp.zeros((E,), jnp.float32), 'gate_w': jax.random.normal(ks[2], (E, D, F), jnp.float32) * STD, 'up_w': jax.random.normal(ks[3], (E, D, F), jnp.float32) * STD, 'down_w': jax.random.normal(ks[4], (E, F, D), jnp.float32) * STD, 'sh_gate_w': jax.random.normal(ks[5], (D, NSH * F), jnp.float32) * STD, 'sh_up_w': jax.random.normal(ks[6], (D, NSH * F), jnp.float32) * STD, 'sh_down_w': jax.random.normal(ks[7], (NSH * F, D), jnp.float32) * STD}
    _L2_ffn_all = _L2_ffn_setup()
    _L2_ffn_in = {k: v for k, v in _L2_ffn_all.items() if k in ('router_w', 'bias', 'gate_w', 'up_w', 'down_w', 'sh_gate_w', 'sh_up_w', 'sh_down_w')}
    del _L2_ffn_all

    def _L3_xattn_setup():
        import jax, jax.numpy as jnp
        import numpy as np
        from jax import lax
        BIG = jnp.float32(1e+30)

        def _pairwise_euclidean(a, b):
            aa = jnp.sum(a * a, axis=-1)[:, None]
            bb = jnp.sum(b * b, axis=-1)[None, :]
            ab = a @ b.T
            return jnp.sqrt(jnp.maximum(aa + bb - 2.0 * ab, 0.0))

        def _dtw_cost(D):
            row0 = jnp.cumsum(D[0])

            def row_step(prev_row, d_row):
                first = d_row[0] + prev_row[0]

                def col_step(left, inp):
                    d_ij, up, diag = inp
                    r = d_ij + jnp.minimum(jnp.minimum(up, left), diag)
                    return (r, r)
                _, rest = lax.scan(col_step, first, (d_row[1:], prev_row[1:], prev_row[:-1]))
                row = jnp.concatenate([first[None], rest])
                return (row, row)
            _, rows = lax.scan(row_step, row0, D[1:])
            return jnp.concatenate([row0[None], rows], axis=0)

        def _backtrack(R, T1, T2):
            L = T1 + T2 - 1

            def step(carry, _):
                i, j, done = carry
                valid = jnp.logical_not(done)
                cd = jnp.where((i > 0) & (j > 0), R[jnp.maximum(i - 1, 0), jnp.maximum(j - 1, 0)], BIG)
                cu = jnp.where(i > 0, R[jnp.maximum(i - 1, 0), j], BIG)
                cl = jnp.where(j > 0, R[i, jnp.maximum(j - 1, 0)], BIG)
                choice = jnp.argmin(jnp.stack([cd, cu, cl]))
                ni = jnp.where(choice <= 1, i - 1, i)
                nj = jnp.where((choice == 0) | (choice == 2), j - 1, j)
                at_origin = (i == 0) & (j == 0)
                ni = jnp.where(at_origin, 0, ni)
                nj = jnp.where(at_origin, 0, nj)
                return ((ni, nj, done | at_origin), (i, j, valid))
            init = (jnp.int32(T1 - 1), jnp.int32(T2 - 1), jnp.bool_(False))
            _, (i_idx, j_idx, valid) = lax.scan(step, init, None, length=L)
            return (i_idx, j_idx, valid)

        def _align_one(small, large):
            T_small, d = small.shape
            T_large = large.shape[0]
            D = _pairwise_euclidean(small, large)
            R = _dtw_cost(D)
            i_idx, j_idx, valid = _backtrack(R, T_small, T_large)
            contrib = small[i_idx] * valid[:, None].astype(small.dtype)
            expanded = jnp.zeros((T_large, d), dtype=small.dtype).at[j_idx].add(contrib)
            return expanded
        key = jax.random.key(seed)
        k1, k2 = jax.random.split(key)
        teacher = jax.random.normal(k1, (16, 100, 256), dtype=jnp.float32)
        student = jax.random.normal(k2, (16, 150, 256), dtype=jnp.float32)
        return {'teacher_features': teacher, 'student_features': student}
    _L3_xattn_all = _L3_xattn_setup()
    _L3_xattn_in = {k: v for k, v in _L3_xattn_all.items() if k in ()}
    del _L3_xattn_all

    def _L3_ffn_setup():
        import jax, jax.numpy as jnp
        import numpy as np
        HIDDEN = 256
        INNER = 1024

        def _weight_quant(w):
            scale = 1.0 / jnp.clip(jnp.mean(jnp.abs(w)), 1e-05)
            wq = jnp.clip(jnp.round(w * scale), -1.0, 1.0) / scale
            return w + jax.lax.stop_gradient(wq - w)

        def _act_quant(x):
            scale = 127.0 / jnp.clip(jnp.max(jnp.abs(x), axis=-1, keepdims=True), 1e-05)
            xq = jnp.clip(jnp.round(x * scale), -128.0, 127.0) / scale
            return x + jax.lax.stop_gradient(xq - x)

        def _bitlinear(x, w):
            return jnp.einsum('bsi,oi->bso', _act_quant(x), _weight_quant(w))
        key = jax.random.key(seed)
        k0, k1, k2, k3 = jax.random.split(key, 4)
        x = jax.random.normal(k0, (4, 512, HIDDEN), dtype=jnp.float32)
        w_gate = jax.random.normal(k1, (INNER, HIDDEN), dtype=jnp.float32) / np.sqrt(HIDDEN)
        w_up = jax.random.normal(k2, (INNER, HIDDEN), dtype=jnp.float32) / np.sqrt(HIDDEN)
        w_down = jax.random.normal(k3, (HIDDEN, INNER), dtype=jnp.float32) / np.sqrt(INNER)
        return {'x': x, 'w_gate': w_gate, 'w_up': w_up, 'w_down': w_down}
    _L3_ffn_all = _L3_ffn_setup()
    _L3_ffn_in = {k: v for k, v in _L3_ffn_all.items() if k in ('w_gate', 'w_up', 'w_down')}
    del _L3_ffn_all
    return {'x': x, 'ctx_1024': ctx_1024, 'mask_Bx1xSxS2_ik1': mask_Bx1xSxS2_ik1, 'mask_BxSxS2_ik0': mask_BxSxS2_ik0, 'g_xattn': g_xattn, 'g_ffn': g_ffn, 'L0_xattn_wq': _L0_xattn_in['wq'], 'L0_xattn_wk': _L0_xattn_in['wk'], 'L0_xattn_wv': _L0_xattn_in['wv'], 'L0_xattn_wo': _L0_xattn_in['wo'], 'L0_xattn_bo': _L0_xattn_in['bo'], 'L0_ffn_attention_mask': _L0_ffn_in['attention_mask'], 'L0_ffn_position_ids': _L0_ffn_in['position_ids'], 'L0_ffn_router_w': _L0_ffn_in['router_w'], 'L0_ffn_router_b': _L0_ffn_in['router_b'], 'L0_ffn_wq': _L0_ffn_in['wq'], 'L0_ffn_wk': _L0_ffn_in['wk'], 'L0_ffn_wv': _L0_ffn_in['wv'], 'L0_ffn_wo': _L0_ffn_in['wo'], 'L0_ffn_w1': _L0_ffn_in['w1'], 'L0_ffn_w2': _L0_ffn_in['w2'], 'L0_ffn_ln1': _L0_ffn_in['ln1'], 'L0_ffn_ln2': _L0_ffn_in['ln2'], 'L1_xattn_w_sim': _L1_xattn_in['w_sim'], 'L1_xattn_b_sim': _L1_xattn_in['b_sim'], 'L1_xattn_W_qv': _L1_xattn_in['W_qv'], 'L1_xattn_b_qv': _L1_xattn_in['b_qv'], 'L1_ffn_gate_w': _L1_ffn_in['gate_w'], 'L1_ffn_w1': _L1_ffn_in['w1'], 'L1_ffn_b1': _L1_ffn_in['b1'], 'L1_ffn_w2': _L1_ffn_in['w2'], 'L1_ffn_b2': _L1_ffn_in['b2'], 'L2_xattn_Wq': _L2_xattn_in['Wq'], 'L2_xattn_bq': _L2_xattn_in['bq'], 'L2_xattn_Wk': _L2_xattn_in['Wk'], 'L2_xattn_bk': _L2_xattn_in['bk'], 'L2_xattn_Wv': _L2_xattn_in['Wv'], 'L2_xattn_bv': _L2_xattn_in['bv'], 'L2_xattn_Wo': _L2_xattn_in['Wo'], 'L2_xattn_bo': _L2_xattn_in['bo'], 'L2_ffn_router_w': _L2_ffn_in['router_w'], 'L2_ffn_bias': _L2_ffn_in['bias'], 'L2_ffn_gate_w': _L2_ffn_in['gate_w'], 'L2_ffn_up_w': _L2_ffn_in['up_w'], 'L2_ffn_down_w': _L2_ffn_in['down_w'], 'L2_ffn_sh_gate_w': _L2_ffn_in['sh_gate_w'], 'L2_ffn_sh_up_w': _L2_ffn_in['sh_up_w'], 'L2_ffn_sh_down_w': _L2_ffn_in['sh_down_w'], 'L3_ffn_w_gate': _L3_ffn_in['w_gate'], 'L3_ffn_w_up': _L3_ffn_in['w_up'], 'L3_ffn_w_down': _L3_ffn_in['w_down']}

def reference(x, ctx_1024, mask_Bx1xSxS2_ik1, mask_BxSxS2_ik0, g_xattn, g_ffn, L0_xattn_wq, L0_xattn_wk, L0_xattn_wv, L0_xattn_wo, L0_xattn_bo, L0_ffn_attention_mask, L0_ffn_position_ids, L0_ffn_router_w, L0_ffn_router_b, L0_ffn_wq, L0_ffn_wk, L0_ffn_wv, L0_ffn_wo, L0_ffn_w1, L0_ffn_w2, L0_ffn_ln1, L0_ffn_ln2, L1_xattn_w_sim, L1_xattn_b_sim, L1_xattn_W_qv, L1_xattn_b_qv, L1_ffn_gate_w, L1_ffn_w1, L1_ffn_b1, L1_ffn_w2, L1_ffn_b2, L2_xattn_Wq, L2_xattn_bq, L2_xattn_Wk, L2_xattn_bk, L2_xattn_Wv, L2_xattn_bv, L2_xattn_Wo, L2_xattn_bo, L2_ffn_router_w, L2_ffn_bias, L2_ffn_gate_w, L2_ffn_up_w, L2_ffn_down_w, L2_ffn_sh_gate_w, L2_ffn_sh_up_w, L2_ffn_sh_down_w, L3_ffn_w_gate, L3_ffn_w_up, L3_ffn_w_down):
    import jax
    import jax.numpy as jnp

    def _L0_xattn_ref(q, k, v, mask, wq, wk, wv, wo, bo):
        import jax, jax.numpy as jnp
        import numpy as np
        import math
        HEAD = 16
        D_MODEL = 256
        HEAD_DIM = D_MODEL // HEAD
        B, S = (2, 512)
        N, Lq, _ = q.shape
        Lk = k.shape[1]
        qh = (q @ wq).reshape(N, Lq, HEAD, HEAD_DIM)
        kh = (k @ wk).reshape(N, Lk, HEAD, HEAD_DIM)
        vh = (v @ wv).reshape(N, Lk, HEAD, HEAD_DIM)
        scores = jnp.einsum('nqha,nkha->nhqk', qh, kh)
        scores = jnp.where(mask == 0, jnp.float32(-10000000000.0), scores)
        attn = jax.nn.softmax(scores / math.sqrt(HEAD_DIM), axis=-1)
        out = jnp.einsum('nhqk,nkha->nqha', attn, vh).reshape(N, Lq, D_MODEL)
        return out @ wo + bo

    def _L0_ffn_ref(x, attention_mask, position_ids, router_w, router_b, wq, wk, wv, wo, w1, w2, ln1, ln2):
        import jax, jax.numpy as jnp
        import numpy as np
        B, S, D, H, F = (4, 1024, 256, 16, 1024)
        CAP = 0.125
        ROPE_BASE = 10000.0

        def rmsnorm(x, g):
            return x * jax.lax.rsqrt(jnp.mean(x * x, -1, keepdims=True) + 1e-06) * g

        def rope(t, pos):
            hd = t.shape[-1]
            inv = 1.0 / ROPE_BASE ** (jnp.arange(0, hd, 2, dtype=jnp.float32) / hd)
            f = pos[:, None, :, None].astype(jnp.float32) * inv
            emb = jnp.concatenate([f, f], axis=-1)
            cos, sin = (jnp.cos(emb), jnp.sin(emb))
            rot = jnp.concatenate([-t[..., hd // 2:], t[..., :hd // 2]], axis=-1)
            return t * cos + rot * sin
        b, s, d = x.shape
        hd = d // H
        weights = (x @ router_w)[..., 0] + router_b[0]
        k = int(CAP * s)
        topv, topi = jax.lax.top_k(weights, k)
        thr = topv[:, -1]
        sel_mask = (weights > thr[:, None]).astype(x.dtype)
        kc = k - 1
        sel_idx = jnp.sort(topi[:, :kc], axis=1)
        bidx = jnp.arange(b)[:, None]
        x_sel = x[bidx, sel_idx]
        pos_sel = position_ids[bidx, sel_idx]
        w_sel = weights[bidx, sel_idx]
        m = attention_mask[:, 0]
        m_sel = m[bidx[:, :, None], sel_idx[:, :, None], sel_idx[:, None, :]]
        hn = rmsnorm(x_sel, ln1)

        def heads(t):
            return t.reshape(b, kc, H, hd).transpose(0, 2, 1, 3)
        q = rope(heads(hn @ wq), pos_sel)
        kk = rope(heads(hn @ wk), pos_sel)
        v = heads(hn @ wv)
        sc = jnp.einsum('bhqd,bhkd->bhqk', q, kk) / np.sqrt(hd).astype(np.float32)
        sc = sc + m_sel[:, None]
        a = jax.nn.softmax(sc, axis=-1)
        o = jnp.einsum('bhqk,bhkd->bhqd', a, v).transpose(0, 2, 1, 3).reshape(b, kc, d) @ wo
        x1 = x_sel + o
        x2 = x1 + jax.nn.gelu(rmsnorm(x1, ln2) @ w1) @ w2
        proc = x2 * w_sel[..., None]
        out = jnp.zeros_like(x).at[bidx, sel_idx].set(proc)
        return out + x * (1.0 - sel_mask)[..., None]

    def _L1_xattn_ref(encoder_hc, decoder_hq, w_sim, b_sim, W_qv, b_qv):
        import jax, jax.numpy as jnp
        import numpy as np
        B, L_ENC, L_DEC, D = (16, 128, 128, 256)
        d = encoder_hc.shape[-1]
        w1, w2, w3 = (w_sim[:d], w_sim[d:2 * d], w_sim[2 * d:])
        Sim = (encoder_hc @ w1)[:, :, None] + (decoder_hq @ w2)[:, None, :] + jnp.einsum('bid,bjd->bij', encoder_hc * w3, decoder_hq) + b_sim[0]
        A = jax.nn.softmax(Sim, axis=2)
        hq_hat = jnp.einsum('bij,bjd->bid', A, decoder_hq)
        Batt = jax.nn.softmax(jnp.max(Sim, axis=2), axis=1)
        hc_bar = jnp.einsum('bi,bid->bd', Batt, encoder_hc)[:, None, :]
        hc_hat = jnp.broadcast_to(hc_bar, encoder_hc.shape)
        feats = jnp.concatenate([encoder_hc, hq_hat, encoder_hc * hq_hat, encoder_hc * hc_hat], axis=-1)
        hcq = feats @ W_qv + b_qv
        return hcq

    def _L1_ffn_ref(hidden_states, gate_w, w1, b1, w2, b2):
        import jax, jax.numpy as jnp
        import numpy as np
        B, S, H, E, DFF = (4, 1024, 256, 8, 1024)
        b, s, h = hidden_states.shape
        x = hidden_states.reshape(-1, h)
        gate_logits = x @ gate_w.T
        gate_probs = jax.nn.softmax(gate_logits, axis=-1)
        expert_idx = jnp.argmax(gate_probs, axis=-1)
        expert_w = jnp.take_along_axis(gate_probs, expert_idx[:, None], axis=1)[:, 0]
        out = jnp.zeros_like(x)
        n_experts = w1.shape[0]
        for e in range(n_experts):
            ye = jax.nn.relu(x @ w1[e] + b1[e]) @ w2[e] + b2[e]
            sel = (expert_idx == e)[:, None]
            out = out + jnp.where(sel, ye * expert_w[:, None], 0.0)
        return out.reshape(b, s, h)

    def _L2_xattn_ref(query, value, attention_mask, Wq, bq, Wk, bk, Wv, bv, Wo, bo):
        import jax, jax.numpy as jnp
        import numpy as np
        import math
        B, T, S, D, N, H = (2, 512, 512, 256, 16, 64)
        q = jnp.einsum('btd,dnh->btnh', query, Wq) + bq
        k = jnp.einsum('bsd,dnh->bsnh', value, Wk) + bk
        v = jnp.einsum('bsd,dnh->bsnh', value, Wv) + bv
        scores = jnp.einsum('bsnh,btnh->bnts', k, q) * (1.0 / math.sqrt(float(H)))
        adder = (1.0 - attention_mask[:, None, :, :].astype(scores.dtype)) * -10000.0
        probs = jax.nn.softmax(scores + adder, axis=-1)
        ctx = jnp.einsum('bnts,bsnh->btnh', probs, v)
        out = jnp.einsum('btnh,nhd->btd', ctx, Wo) + bo
        return out

    def _L2_ffn_ref(hidden_states, router_w, bias, gate_w, up_w, down_w, sh_gate_w, sh_up_w, sh_down_w):
        import jax, jax.numpy as jnp
        import numpy as np
        B, S, D = (1, 512, 256)
        E, F = (16, 256)
        NG, TKG, K = (4, 2, 4)
        NSH = 2
        SCALE = 2.5
        STD = 0.02
        EPG = E // NG

        def _route(x_flat, router_w, bias):
            logits = x_flat.astype(jnp.float32) @ router_w.T
            scores = jax.nn.sigmoid(logits)
            s = scores + bias[None, :]
            sg = s.reshape(-1, NG, EPG)
            group_score = jax.lax.top_k(sg, 2)[0].sum(-1)
            gidx = jax.lax.top_k(group_score, TKG)[1]
            gmask = jnp.sum(jax.nn.one_hot(gidx, NG, dtype=jnp.float32), axis=1) > 0
            emask = jnp.repeat(gmask, EPG, axis=1)
            masked = jnp.where(emask, s, -1.0)
            topk_idx = jax.lax.top_k(masked, K)[1]
            tw = jnp.take_along_axis(scores, topk_idx, axis=1)
            tw = tw / (tw.sum(-1, keepdims=True) + 1e-20)
            tw = tw * SCALE
            return (topk_idx, tw)
        x = hidden_states.reshape(-1, D)
        topk_idx, tw = _route(x, router_w, bias)
        combine = (jax.nn.one_hot(topk_idx, E, dtype=tw.dtype) * tw[..., None]).sum(1)
        h = jnp.einsum('td,edf->etf', x, gate_w)
        u = jnp.einsum('td,edf->etf', x, up_w)
        y = jnp.einsum('etf,efd->etd', jax.nn.silu(h) * u, down_w)
        routed = jnp.einsum('etd,te->td', y, combine)
        sh = jax.nn.silu(x @ sh_gate_w) * (x @ sh_up_w) @ sh_down_w
        return (routed + sh).reshape(hidden_states.shape)

    def _L3_xattn_ref(teacher_features, student_features):
        import jax, jax.numpy as jnp
        import numpy as np
        from jax import lax
        BIG = jnp.float32(1e+30)

        def _pairwise_euclidean(a, b):
            aa = jnp.sum(a * a, axis=-1)[:, None]
            bb = jnp.sum(b * b, axis=-1)[None, :]
            ab = a @ b.T
            return jnp.sqrt(jnp.maximum(aa + bb - 2.0 * ab, 0.0))

        def _dtw_cost(D):
            row0 = jnp.cumsum(D[0])

            def row_step(prev_row, d_row):
                first = d_row[0] + prev_row[0]

                def col_step(left, inp):
                    d_ij, up, diag = inp
                    r = d_ij + jnp.minimum(jnp.minimum(up, left), diag)
                    return (r, r)
                _, rest = lax.scan(col_step, first, (d_row[1:], prev_row[1:], prev_row[:-1]))
                row = jnp.concatenate([first[None], rest])
                return (row, row)
            _, rows = lax.scan(row_step, row0, D[1:])
            return jnp.concatenate([row0[None], rows], axis=0)

        def _backtrack(R, T1, T2):
            L = T1 + T2 - 1

            def step(carry, _):
                i, j, done = carry
                valid = jnp.logical_not(done)
                cd = jnp.where((i > 0) & (j > 0), R[jnp.maximum(i - 1, 0), jnp.maximum(j - 1, 0)], BIG)
                cu = jnp.where(i > 0, R[jnp.maximum(i - 1, 0), j], BIG)
                cl = jnp.where(j > 0, R[i, jnp.maximum(j - 1, 0)], BIG)
                choice = jnp.argmin(jnp.stack([cd, cu, cl]))
                ni = jnp.where(choice <= 1, i - 1, i)
                nj = jnp.where((choice == 0) | (choice == 2), j - 1, j)
                at_origin = (i == 0) & (j == 0)
                ni = jnp.where(at_origin, 0, ni)
                nj = jnp.where(at_origin, 0, nj)
                return ((ni, nj, done | at_origin), (i, j, valid))
            init = (jnp.int32(T1 - 1), jnp.int32(T2 - 1), jnp.bool_(False))
            _, (i_idx, j_idx, valid) = lax.scan(step, init, None, length=L)
            return (i_idx, j_idx, valid)

        def _align_one(small, large):
            T_small, d = small.shape
            T_large = large.shape[0]
            D = _pairwise_euclidean(small, large)
            R = _dtw_cost(D)
            i_idx, j_idx, valid = _backtrack(R, T_small, T_large)
            contrib = small[i_idx] * valid[:, None].astype(small.dtype)
            expanded = jnp.zeros((T_large, d), dtype=small.dtype).at[j_idx].add(contrib)
            return expanded
        return jax.vmap(_align_one)(teacher_features, student_features)

    def _L3_ffn_ref(x, w_gate, w_up, w_down):
        import jax, jax.numpy as jnp
        import numpy as np
        HIDDEN = 256
        INNER = 1024

        def _weight_quant(w):
            scale = 1.0 / jnp.clip(jnp.mean(jnp.abs(w)), 1e-05)
            wq = jnp.clip(jnp.round(w * scale), -1.0, 1.0) / scale
            return w + jax.lax.stop_gradient(wq - w)

        def _act_quant(x):
            scale = 127.0 / jnp.clip(jnp.max(jnp.abs(x), axis=-1, keepdims=True), 1e-05)
            xq = jnp.clip(jnp.round(x * scale), -128.0, 127.0) / scale
            return x + jax.lax.stop_gradient(xq - x)

        def _bitlinear(x, w):
            return jnp.einsum('bsi,oi->bso', _act_quant(x), _weight_quant(w))
        gate = jax.nn.silu(_bitlinear(x, w_gate))
        up = _bitlinear(x, w_up)
        return _bitlinear(gate * up, w_down)
    x = x + jnp.tanh(g_xattn[0]) * _L0_xattn_ref(_layernorm(x, axis=-1), ctx_1024, ctx_1024, mask_Bx1xSxS2_ik1, L0_xattn_wq, L0_xattn_wk, L0_xattn_wv, L0_xattn_wo, L0_xattn_bo)
    x = x + jnp.tanh(g_ffn[0]) * _L0_ffn_ref(_layernorm(x, axis=-1), L0_ffn_attention_mask, L0_ffn_position_ids, L0_ffn_router_w, L0_ffn_router_b, L0_ffn_wq, L0_ffn_wk, L0_ffn_wv, L0_ffn_wo, L0_ffn_w1, L0_ffn_w2, L0_ffn_ln1, L0_ffn_ln2)
    x = x + jnp.tanh(g_xattn[1]) * _L1_xattn_ref(_layernorm(x, axis=-1), ctx_1024, L1_xattn_w_sim, L1_xattn_b_sim, L1_xattn_W_qv, L1_xattn_b_qv)
    x = x + jnp.tanh(g_ffn[1]) * _L1_ffn_ref(_layernorm(x, axis=-1), L1_ffn_gate_w, L1_ffn_w1, L1_ffn_b1, L1_ffn_w2, L1_ffn_b2)
    x = x + jnp.tanh(g_xattn[2]) * _L2_xattn_ref(_layernorm(x, axis=-1), ctx_1024, mask_BxSxS2_ik0, L2_xattn_Wq, L2_xattn_bq, L2_xattn_Wk, L2_xattn_bk, L2_xattn_Wv, L2_xattn_bv, L2_xattn_Wo, L2_xattn_bo)
    x = x + jnp.tanh(g_ffn[2]) * _L2_ffn_ref(_layernorm(x, axis=-1), L2_ffn_router_w, L2_ffn_bias, L2_ffn_gate_w, L2_ffn_up_w, L2_ffn_down_w, L2_ffn_sh_gate_w, L2_ffn_sh_up_w, L2_ffn_sh_down_w)
    x = x + jnp.tanh(g_xattn[3]) * _L3_xattn_ref(ctx_1024, _layernorm(x, axis=-1))
    x = x + jnp.tanh(g_ffn[3]) * _L3_ffn_ref(_layernorm(x, axis=-1), L3_ffn_w_gate, L3_ffn_w_up, L3_ffn_w_down)
    return x

_drawn_inputs = setup_inputs


def setup_inputs(seed=0):
    import zlib

    import numpy as np

    out = dict(_drawn_inputs(seed))
    spreads = {'L0_ffn_ln1': (1.0, 0.6),
     'L0_ffn_ln2': (1.0, 0.6),
     'L1_ffn_b1': (0.0, 0.8),
     'L1_ffn_b2': (0.0, 0.385),
     'L2_xattn_bq': (0.0, 0.8),
     'L2_xattn_bk': (0.0, 0.8),
     'L2_xattn_bv': (0.0, 0.1),
     'L2_xattn_bo': (0.0, 0.1),
     'L2_ffn_bias': (0.0, 0.477)}
    factors = {'g_ffn': 8.0,
     'L0_xattn_bo': 8.0,
     'L0_ffn_wq': 8.0,
     'L0_ffn_wk': 8.0,
     'L0_ffn_wv': 3.369,
     'L0_ffn_wo': 3.463,
     'L2_xattn_Wq': 8.0,
     'L2_xattn_Wk': 8.0,
     'L2_ffn_router_w': 4.37,
     'L2_ffn_gate_w': 3.254,
     'L2_ffn_up_w': 3.198,
     'L2_ffn_sh_gate_w': 2.899,
     'L2_ffn_sh_up_w': 2.854,
     'L2_ffn_sh_down_w': 2.868}
    for name, (base, spread) in spreads.items():
        noise = np.random.default_rng([zlib.crc32(name.encode()), seed]).standard_normal(out[name].shape)
        drawn = base * np.exp(spread * noise) if base else spread * noise
        out[name] = jnp.asarray(drawn.astype(out[name].dtype))
    for name, factor in factors.items():
        out[name] = (out[name] * factor).astype(out[name].dtype)
    return out
```

```python
from contextlib import ExitStack

import numpy as np

import concourse.bass as bass
from concourse import mybir



F32 = mybir.dt.float32
U32 = mybir.dt.uint32
BF16 = mybir.dt.bfloat16
I32 = mybir.dt.int32
ALU = mybir.AluOpType
ACT = mybir.ActivationFunctionType
AX = mybir.AxisListType

P = 128
B = 16
D = 256
KT = D // P
LN_EPS = 1e-5
BIG = 1e30


def after(eng, sem, count):
    if isinstance(count, int) and count <= 0:
        return
    eng.wait_ge(sem, count)


def loads(b, j):
    return (b - j) * 8 + 16


def settle(eng, sem):
    eng.sem_inc(sem, 1)


def over_batches(eng, body, n=B):
    body(0, 0, True, False)
    body(1, 1, False, False)
    with eng.Fori(0, (n - 4) // 2) as i:
        body(0, i * 2 + 2, False, False)
        body(1, i * 2 + 3, False, False)
    body(0, n - 2, False, False)
    body(1, n - 1, False, True)


def chain(eng, sem, base):
    count = [0]

    def link(ins):
        ins.then_inc(sem, 1)
        count[0] += 1
        eng.wait_ge(sem, base + count[0])

    link.count = count
    return link


def cols(t, start, n):
    return t[:, bass.ds(start, n)]


class Phases:

    def __init__(self, nc):
        self.nc, self.stack = nc, None

    def open(self):
        self.close()
        self.stack = ExitStack()
        return self.stack.enter_context(self.nc.Block())

    def close(self):
        if self.stack is not None:
            self.stack.close()
        self.stack = None


class Core:

    def __init__(self, nc, ins, out, ctx):
        self.nc, self.ins, self.out, self.ctx = nc, ins, out, ctx
        self.sems = []
        sb = self.sbuf_in(ctx)
        self.x = sb("x", [P, B * D])
        self.stats = sb("stats", [P, B * 6])
        self.rstd = sb("rstd", [P, B])
        self.neg_mean_rstd = sb("neg_mean_rstd", [P, B])
        self.ident = sb("ident", [P, P])
        self.ones = sb("ones", [P, P])
        self.gates = sb("gates", [P, 8])

    def sbuf_in(self, ctx):
        return lambda name, shape, dt=F32: ctx.enter_context(self.nc.sbuf_tensor(name, shape, dt))

    def banks_in(self, ctx, tag):
        return [ctx.enter_context(self.nc.psum_tensor(f"{tag}_bank{i}", [P, 512], F32)) for i in range(8)]

    def sems_in(self, tag, names):
        made = {n: self.nc.alloc_semaphore(name=f"{tag}_{n}") for n in names}
        self.sems.extend(made.values())
        return made

    def give_back_sems(self):
        self.nc.clear_and_free_semaphores(self.sems)
        self.nc.all_engine_barrier()
        self.sems = []

    def gate(self, layer, ffn):
        k = 4 * ffn + layer
        return self.gates[:, k:k + 1]


def load_and_prepare(core):
    nc, ins = core.nc, core.ins
    with ExitStack() as ctx:
        s = core.sems_in("prep", ["x_loaded", "gates_loaded", "cleared", "stats"])

        block = ctx.enter_context(nc.Block())

        @block.sync
        def _(sp):
            for b in range(0, B, 4):
                sp.dma_start(core.x[:, b * D:(b + 4) * D].rearrange("p (b d) -> p b d", d=D),
                             ins["x"][b:b + 4].rearrange("b s d -> s b d")).then_inc(s["x_loaded"], 16)

        @block.scalar
        def _(act):
            for k, name in enumerate(("g_xattn", "g_ffn")):
                act.dma_start(core.gates[:, 4 * k:4 * k + 4],
                              ins[name].rearrange("(a n) -> a n", a=1).to_broadcast([P, 4])
                              ).then_inc(s["gates_loaded"], 16)
            act.wait_ge(s["gates_loaded"], 32)
            nc.scalar.activation(core.gates[:, :], core.gates[:, :], ACT.Tanh)

        @block.gpsimd
        def _(pool):
            nc.gpsimd.memset(core.ident[:, :], 0.0).then_inc(s["cleared"], 1)
            nc.gpsimd.memset(core.ones[:, :], 1.0)
            pool.wait_ge(s["cleared"], 1)
            nc.gpsimd.affine_select(out=core.ident[:, :], in_=core.ident[:, :], compare_op=ALU.not_equal,
                                    fill=1.0, base=0, pattern=[[-1, P]],
                                    channel_multiplier=1).then_inc(s["cleared"], 1)

        @block.vector
        def _(dve):
            for b in range(B):
                if b == 0:
                    dve.wait_ge(s["x_loaded"], 64)
                nc.vector.bn_stats(core.stats[:, 6 * b:6 * b + 6], core.x[:, b * D:(b + 1) * D])


def finish_norm_vector(core, dve, s, temps):
    nc = core.nc
    st = core.stats[:, :].rearrange("p (b k) -> p b k", k=6)
    mean_e, var_e, mean_o, var_o = st[:, :, 1], st[:, :, 2], st[:, :, 4], st[:, :, 5]
    half, var, mean, root = (temps[:, k, :] for k in range(4))
    link = chain(dve, s["norm_step"], 0)
    link(nc.vector.tensor_tensor(half, mean_e, mean_o, ALU.subtract))
    link(nc.vector.tensor_tensor(var, var_e, var_o, ALU.add))
    link(nc.vector.tensor_tensor(half, half, half, ALU.mult))
    link(nc.vector.tensor_scalar(var, var, 1.0 / D, LN_EPS, ALU.mult, ALU.add))
    nc.vector.scalar_tensor_tensor(var, half, 0.25, var, ALU.mult, ALU.add).then_inc(s["norm_var"], 1)
    link(nc.vector.tensor_tensor(mean, mean_e, mean_o, ALU.add))
    dve.wait_ge(s["norm_root"], 1)
    link(nc.vector.reciprocal(core.rstd[:, :], root))
    link(nc.vector.scalar_tensor_tensor(core.neg_mean_rstd[:, :], mean, -0.5, core.rstd[:, :], ALU.mult, ALU.mult))


def finish_norm_scalar(core, act, s, temps):
    act.wait_ge(s["norm_var"], 1)
    core.nc.scalar.activation(temps[:, 3, :], temps[:, 1, :], ACT.Sqrt).then_inc(s["norm_root"], 1)


NORM_SEMS = ["norm_step", "norm_var", "norm_root"]


def normalise(core, out, b):
    return core.nc.vector.tensor_scalar(out, cols(core.x, b * D, D), cols(core.rstd, b, 1),
                                        cols(core.neg_mean_rstd, b, 1), ALU.mult, ALU.add)


def take_stats(core, b):
    return core.nc.vector.bn_stats(cols(core.stats, b * 6, 6), cols(core.x, b * D, D))


def store_result(core):
    nc = core.nc
    s = core.sems_in("store", ["stored"])
    with nc.Block() as block:
        @block.sync
        def _(sp):
            for b in range(0, B, 4):
                sp.dma_start(core.out[b:b + 4].rearrange("b s d -> s b d"),
                             core.x[:, b * D:(b + 4) * D].rearrange("p (b d) -> p b d", d=D)
                             ).then_inc(s["stored"], 16)
            sp.wait_ge(s["stored"], 64)


def attention(core, tag, layer, head_dim, mask_name, mask_of, wname, biased):
    nc, ins = core.nc, core.ins
    H = 16
    E = H * head_dim
    small = head_dim == 16
    QT = 4 if small else E // P
    KTL = E // P
    VW = head_dim + 1
    scale = head_dim ** -0.5
    with ExitStack() as ctx:
        sb = core.sbuf_in(ctx)
        wq = sb(f"{tag}_wq", [P, KT, QT * P])
        wk = sb(f"{tag}_wk", [P, KT, E])
        wv = sb(f"{tag}_wv", [P, KT, E])
        wo = sb(f"{tag}_wo", [P, KTL, D])
        bo = sb(f"{tag}_bo", [1, D])
        if biased:
            bq = sb(f"{tag}_bq", [P, KTL])
            bk = sb(f"{tag}_bk", [P, KTL])
            bv = sb(f"{tag}_bv", [1, E])
        mask_diag = sb(f"{tag}_mask_diag", [P, P], BF16)
        temps = sb(f"{tag}_temps", [P, 4, B])
        ctx_in = [sb(f"{tag}_ctx{j}", [P, D]) for j in range(2)]
        mask_in = [sb(f"{tag}_mask{j}", [P, P], I32) for j in range(2)]
        mask_add = [sb(f"{tag}_mask_add{j}", [P, P], BF16) for j in range(2)]
        xn = [sb(f"{tag}_xn{j}", [P, D]) for j in range(2)]
        xcT = [sb(f"{tag}_xcT{j}", [P, 2 * KT, P]) for j in range(2)]
        qT = [sb(f"{tag}_qT{j}", [P, QT, P]) for j in range(2)]
        kT = [sb(f"{tag}_kT{j}", [P, KTL, P]) for j in range(2)]
        v1 = [sb(f"{tag}_v1{j}", [P, H, VW]) for j in range(2)]
        top = sb(f"{tag}_top", [P, 2, 4])
        shifted = [sb(f"{tag}_shifted{j}", [P, 4, P]) for j in range(2)]
        probs = [sb(f"{tag}_probs{j}", [P, 4, P]) for j in range(2)]
        probsT = [sb(f"{tag}_probsT{j}", [P, 4, P]) for j in range(2)]
        inv_sum = sb(f"{tag}_inv_sum", [P, 2, 4])
        heads = [sb(f"{tag}_heads{j}", [P, E]) for j in range(2)]
        headsT = sb(f"{tag}_headsT", [P, KTL, P])
        bank = core.banks_in(ctx, tag)
        front_bank, score_bank, pT_bank, out_bank, back_bank = bank[0:2], bank[2:4], bank[4:6], bank[6], bank[7]
        s = core.sems_in(tag, NORM_SEMS + [
            "weights", "diag", "ctx_in0", "ctx_in1", "mask_in0", "mask_in1", "mask_add", "xn", "filled", "evicted_act", "evicted_dve",
            "scores", "maxed", "shifted", "exped", "pT", "pT_out", "pv", "inv", "normed", "ones_col",
            "headsT", "headsT_out", "projected", "updated", "passed"])

        if small:
            fills = ["T", "Q0", "KV"]
            slots = [[0], [1], [2], []]
        else:
            fills = ["T", "Q0", "Q1", "K0", "K1", "V0", "V1"]
            slots = [[0, 1], [2, 3], [4, 5, 6], []]
        NF = len(fills)
        by_dve = [f[0] in "QK" and biased for f in fills]
        NA, ND = NF - sum(by_dve), sum(by_dve)
        TB = (KTL + 3) // 4

        def evicted(eng, b, f):
            if by_dve[f]:
                after(eng, s["evicted_dve"], b * ND + sum(by_dve[:f + 1]))
            else:
                after(eng, s["evicted_act"], b * NA + f + 1 - sum(by_dve[:f + 1]))

        def head_of(g, i):
            return 2 * g + 8 * (i // 2) + i % 2 if small else 8 * (g // 2) + 2 * i + g % 2

        def head_at(h):
            if small:
                i, odd = h // 2, h % 2
                return 2 * odd + i // 4, i // 4, slice(32 * (i % 4), 32 * (i % 4) + 32)
            return h // 2, h // 2, slice(64 * (h % 2), 64 * (h % 2) + 64)

        def of_unit(t, g):
            if small:
                return t.rearrange("p (a r o c) -> p r a o c", a=2, r=4, o=2)[:, g]
            return t.rearrange("p (m i s c) -> p m i s c", m=2, i=4, s=2)[:, g // 2, :, g % 2:g % 2 + 1]

        wload = {"wq": 2 * KT if small else KT, "wk": KT, "wv": KT, "wo": 1, "bo": 1}
        n_weights = sum(wload.values()) + (3 if biased else 0)

        block = ctx.enter_context(nc.Block())

        @block.sync
        def _(sp):
            def w2d(name):
                w = ins[wname[name]]
                return w if len(w.shape) == 2 else w.rearrange("d n h -> d (n h)")

            def loaded(dst, src, scattered=False):
                sp.dma_start(dst, src, allow_slow_non_contiguous=scattered).then_inc(s["weights"], 16)

            if small:
                sp.wait_ge(s["diag"], 2)
                for k in range(KT):
                    for odd in range(2):
                        dst = wq[:, k, odd * D:(odd + 1) * D].rearrange("p (i o c) -> p i o c", o=2, c=16)
                        src = w2d("wq")[k * P:(k + 1) * P, :].rearrange("p (i o c) -> p i o c", o=2, c=16)
                        loaded(dst[:, :, odd, :], src[:, :, odd, :])
            else:
                for k in range(KT):
                    loaded(wq[:, k, :], w2d("wq")[k * P:(k + 1) * P, :])
            for k in range(KT):
                loaded(wk[:, k, :], w2d("wk")[k * P:(k + 1) * P, :])
                loaded(wv[:, k, :], w2d("wv")[k * P:(k + 1) * P, :])
            wo_d = ins[wname["wo"]]
            wo_d = wo_d if len(wo_d.shape) == 2 else wo_d.rearrange("n h d -> (n h) d")
            loaded(wo[:, :, :], wo_d.rearrange("(t p) d -> p t d", p=P))
            loaded(bo[:, :], ins[wname["bo"]].rearrange("(a n) -> a n", a=1))
            if biased:
                for name, dst in (("bq", bq), ("bk", bk)):
                    flat = ins[wname[name]].rearrange("n h -> (n h)")
                    loaded(dst[:, :], flat.rearrange("(t p) -> p t", p=P), True)
                loaded(bv[:, :], ins[wname["bv"]].rearrange("(a n) h -> a (n h)", a=1))

            mask = ins[mask_name]
            if len(mask.shape) == 4:
                mask = mask.rearrange("b a q k -> b (a q) k")

            def body(j, b, first, last):
                if not isinstance(b, int):
                    evicted(sp, b - 2, 0)
                    settle(sp, s["passed"])
                    sp.wait_ge(s["mask_add"], b - 1)
                    settle(sp, s["passed"])
                sp.dma_start(ctx_in[j][:, :], one(ins["ctx_1024"], b)).then_inc(s[f"ctx_in{j}"], 16)
                sp.dma_start(mask_in[j][:, :], one(mask, b)).then_inc(s[f"mask_in{j}"], 16)

            load_batches(sp, body)

        @block.gpsimd
        def _(pool):
            nc.gpsimd.memset(mask_diag[:, :], 0.0).then_inc(s["diag"], 1)
            if small:
                nc.gpsimd.memset(wq[:, :, :], 0.0).then_inc(s["diag"], 1)
            for j in range(2):
                nc.gpsimd.memset(v1[j][:, :, head_dim], 1.0).then_inc(s["ones_col"], 1)
            pool.wait_ge(s["diag"], 2 if small else 1)
            nc.gpsimd.affine_select(out=mask_diag[:, :], in_=mask_diag[:, :], compare_op=ALU.not_equal,
                                    fill=mask_of["diag"], base=0, pattern=[[-1, P]],
                                    channel_multiplier=1).then_inc(s["diag"], 1)

        @block.tensor
        def _(pe):
            def front(j, b, f):
                kind = fills[f]
                n = j * NF + f
                dst = front_bank[n % 2]
                if not (isinstance(b, int) and b * NF + f < 2):
                    if f >= 2:
                        evicted(pe, b, f - 2)
                    else:
                        evicted(pe, b - 1, NF - 2 + f)
                if kind == "T":
                    pe.wait_ge(s["xn"], b + 1)
                    pe.wait_ge(s[f"ctx_in{j}"], loads(b, j))
                    for k in range(KT):
                        nc.tensor.transpose(dst[:, k * P:(k + 1) * P], xn[j][:, k * P:(k + 1) * P], core.ident[:, :])
                    for k in range(KT):
                        last = nc.tensor.transpose(dst[:, (KT + k) * P:(KT + k + 1) * P],
                                                   ctx_in[j][:, k * P:(k + 1) * P], core.ident[:, :])
                    last.then_inc(s["filled"], 1)
                    return
                evicted(pe, b, 0)
                if kind[0] in "QK":
                    w, of = (wq, 0) if kind[0] == "Q" else (wk, KT)
                    tiles = range(4 * int(kind[1]), 4 * int(kind[1]) + 4) if kind != "KV" else range(KTL)
                    for i, t in enumerate(tiles):
                        for k in range(KT):
                            last = nc.tensor.matmul(dst[:, i * P:(i + 1) * P], w[:, k, t * P:(t + 1) * P],
                                                    xcT[j][:, of + k, :], start=(k == 0), stop=(k == KT - 1))
                if kind in ("KV", "V0", "V1"):
                    at, w0, nw = (D, 0, E) if kind == "KV" else (0, 512 * int(kind[1]), 512)
                    for k in range(KT):
                        last = nc.tensor.matmul(dst[:, at:at + nw], xcT[j][:, KT + k, :], wv[:, k, w0:w0 + nw],
                                                start=(k == 0), stop=(k == KT - 1 and not biased))
                    if biased:
                        last = nc.tensor.matmul(dst[:, at:at + nw], core.ones[0:1, :], bv[0:1, w0:w0 + nw],
                                                start=False, stop=True)
                last.then_inc(s["filled"], 1)

            def scores(j, b, g):
                u = b * 4 + g
                dst = score_bank[g % 2]
                if g == 0:
                    for f in range(NF - 2, NF):
                        evicted(pe, b, f)
                    pe.wait_ge(s["evicted_act"], b * NA + NA)
                    if ND:
                        pe.wait_ge(s["evicted_dve"], b * ND + ND)
                    pe.wait_ge(s["mask_add"], b + 1)
                after(pe, s["shifted"], u - 1)
                nc.tensor.matmul(dst[:, :].rearrange("p (h k) -> p h k", h=4), mask_diag[:, :],
                                 mask_add[j][:, None, :].to_broadcast([P, 4, P]), start=True, stop=False)
                for i in range(4):
                    tq, tk, rows = head_at(head_of(g, i))
                    last = nc.tensor.matmul(dst[:, i * P:(i + 1) * P], qT[j][rows, tq, :], kT[j][rows, tk, :],
                                            start=False, stop=(i == 3))
                last.then_inc(s["scores"], 1)

            def transposed(j, b, g):
                u = b * 4 + g
                pe.wait_ge(s["exped"], u + 1)
                after(pe, s["pT_out"], u - 1)
                for i in range(4):
                    last = nc.tensor.transpose(pT_bank[g % 2][:, i * P:(i + 1) * P], probs[g % 2][:, i, :],
                                               core.ident[:, :])
                last.then_inc(s["pT"], 1)

            def weighted(j, b, g):
                u = b * 4 + g
                pe.wait_ge(s["pT_out"], u + 1)
                after(pe, s["normed"], u)
                for i in range(4):
                    last = nc.tensor.matmul(out_bank[:, i * VW:(i + 1) * VW], probsT[g % 2][:, i, :],
                                            v1[j][:, head_of(g, i), :], start=True, stop=True)
                last.then_inc(s["pv"], 1)

            def back_transpose(j, b, t):
                pe.wait_ge(s["normed"], 4 * b + 4)
                if t == 0:
                    after(pe, s["updated"], b)
                else:
                    pe.wait_ge(s["headsT_out"], b * TB + t)
                for i in range(4 * t, min(4 * t + 4, KTL)):
                    last = nc.tensor.transpose(back_bank[:, (i - 4 * t) * P:(i - 4 * t + 1) * P],
                                               heads[j][:, i * P:(i + 1) * P], core.ident[:, :])
                last.then_inc(s["headsT"], 1)

            def back_project(j, b):
                pe.wait_ge(s["headsT_out"], (b + 1) * TB)
                for i in range(KTL):
                    nc.tensor.matmul(back_bank[:, 0:D], headsT[:, i, :], wo[:, i, :], start=(i == 0), stop=False)
                nc.tensor.matmul(back_bank[:, 0:D], core.ones[0:1, :], bo[0:1, :],
                                 start=False, stop=True).then_inc(s["projected"], 1)

            def body(j, b, first, last):
                for g in range(4):
                    if g < 3:
                        scores(j, b, g + 1)
                    elif not last:
                        scores(1 - j, b + 1, 0)
                    transposed(j, b, g)
                    if not last:
                        for f in slots[g]:
                            front(1 - j, b + 1, f)
                    if not first and g < TB:
                        back_transpose(1 - j, b - 1, g)
                    if not first and g == TB:
                        back_project(1 - j, b - 1)
                    weighted(j, b, g)

            pe.wait_ge(s["weights"], 16 * n_weights)
            pe.wait_ge(s["diag"], 3 if small else 2)
            pe.wait_ge(s["ones_col"], 2)
            for f in range(NF):
                front(0, 0, f)
            scores(0, 0, 0)
            over_batches(pe, body)
            for t in range(TB):
                back_transpose(1, B - 1, t)
            back_project(1, B - 1)

        @block.scalar
        def _(act):
            def take(j, b, f):
                if by_dve[f]:
                    return
                n = j * NF + f
                src = front_bank[n % 2]
                kind = fills[f]
                act.wait_ge(s["filled"], b * NF + f + 1)
                after(act, s["pv"], 4 * (b - 1))
                if kind == "T":
                    nc.scalar.copy(xcT[j][:, :, :].rearrange("p t c -> p (t c)"), src[:, :]).then_inc(s["evicted_act"], 1)
                elif kind[0] == "Q":
                    t0 = 4 * int(kind[1])
                    nc.scalar.copy(qT[j][:, t0:t0 + 4, :].rearrange("p t c -> p (t c)"), src[:, :]
                                   ).then_inc(s["evicted_act"], 1)
                elif kind == "KV":
                    nc.scalar.copy(kT[j][:, :, :].rearrange("p t c -> p (t c)"), src[:, 0:E])
                    nc.scalar.copy(v1[j][:, :, 0:head_dim], src[:, D:D + E].rearrange("p (h c) -> p h c", c=head_dim)
                                   ).then_inc(s["evicted_act"], 1)
                else:
                    h0 = 8 * int(kind[1])
                    nc.scalar.copy(v1[j][:, h0:h0 + 8, 0:head_dim],
                                   src[:, :].rearrange("p (h c) -> p h c", c=head_dim)).then_inc(s["evicted_act"], 1)

            def exp(b, g):
                u = b * 4 + g
                act.wait_ge(s["shifted"], u + 1)
                after(act, s["pT"], u - 1)
                nc.scalar.activation(probs[g % 2][:, :, :], shifted[g % 2][:, :, :], ACT.Exp, scale=scale
                                     ).then_inc(s["exped"], 1)

            def take_pT(b, g):
                u = b * 4 + g
                act.wait_ge(s["pT"], u + 1)
                after(act, s["pv"], u - 1)
                nc.scalar.copy(probsT[g % 2][:, :, :].rearrange("p h q -> p (h q)"), pT_bank[g % 2][:, :]
                               ).then_inc(s["pT_out"], 1)

            def take_headsT(b, t):
                act.wait_ge(s["headsT"], b * TB + t + 1)
                after(act, s["projected"], b)
                n = min(4, KTL - 4 * t)
                nc.scalar.copy(headsT[:, 4 * t:4 * t + n, :].rearrange("p t c -> p (t c)"), back_bank[:, 0:n * P]
                               ).then_inc(s["headsT_out"], 1)

            def body(j, b, first, last):
                for g in range(4):
                    take_pT(b, g)
                    if g < 3:
                        exp(b, g + 1)
                    if not last:
                        for f in slots[g]:
                            take(1 - j, b + 1, f)
                    if not first and g < TB:
                        take_headsT(b - 1, g)
                    if g == 3 and not last:
                        exp(b + 1, 0)

            finish_norm_scalar(core, act, s, temps)
            for f in range(NF):
                take(0, 0, f)
            exp(0, 0)
            over_batches(act, body)
            for t in range(TB):
                take_headsT(B - 1, t)

        @block.vector
        def _(dve):
            def prepare(j, b):
                if not isinstance(b, int) or b >= 2:
                    evicted(dve, b - 2, 0)
                normalise(core, xn[j][:, :], b).then_inc(s["xn"], 1)
                dve.wait_ge(s[f"mask_in{j}"], loads(b, j))
                after(dve, s["scores"], 4 * (b - 1))
                nc.vector.tensor_scalar(mask_add[j][:, :], mask_in[j][:, :], mask_of["compare"], mask_of["times"],
                                        mask_of["op"], ALU.mult).then_inc(s["mask_add"], 1)

            def take(j, b, f):
                if not by_dve[f]:
                    return
                src = front_bank[(j * NF + f) % 2]
                kind = fills[f]
                dst, bias = (qT, bq) if kind[0] == "Q" else (kT, bk)
                t0 = 4 * int(kind[1])
                dve.wait_ge(s["filled"], b * NF + f + 1)
                after(dve, s["scores"], 4 * (b - 1))
                nc.vector.tensor_tensor(dst[j][:, t0:t0 + 4, :], src[:, :].rearrange("p (t c) -> p t c", t=4),
                                        bias[:, t0:t0 + 4, None].to_broadcast([P, 4, P]), ALU.add
                                        ).then_inc(s["evicted_dve"], 1)

            def shift(b, g):
                u = b * 4 + g
                src = score_bank[g % 2][:, :].rearrange("p (h k) -> p h k", h=4)
                dve.wait_ge(s["scores"], u + 1)
                nc.vector.tensor_reduce(top[:, g % 2, :], src, AX.X, ALU.max).then_inc(s["maxed"], 1)
                dve.wait_ge(s["maxed"], u + 1)
                after(dve, s["exped"], u - 1)
                nc.vector.tensor_tensor(shifted[g % 2][:, :, :], src,
                                        top[:, g % 2, :][:, :, None].to_broadcast([P, 4, P]), ALU.subtract
                                        ).then_inc(s["shifted"], 1)

            def norm(j, b, g):
                u = b * 4 + g
                pairs = dict(a=2, o=2) if small else dict(a=4, o=1)
                src = out_bank[:, 0:4 * VW].rearrange("p (h c) -> p h c", h=4)
                src4 = out_bank[:, 0:4 * VW].rearrange("p (a o c) -> p a o c", **pairs)
                inv4 = inv_sum[:, g % 2, :].rearrange("p (a o) -> p a o", **pairs)
                dve.wait_ge(s["pv"], u + 1)
                nc.vector.reciprocal(inv_sum[:, g % 2, :], src[:, :, head_dim]).then_inc(s["inv"], 1)
                dve.wait_ge(s["inv"], u + 1)
                after(dve, s["projected"], b - 1)
                nc.vector.tensor_tensor(of_unit(heads[j][:, :], g), src4[:, :, :, 0:head_dim],
                                        inv4[:, :, :, None].to_broadcast([P, pairs["a"], pairs["o"], head_dim]),
                                        ALU.mult
                                        ).then_inc(s["normed"], 1)

            def update(b):
                dve.wait_ge(s["projected"], b + 1)
                nc.vector.scalar_tensor_tensor(cols(core.x, b * D, D), back_bank[:, 0:D], core.gate(layer, 0),
                                               cols(core.x, b * D, D), ALU.mult, ALU.add).then_inc(s["updated"], 1)
                dve.wait_ge(s["updated"], b + 1)
                take_stats(core, b)

            def body(j, b, first, last):
                for g in range(4):
                    if g < 3:
                        shift(b, g + 1)
                    if not last:
                        if g == 0:
                            prepare(1 - j, b + 1)
                        for f in slots[g]:
                            take(1 - j, b + 1, f)
                        if g == 3:
                            shift(b + 1, 0)
                    norm(j, b, g)
                    if not first and g == TB:
                        update(b - 1)

            finish_norm_vector(core, dve, s, temps)
            if biased:
                dve.wait_ge(s["weights"], 16 * n_weights)
            prepare(0, 0)
            for f in range(NF):
                take(0, 0, f)
            shift(0, 0)
            over_batches(dve, body)
            update(B - 1)


def one(ap, b):
    return ap[bass.ds(b, 1)].rearrange("a p d -> (a p) d")


def load_batches(sp, body):
    body(0, 0, True, False)
    body(1, 1, False, False)
    with sp.Fori(1, B // 2) as i:
        body(0, i * 2, False, False)
        body(1, i * 2 + 1, False, False)


L0_X = dict(wq="L0_xattn_wq", wk="L0_xattn_wk", wv="L0_xattn_wv", wo="L0_xattn_wo", bo="L0_xattn_bo")
L2_X = dict(wq="L2_xattn_Wq", wk="L2_xattn_Wk", wv="L2_xattn_Wv", wo="L2_xattn_Wo", bo="L2_xattn_bo",
            bq="L2_xattn_bq", bk="L2_xattn_bk", bv="L2_xattn_bv")
L0_MASK = dict(compare=0.0, times=-1e10, op=ALU.is_equal, diag=1.0)
L2_MASK = dict(compare=1.0, times=800.0, op=ALU.subtract, diag=100.0)


def depth_routed_block(core):
    nc, ins = core.nc, core.ins
    tag = "L0f"
    H, HD = 16, 16
    KEEP = 15
    SLOTS = 16
    G = 2
    F = 1024
    FT = F // P
    XW = D + 2
    OFF = -1e30
    TWO_PI = 2 * np.pi
    MAGIC = 1.5 * 2.0 ** 23
    with ExitStack() as ctx:
        sb = core.sbuf_in(ctx)
        router_w = sb("router_w", [P, KT])
        router_b = sb("router_b", [P, 1])
        ln1 = sb("ln1", [P, D])
        ln2 = sb("ln2", [P, D])
        w4 = sb("L0f_w4", [P, 4, KT, D])
        w1 = sb("L0f_w1", [P, KT, F])
        w2 = sb("L0f_w2", [P, FT, D])
        attn_mask = sb("attn_mask", [P, 4, P])
        pos_in = sb("pos_in", [P, 4], I32)
        pos = sb("pos", [P, B])
        temps = sb("L0f_temps", [P, 4, B])
        column = sb("L0f_column", [P, P])
        earlier = sb("earlier", [P, P])
        first_slot = sb("first_slot", [P, B])
        apart = sb("apart", [P, P])
        weight = sb("weight", [P, B])
        above = sb("above", [P, B])
        equal = sb("equal", [P, B])
        at_least = sb("at_least", [P, B])
        slot = sb("slot", [P, B])
        unchosen = sb("unchosen", [P, B])
        xn = [sb(f"L0f_xn{j}", [P, D]) for j in range(2)]
        xT = [sb(f"L0f_xT{j}", [P, D]) for j in range(2)]
        x_aug = [sb(f"x_aug{j}", [P, XW]) for j in range(2)]
        spread = [sb(f"spread{j}", [P, P]) for j in range(2)]
        junk = [sb(f"L0f_junk{j}", [P, P]) for j in range(3)]
        pick = [sb(f"pick{j}", [P, P]) for j in range(2)]
        masked = [sb(f"masked{j}", [P, P]) for j in range(2)]
        zero_row = sb("zero_row", [1, XW])
        chosen = sb("chosen", [P, G, XW])
        mask = sb("L0f_mask", [P, G, P])
        result = sb("L0f_result", [P, G, D])
        bank = core.banks_in(ctx, tag)
        s = core.sems_in(tag, NORM_SEMS + [
            "router", "weights", "small", "consts", "xn", "T", "T_out", "w", "w_out", "spread", "row", "counted",
            "step", "slots", "aug", "pick", "U", "U_out", "gathered", "mask_in"])
        phases = Phases(nc)

        block = phases.open()

        @block.sync
        def _(sp):
            sp.dma_start(router_w[:, :], ins["L0_ffn_router_w"].rearrange("(k p) a -> p (k a)", p=P),
                         allow_slow_non_contiguous=True).then_inc(s["router"], 16)
            sp.dma_start(router_b[:, :], ins["L0_ffn_router_b"].rearrange("(a n) -> a n", a=1).to_broadcast([P, 1])
                         ).then_inc(s["router"], 16)
            sp.dma_start(pos_in[:, :], ins["L0_ffn_position_ids"][:, 0:P].rearrange("b s -> s b"),
                         allow_slow_non_contiguous=True).then_inc(s["router"], 16)
            sp.dma_start(attn_mask[:, :, :], ins["L0_ffn_attention_mask"][:, 0, 0:P, 0:P].rearrange("b q k -> q b k")
                         ).then_inc(s["mask_in"], 16)
            for n, name in enumerate(("wq", "wk", "wv", "wo")):
                sp.dma_start(w4[:, n, :, :], ins[f"L0_ffn_{name}"].rearrange("(k p) n -> p k n", p=P)
                             ).then_inc(s["weights"], 16)
            sp.dma_start(w1[:, :, :], ins["L0_ffn_w1"].rearrange("(k p) n -> p k n", p=P)).then_inc(s["weights"], 16)
            sp.dma_start(w2[:, :, :], ins["L0_ffn_w2"].rearrange("(k p) n -> p k n", p=P)).then_inc(s["weights"], 16)
            for name, dst in (("ln1", ln1), ("ln2", ln2)):
                sp.dma_start(dst[:, :], ins[f"L0_ffn_{name}"].rearrange("(a n) -> a n", a=1).to_broadcast([P, D])
                             ).then_inc(s["weights"], 16)
            sp.wait_ge(s["weights"], 16 * 8)

        @block.gpsimd
        def _(pool):
            nc.gpsimd.iota(column[:, :], [[1, P]], 0, 0, allow_small_or_imprecise_dtypes=True).then_inc(s["consts"], 1)
            nc.gpsimd.memset(zero_row[:, :], 0.0).then_inc(s["consts"], 1)
            nc.gpsimd.iota(first_slot[:, :], [[0, G], [SLOTS, B // G]], 0, 0, allow_small_or_imprecise_dtypes=True
                           ).then_inc(s["consts"], 1)
            nc.gpsimd.memset(earlier[:, :], 1.0).then_inc(s["small"], 1)
            nc.gpsimd.memset(apart[:, :], 0.0).then_inc(s["small"], 1)
            pool.wait_ge(s["small"], 2)
            nc.gpsimd.affine_select(out=earlier[:, :], in_=earlier[:, :], compare_op=ALU.is_gt, fill=0.0, base=0,
                                    pattern=[[-1, P]], channel_multiplier=1).then_inc(s["consts"], 1)
            blocks = apart[:, :].rearrange("p (k c) -> p k c", c=SLOTS)
            nc.gpsimd.affine_select(out=blocks, in_=blocks, compare_op=ALU.is_ge, fill=OFF, base=0,
                                    pattern=[[-SLOTS, P // SLOTS], [0, SLOTS]], channel_multiplier=1
                                    ).then_inc(s["small"], 1)
            pool.wait_ge(s["small"], 3)
            nc.gpsimd.affine_select(out=blocks, in_=blocks, compare_op=ALU.is_ge, fill=OFF, base=SLOTS - 1,
                                    pattern=[[SLOTS, P // SLOTS], [0, SLOTS]], channel_multiplier=-1
                                    ).then_inc(s["small"], 1)
            pool.wait_ge(s["small"], 4)
            nc.gpsimd.memset(blocks[:, :, KEEP], OFF).then_inc(s["consts"], 1)

        @block.tensor
        def _(pe):
            def transposed(j, b):
                pe.wait_ge(s["xn"], b + 1)
                after(pe, s["T_out"], b - 1)
                for k in range(KT):
                    t = nc.tensor.transpose(bank[j][:, k * P:(k + 1) * P], xn[j][:, k * P:(k + 1) * P],
                                            core.ident[:, :])
                t.then_inc(s["T"], 1)

            def route(j, b, first, last):
                if not last:
                    transposed(1 - j, b + 1)
                pe.wait_ge(s["T_out"], b + 1)
                after(pe, s["w_out"], b - 1)
                for k in range(KT):
                    t = nc.tensor.matmul(bank[2 + j][:, 0:1], xT[j][:, k * P:(k + 1) * P], router_w[:, k:k + 1],
                                         start=(k == 0), stop=(k == KT - 1))
                t.then_inc(s["w"], 1)

            def row(j, b, first, last):
                pe.wait_ge(s["spread"], b + 1)
                after(pe, s["counted"], b - 1)
                nc.tensor.matmul(bank[j][:, 0:P], core.ones[:, :], spread[j][:, :], start=True, stop=True
                                 ).then_inc(s["row"], 1)

            def gather(j, b, m, tile):
                pe.wait_ge(s["pick"], b + 1)
                after(pe, s["U_out"], b - 1)
                nc.tensor.matmul(bank[j][:, 0:P], attn_mask[:, m, :], pick[j][:, :], start=True, stop=True
                                 ).then_inc(s["U"], 1)
                pe.wait_ge(s["aug"], b + 1)
                nc.tensor.matmul(bank[4 + tile][:, 0:XW], pick[j][:, :], x_aug[j][:, :], start=False, stop=False)
                pe.wait_ge(s["U_out"], b + 1)
                nc.tensor.matmul(bank[6 + tile][:, 0:P], masked[j][:, :], pick[j][:, :], start=False, stop=False
                                 ).then_inc(s["gathered"], 1)

            def zero(tile, start, stop):
                nc.tensor.matmul(bank[4 + tile][:, 0:XW], zero_row[0:1, 0:P], zero_row[0:1, :],
                                 start=start, stop=stop)
                nc.tensor.matmul(bank[6 + tile][:, 0:P], zero_row[0:1, 0:P], zero_row[0:1, 0:P],
                                 start=start, stop=stop)

            pe.wait_ge(s["router"], 48)
            pe.wait_ge(s["consts"], 5)
            transposed(0, 0)
            over_batches(pe, route)
            over_batches(pe, row)
            pe.wait_ge(s["mask_in"], 16)
            for tile in range(G):
                zero(tile, True, False)
            for b in range(4):
                gather(b % 2, b, b, 0)
            with pe.Fori(2, 4) as i:
                for j in range(2):
                    gather(j, i * 2 + j, 3, 0)
            with pe.Fori(4, 8) as i:
                for j in range(2):
                    gather(j, i * 2 + j, 3, 1)
            for tile in range(G):
                zero(tile, False, True)

        @block.scalar
        def _(act):
            def take_T(j, b, first, last):
                act.wait_ge(s["T"], b + 1)
                after(act, s["w"], b - 1)
                nc.scalar.copy(xT[j][:, :], bank[j][:, 0:D]).then_inc(s["T_out"], 1)

            def take_U(j, b, first, last):
                act.wait_ge(s["U"], b + 1)
                after(act, s["gathered"], b - 1)
                nc.scalar.copy(masked[j][:, :], bank[j][:, 0:P]).then_inc(s["U_out"], 1)

            finish_norm_scalar(core, act, s, temps)
            over_batches(act, take_T)
            over_batches(act, take_U)

        @block.vector
        def _(dve):
            def norm(j, b):
                after(dve, s["T"], b - 1)
                normalise(core, xn[j][:, :], b).then_inc(s["xn"], 1)

            def route(j, b, first, last):
                if not last:
                    norm(1 - j, b + 1)
                dve.wait_ge(s["w"], b + 1)
                nc.vector.tensor_tensor(cols(weight, b, 1), bank[2 + j][:, 0:1], router_b[:, :], ALU.add
                                        ).then_inc(s["w_out"], 1)

            def diagonal(j, b):
                after(dve, s["row"], b - 1)
                nc.vector.tensor_scalar(spread[j][:, :], core.ident[:, :], cols(weight, b, 1), None, ALU.mult
                                        ).then_inc(s["spread"], 1)

            def count(j, b, first, last):
                if not last:
                    diagonal(1 - j, b + 1)
                dve.wait_ge(s["row"], b + 1)
                src = bank[j][:, 0:P]
                after(dve, s["counted"], b)
                nc.vector.tensor_scalar(junk[0][:, :], src, cols(weight, b, 1), 0.0, ALU.is_gt, ALU.add,
                                        accum_out=cols(above, b, 1))
                nc.vector.scalar_tensor_tensor(junk[1][:, :], src, cols(weight, b, 1), earlier[:, :],
                                               ALU.is_equal, ALU.mult, accum_out=cols(equal, b, 1))
                nc.vector.tensor_scalar(junk[2][:, :], src, cols(weight, b, 1), 0.0, ALU.is_ge, ALU.add,
                                        accum_out=cols(at_least, b, 1)).then_inc(s["counted"], 1)

            def pick_tokens(j, b, first, last):
                after(dve, s["gathered"], b - 1)
                nc.vector.tensor_scalar(pick[j][:, :], column[:, :], cols(slot, b, 1), None, ALU.is_equal
                                        ).then_inc(s["pick"], 1)
                nc.vector.tensor_copy(x_aug[j][:, D:D + 1], cols(pos, b, 1))
                nc.vector.tensor_copy(x_aug[j][:, D + 1:D + 2], cols(weight, b, 1))
                normalise(core, x_aug[j][:, 0:D], b).then_inc(s["aug"], 1)

            finish_norm_vector(core, dve, s, temps)
            dve.wait_ge(s["router"], 48)
            dve.wait_ge(s["consts"], 5)
            norm(0, 0)
            over_batches(dve, route)
            dve.wait_ge(s["w_out"], B)
            diagonal(0, 0)
            over_batches(dve, count)
            dve.wait_ge(s["counted"], B)
            link = chain(dve, s["step"], 0)
            link(nc.vector.tensor_copy(pos[:, 0:4], pos_in[:, :]))
            link(nc.vector.tensor_copy(pos[:, 4:B], pos[:, 3:4].to_broadcast([P, B - 4])))
            link(nc.vector.tensor_tensor(slot[:, :], above[:, :], equal[:, :], ALU.add))
            link(nc.vector.tensor_scalar(equal[:, :], slot[:, :], float(KEEP), 1000.0, ALU.is_ge, ALU.mult))
            link(nc.vector.tensor_tensor(slot[:, :], slot[:, :], equal[:, :], ALU.add))
            link(nc.vector.tensor_tensor(slot[:, :], slot[:, :], first_slot[:, :], ALU.add))
            link(nc.vector.tensor_scalar(unchosen[:, :], at_least[:, :], float(KEEP), None, ALU.is_gt))
            over_batches(dve, pick_tokens)

        t1 = core.sems_in("L0t", [
            "zeros", "chosen", "sq", "ss", "root", "inv", "hn", "hT", "hT_out", "qkv", "v_out", "angle", "sin",
            "rope", "spread_q", "qkT", "qkT_out", "scores", "masked", "exped", "pT", "pT_out", "pv", "normed", "oT",
            "oT_out", "o", "x1", "up", "gelu", "down", "done", "step"])
        freq = sb("freq", [P, HD // 2])
        ang = sb("ang", [P, G, 2, HD // 2])
        turns = sb("turns", [P, G, 2, HD // 2])
        sincos = sb("sincos", [P, G, 2, HD // 2])
        ss = sb("ss", [P, 4, G])
        hn = sb("hn", [P, G, D])
        hT = sb("hT", [P, G, KT, P])
        rot = [sb(f"rot{i}", [P, 2 * D]) for i in range(2)]
        qk = sb("qk", [P, G, 2 * D])
        q_eo = sb("q_eo", [P, G, 2, D])
        v1 = sb("L0f_v1", [P, G, H, HD + 1])
        qT = sb("L0f_qT", [P, G, 4, P])
        kT = sb("L0f_kT", [P, G, KT, P])
        top = sb("L0f_top", [P, 2, 4])
        shifted = [sb(f"L0f_shifted{j}", [P, 4, P]) for j in range(2)]
        probs = [sb(f"L0f_probs{j}", [P, 4, P]) for j in range(2)]
        probsT = [sb(f"L0f_probsT{j}", [P, 4, P]) for j in range(2)]
        inv_sum = sb("L0f_inv", [P, 2, 4])
        heads = sb("L0f_heads", [P, G, D])
        x1 = sb("x1", [P, G, D])
        hid = sb("hid", [P, FT, G * P])
        inv_freq = [float(np.float32(1.0) / np.float32(10000.0) ** (np.float32(2 * i) / np.float32(HD)))
                    for i in range(HD // 2)]

        block = phases.open()

        @block.gpsimd
        def _(pool):
            nc.gpsimd.memset(q_eo[:, :, :, :], 0.0).then_inc(t1["zeros"], 1)
            for g in range(G):
                nc.gpsimd.memset(v1[:, g, :, HD], 1.0).then_inc(t1["zeros"], 1)
            for i, f in enumerate(inv_freq):
                nc.gpsimd.memset(freq[:, i:i + 1], f).then_inc(t1["zeros"], 1)

        def head_at(h):
            i, odd = h // 2, h % 2
            return 2 * odd + i // 4, i // 4, slice(32 * (i % 4), 32 * (i % 4) + 32)

        @block.tensor
        def _(pe):
            def transpose_rows(src, n):
                for g in range(G):
                    for k in range(KT):
                        t = nc.tensor.transpose(bank[0][:, (g * KT + k) * P:(g * KT + k + 1) * P],
                                                src[:, g, k * P:(k + 1) * P], core.ident[:, :])
                t.then_inc(t1["hT"], 1)

            pe.wait_ge(t1["hn"], 1)
            transpose_rows(hn, 0)
            pe.wait_ge(t1["hT_out"], 1)
            for g in range(G):
                for n in range(3):
                    dst = bank[1 + g][:, n * D:(n + 1) * D] if n < 2 else bank[3][:, g * D:(g + 1) * D]
                    for k in range(KT):
                        t = nc.tensor.matmul(dst, hT[:, g, k, :], w4[:, n, k, :], start=(k == 0), stop=(k == KT - 1))
            t.then_inc(t1["qkv"], 1)
            pe.wait_ge(t1["spread_q"], 1)
            for g in range(G):
                after(pe, t1["qkT_out"], 2 * g)
                for i in range(4):
                    nc.tensor.transpose(bank[4][:, i * P:(i + 1) * P],
                                        q_eo[:, g, i // 2, (i % 2) * P:(i % 2 + 1) * P], core.ident[:, :])
                for k in range(KT):
                    t = nc.tensor.transpose(bank[5][:, k * P:(k + 1) * P],
                                            qk[:, g, D + k * P:D + (k + 1) * P], core.ident[:, :])
                t.then_inc(t1["qkT"], 1)
            pe.wait_ge(t1["qkT_out"], 4)
            pe.wait_ge(t1["v_out"], 1)

            def scores(u):
                g, r = u // 4, u % 4
                after(pe, t1["masked"], u - 1)
                for i in range(4):
                    tq, tk, rows = head_at(2 * r + 8 * (i // 2) + i % 2)
                    t = nc.tensor.matmul(bank[6 + u % 2][:, i * P:(i + 1) * P], qT[rows, g, tq, :], kT[rows, g, tk, :],
                                         start=True, stop=True)
                t.then_inc(t1["scores"], 1)

            scores(0)
            for u in range(8):
                g, r = u // 4, u % 4
                if u < 7:
                    scores(u + 1)
                pe.wait_ge(t1["exped"], u + 1)
                after(pe, t1["pT_out"], u - 1)
                for i in range(4):
                    t = nc.tensor.transpose(bank[4 + u % 2][:, i * P:(i + 1) * P], probs[u % 2][:, i, :],
                                            core.ident[:, :])
                t.then_inc(t1["pT"], 1)
                pe.wait_ge(t1["pT_out"], u + 1)
                after(pe, t1["normed"], u)
                for i in range(4):
                    t = nc.tensor.matmul(bank[1][:, i * (HD + 1):(i + 1) * (HD + 1)], probsT[u % 2][:, i, :],
                                         v1[:, g, 2 * r + 8 * (i // 2) + i % 2, :], start=True, stop=True)
                t.then_inc(t1["pv"], 1)
            pe.wait_ge(t1["normed"], 8)
            transpose_rows(heads, 1)
            pe.wait_ge(t1["hT_out"], 2)
            for g in range(G):
                for k in range(KT):
                    t = nc.tensor.matmul(bank[2][:, g * D:(g + 1) * D], hT[:, g, k, :], w4[:, 3, k, :],
                                         start=(k == 0), stop=(k == KT - 1))
            t.then_inc(t1["o"], 1)
            pe.wait_ge(t1["hn"], 2)
            transpose_rows(hn, 2)
            pe.wait_ge(t1["hT_out"], 3)
            for m in range(FT):
                for k in range(KT):
                    t = nc.tensor.matmul(bank[4 + m // 2][:, (m % 2) * G * P:(m % 2 + 1) * G * P]
                                         .rearrange("p (g c) -> p g c", g=G), w1[:, k, m * P:(m + 1) * P],
                                         hT[:, :, k, :], start=(k == 0), stop=(k == KT - 1))
                if m % 2:
                    t.then_inc(t1["up"], 1)
            pe.wait_ge(t1["gelu"], 4)
            for g in range(G):
                for m in range(FT):
                    t = nc.tensor.matmul(bank[3][:, g * D:(g + 1) * D], hid[:, m, g * P:(g + 1) * P], w2[:, m, :],
                                         start=(m == 0), stop=(m == FT - 1))
            t.then_inc(t1["down"], 1)

        @block.scalar
        def _(act):
            def square(src, n):
                for g in range(G):
                    t = nc.scalar.activation(hn[:, g, :], src[:, g, 0:D], ACT.Square, accum_out=ss[:, 0, g:g + 1])
                t.then_inc(t1["sq"], 1)
                act.wait_ge(t1["ss"], n + 1)
                nc.scalar.activation(ss[:, 2, :], ss[:, 1, :], ACT.Sqrt).then_inc(t1["root"], 1)

            def take_hT(n):
                act.wait_ge(t1["hT"], n + 1)
                nc.scalar.copy(hT[:, :, :, :].rearrange("p g k c -> p (g k c)"), bank[0][:, :]).then_inc(t1["hT_out"], 1)

            act.wait_ge(t1["chosen"], 1)
            square(chosen, 0)
            act.wait_ge(t1["angle"], 1)
            nc.scalar.activation(sincos[:, :, :, :].rearrange("p g t i -> p (g t i)"),
                                 ang[:, :, :, :].rearrange("p g t i -> p (g t i)"), ACT.Sin).then_inc(t1["sin"], 1)
            take_hT(0)
            act.wait_ge(t1["qkv"], 1)
            act.wait_ge(t1["zeros"], 3)
            for g in range(G):
                t = nc.scalar.copy(v1[:, g, :, 0:HD], bank[3][:, g * D:(g + 1) * D].rearrange("p (h c) -> p h c", c=HD))
            t.then_inc(t1["v_out"], 1)
            act.wait_ge(t1["rope"], 2)
            act.wait_ge(t1["zeros"], 1)
            for g in range(G):
                for odd in range(2):
                    dst = q_eo[:, g, odd, :].rearrange("p (i o c) -> p i o c", o=2, c=HD)
                    src = qk[:, g, 0:D].rearrange("p (i o c) -> p i o c", o=2, c=HD)
                    t = nc.scalar.copy(dst[:, :, odd, :], src[:, :, odd, :])
            t.then_inc(t1["spread_q"], 1)
            for g in range(G):
                act.wait_ge(t1["qkT"], g + 1)
                nc.scalar.copy(qT[:, g, :, :].rearrange("p t c -> p (t c)"), bank[4][:, :]).then_inc(t1["qkT_out"], 1)
                nc.scalar.copy(kT[:, g, :, :].rearrange("p t c -> p (t c)"), bank[5][:, 0:D]).then_inc(t1["qkT_out"], 1)

            def exp(u):
                act.wait_ge(t1["masked"], u + 1)
                after(act, t1["pT"], u - 1)
                nc.scalar.activation(probs[u % 2][:, :, :], shifted[u % 2][:, :, :], ACT.Exp).then_inc(t1["exped"], 1)

            exp(0)
            for u in range(8):
                if u < 7:
                    exp(u + 1)
                act.wait_ge(t1["pT"], u + 1)
                after(act, t1["pv"], u - 1)
                nc.scalar.copy(probsT[u % 2][:, :, :].rearrange("p h c -> p (h c)"), bank[4 + u % 2][:, :]
                               ).then_inc(t1["pT_out"], 1)
            take_hT(1)
            act.wait_ge(t1["x1"], 1)
            square(x1, 1)
            take_hT(2)
            for m in range(FT // 2):
                act.wait_ge(t1["up"], m + 1)
                nc.scalar.activation(hid[:, 2 * m:2 * m + 2, :].rearrange("p m c -> p (m c)"), bank[4 + m][:, :],
                                     ACT.Gelu_apprx_tanh).then_inc(t1["gelu"], 1)

        @block.vector
        def _(dve):
            link = chain(dve, t1["step"], 0)

            def rms(src, ln, n):
                dve.wait_ge(t1["sq"], n + 1)
                nc.vector.tensor_scalar(ss[:, 1, :], ss[:, 0, :], 1.0 / D, 1e-6, ALU.mult, ALU.add
                                        ).then_inc(t1["ss"], 1)
                dve.wait_ge(t1["root"], n + 1)
                link(nc.vector.reciprocal(ss[:, 3, :], ss[:, 2, :]))
                for g in range(G):
                    t = nc.vector.scalar_tensor_tensor(hn[:, g, :], src[:, g, 0:D], ss[:, 3, g:g + 1], ln[:, :],
                                                       ALU.mult, ALU.mult)
                t.then_inc(t1["hn"], 1)

            for g in range(G):
                t = nc.vector.tensor_copy(chosen[:, g, :], bank[4 + g][:, 0:XW])
            t.then_inc(t1["chosen"], 1)
            for g in range(G):
                nc.vector.tensor_tensor(mask[:, g, :], bank[6 + g][:, 0:P], apart[:, :], ALU.add)
            dve.wait_ge(t1["chosen"], 1)
            dve.wait_ge(t1["zeros"], 11)
            for g in range(G):
                link(nc.vector.tensor_scalar(ang[:, g, 0, :], freq[:, :], chosen[:, g, D:D + 1], None, ALU.mult))
            turn_hi = float(np.float32(TWO_PI).view(np.uint32) & np.uint32(0xFFFFF000)
                            if False else np.float32(6.28125))
            turn_mid = float(np.float32(np.floor((TWO_PI - turn_hi) * 2.0 ** 21) / 2.0 ** 21))
            turn_lo = float(np.float32(TWO_PI - turn_hi - turn_mid))
            link(nc.vector.tensor_scalar(turns[:, :, 0, :], ang[:, :, 0, :], 1.0 / TWO_PI, MAGIC, ALU.mult, ALU.add))
            link(nc.vector.tensor_scalar(turns[:, :, 0, :], turns[:, :, 0, :], -MAGIC, None, ALU.add))
            link(nc.vector.tensor_scalar(turns[:, :, 1, :], ang[:, :, 0, :], 1.0 / TWO_PI, 0.25, ALU.mult, ALU.add))
            link(nc.vector.tensor_scalar(turns[:, :, 1, :], turns[:, :, 1, :], MAGIC, None, ALU.add))
            link(nc.vector.tensor_scalar(turns[:, :, 1, :], turns[:, :, 1, :], -MAGIC, None, ALU.add))
            link(nc.vector.tensor_copy(ang[:, :, 1, :], ang[:, :, 0, :]))
            ang2 = ang[:, :, :, :].rearrange("p g t i -> p (g t i)")
            turns2 = turns[:, :, :, :].rearrange("p g t i -> p (g t i)")
            for part in (turn_hi, turn_mid, turn_lo):
                link(nc.vector.scalar_tensor_tensor(ang2, turns2, -part, ang2, ALU.mult, ALU.add))
            link(nc.vector.tensor_scalar(ang[:, :, 1, :], ang[:, :, 1, :], float(np.pi / 2), None, ALU.add))
            link(nc.vector.tensor_scalar(ang2, ang2, -3.14159, 3.14159, ALU.max, ALU.min))
            dve.sem_inc(t1["angle"], 1)
            rms(chosen, ln1, 0)
            dve.wait_ge(t1["qkv"], 1)
            dve.wait_ge(t1["sin"], 1)
            HH = HD // 2
            for g in range(G):
                src = bank[1 + g][:, :].rearrange("p (h t i) -> p h t i", t=2, i=HH)
                dst = qk[:, g, :].rearrange("p (h t i) -> p h t i", t=2, i=HH)
                a = rot[0][:, :].rearrange("p (t h i) -> p t h i", t=2, i=HH)
                c = rot[1][:, :].rearrange("p (t h i) -> p t h i", t=2, i=HH)
                sin = sincos[:, g, 0, None, :].to_broadcast([P, 2 * H, HH])
                cos = sincos[:, g, 1, None, :].to_broadcast([P, 2 * H, HH])
                for t in range(2):
                    nc.vector.tensor_tensor(a[:, t], src[:, :, t, :], cos, ALU.mult)
                    link(nc.vector.tensor_tensor(c[:, t], src[:, :, 1 - t, :], sin, ALU.mult))
                nc.vector.tensor_tensor(dst[:, :, 0, :], a[:, 0], c[:, 0], ALU.subtract)
                link(nc.vector.tensor_tensor(dst[:, :, 1, :], a[:, 1], c[:, 1], ALU.add))
                dve.sem_inc(t1["rope"], 1)

            def shift(u):
                g, j = u // 4, u % 2
                src = bank[6 + j][:, :].rearrange("p (h k) -> p h k", h=4)
                dve.wait_ge(t1["scores"], u + 1)
                after(dve, t1["exped"], u - 1)
                link(nc.vector.scalar_tensor_tensor(shifted[j][:, :, :], src, HD ** -0.5,
                                                    mask[:, g, None, :].to_broadcast([P, 4, P]), ALU.mult, ALU.add))
                link(nc.vector.tensor_reduce(top[:, j, :], shifted[j][:, :, :], AX.X, ALU.max))
                nc.vector.tensor_tensor(shifted[j][:, :, :], shifted[j][:, :, :],
                                        top[:, j, :][:, :, None].to_broadcast([P, 4, P]), ALU.subtract
                                        ).then_inc(t1["masked"], 1)

            shift(0)
            for u in range(8):
                g, r = u // 4, u % 4
                if u < 7:
                    shift(u + 1)
                dve.wait_ge(t1["pv"], u + 1)
                src = bank[1][:, 0:4 * (HD + 1)].rearrange("p (h c) -> p h c", h=4)
                src4 = bank[1][:, 0:4 * (HD + 1)].rearrange("p (a o c) -> p a o c", a=2, o=2)
                link(nc.vector.reciprocal(inv_sum[:, u % 2, :], src[:, :, HD]))
                inv4 = inv_sum[:, u % 2, :].rearrange("p (a o) -> p a o", a=2)
                dst = heads[:, g, :].rearrange("p (a r o c) -> p r a o c", a=2, r=4, o=2)[:, r]
                nc.vector.tensor_tensor(dst, src4[:, :, :, 0:HD],
                                        inv4[:, :, :, None].to_broadcast([P, 2, 2, HD]), ALU.mult
                                        ).then_inc(t1["normed"], 1)
            dve.wait_ge(t1["o"], 1)
            for g in range(G):
                t = nc.vector.tensor_tensor(x1[:, g, :], chosen[:, g, 0:D], bank[2][:, g * D:(g + 1) * D], ALU.add)
            t.then_inc(t1["x1"], 1)
            dve.wait_ge(t1["x1"], 1)
            rms(x1, ln2, 1)
            dve.wait_ge(t1["down"], 1)
            for g in range(G):
                link(nc.vector.tensor_tensor(x1[:, g, :], x1[:, g, :], bank[3][:, g * D:(g + 1) * D], ALU.add))
                nc.vector.tensor_scalar(result[:, g, :], x1[:, g, :], chosen[:, g, D + 1:D + 2], None, ALU.mult)

        q = core.sems_in("L0b", ["pick", "xn", "pickT", "pickT_out", "out", "mixed", "updated"])
        pickT = masked
        block = phases.open()

        @block.tensor
        def _(pe):
            def transposed(j, b):
                pe.wait_ge(q["pick"], b + 1)
                after(pe, q["pickT_out"], b - 1)
                nc.tensor.transpose(bank[j][:, 0:P], pick[j][:, :], core.ident[:, :]).then_inc(q["pickT"], 1)

            def scatter(j, b, tile):
                pe.wait_ge(q["pickT_out"], b + 1)
                after(pe, q["mixed"], b - 1)
                nc.tensor.matmul(bank[2 + j][:, 0:D], pickT[j][:, :], result[:, tile, :], start=True, stop=True
                                 ).then_inc(q["out"], 1)

            def pair(i, tile, more=True):
                transposed(1, i * 2 + 1)
                scatter(0, i * 2, tile)
                if more:
                    transposed(0, i * 2 + 2)
                scatter(1, i * 2 + 1, tile)

            transposed(0, 0)
            pair(0, 0)
            with pe.Fori(1, 4) as i:
                pair(i, 0)
            with pe.Fori(4, 7) as i:
                pair(i, 1)
            pair(7, 1, False)

        @block.scalar
        def _(act):
            def body(j, b, first, last):
                act.wait_ge(q["pickT"], b + 1)
                after(act, q["out"], b - 1)
                nc.scalar.copy(pickT[j][:, :], bank[j][:, 0:P]).then_inc(q["pickT_out"], 1)

            over_batches(act, body)

        @block.vector
        def _(dve):
            def front(j, b):
                after(dve, q["pickT"], b - 1)
                after(dve, q["mixed"], b - 1)
                nc.vector.tensor_scalar(pick[j][:, :], column[:, :], cols(slot, b, 1), None, ALU.is_equal
                                        ).then_inc(q["pick"], 1)
                normalise(core, xn[j][:, :], b).then_inc(q["xn"], 1)

            def body(j, b, first, last):
                if not last:
                    front(1 - j, b + 1)
                dve.wait_ge(q["out"], b + 1)
                dve.wait_ge(q["xn"], b + 1)
                nc.vector.scalar_tensor_tensor(xT[j][:, :], xn[j][:, :], cols(unchosen, b, 1), bank[2 + j][:, 0:D],
                                               ALU.mult, ALU.add).then_inc(q["mixed"], 1)
                dve.wait_ge(q["mixed"], b + 1)
                nc.vector.scalar_tensor_tensor(cols(core.x, b * D, D), xT[j][:, :], core.gate(0, 1),
                                               cols(core.x, b * D, D), ALU.mult, ALU.add).then_inc(q["updated"], 1)
                dve.wait_ge(q["updated"], b + 1)
                take_stats(core, b)

            front(0, 0)
            over_batches(dve, body)

        phases.close()


def bidirectional_attention(core):
    nc, ins = core.nc, core.ins
    tag = "L1x"
    with ExitStack() as ctx:
        sb = core.sbuf_in(ctx)
        w_sim = sb("w_sim", [P, 3, KT])
        b_sim = sb("b_sim", [P, 1])
        w_qv = sb("w_qv", [P, 4 * KT, D])
        b_qv = sb("b_qv", [1, D])
        temps = sb("L1x_temps", [P, 4, B])
        neg_max = sb("neg_max", [P, B])
        hT_all = sb("hT_all", [P, B * D])
        ctx_in = [sb(f"L1x_ctx{j}", [P, D]) for j in range(2)]
        xn = [sb(f"L1x_xn{j}", [P, D]) for j in range(2)]
        xcT = [sb(f"L1x_xcT{j}", [P, 2 * KT, P]) for j in range(2)]
        xw = [sb(f"xw{j}", [P, KT, P]) for j in range(2)]
        raw = [sb(f"raw{j}", [P, P]) for j in range(2)]
        row_sum = [sb(f"row_sum{j}", [P, 1]) for j in range(2)]
        inv_row = [sb(f"inv_row{j}", [P, 1]) for j in range(2)]
        attn = [sb(f"attn{j}", [P, P]) for j in range(2)]
        attnT = [sb(f"attnT{j}", [P, P]) for j in range(2)]
        maxT = sb("maxT", [B, 4, P])
        row = sb("row", [B, 4])
        batt = sb("batt", [P, B])
        hT = [sb(f"hT{j}", [P, D]) for j in range(2)]
        xT = [sb(f"xT{j}", [P, D]) for j in range(2)]
        xh = [sb(f"xh{j}", [P, D]) for j in range(2)]
        c_col = [sb(f"c_col{j}", [P, KT]) for j in range(2)]
        w_xc = [sb(f"w_xc{j}", [P, KT, D]) for j in range(2)]
        bank = core.banks_in(ctx, tag)
        s = core.sems_in(tag, NORM_SEMS + [
            "weights", "ctx_in0", "ctx_in1", "passed", "xn", "T", "T_out", "xw", "sim", "neg_max", "exped", "inv",
            "attn", "attnT", "attnT_out", "h", "h_out"])

        phases = Phases(nc)
        block = phases.open()

        @block.sync
        def _(sp):
            sp.dma_start(w_sim[:, :, :], ins["L1_xattn_w_sim"].rearrange("(w k p) -> p w k", w=3, p=P),
                         allow_slow_non_contiguous=True).then_inc(s["weights"], 16)
            sp.dma_start(b_sim[:, :], ins["L1_xattn_b_sim"].rearrange("(a n) -> a n", a=1).to_broadcast([P, 1])
                         ).then_inc(s["weights"], 16)
            sp.dma_start(w_qv[:, :, :], ins["L1_xattn_W_qv"].rearrange("(t p) n -> p t n", p=P)
                         ).then_inc(s["weights"], 16)
            sp.dma_start(b_qv[:, :], ins["L1_xattn_b_qv"].rearrange("(a n) -> a n", a=1)).then_inc(s["weights"], 16)

            def body(j, b, first, last):
                if not isinstance(b, int):
                    sp.wait_ge(s["h"], b - 1)
                    settle(sp, s["passed"])
                sp.dma_start(ctx_in[j][:, :], one(ins["ctx_1024"], b)).then_inc(s[f"ctx_in{j}"], 16)

            load_batches(sp, body)

        @block.tensor
        def _(pe):
            def transposed(j, b):
                pe.wait_ge(s["xn"], b + 1)
                pe.wait_ge(s[f"ctx_in{j}"], loads(b, j))
                after(pe, s["T_out"], b - 1)
                for k in range(KT):
                    nc.tensor.transpose(bank[j][:, k * P:(k + 1) * P], xn[j][:, k * P:(k + 1) * P], core.ident[:, :])
                for k in range(KT):
                    t = nc.tensor.transpose(bank[j][:, (KT + k) * P:(KT + k + 1) * P],
                                            ctx_in[j][:, k * P:(k + 1) * P], core.ident[:, :])
                t.then_inc(s["T"], 1)

            def similarity(j, b):
                pe.wait_ge(s["T_out"], b + 1)
                pe.wait_ge(s["xw"], b + 1)
                after(pe, s["exped"], b - 1)
                for k in range(KT):
                    nc.tensor.matmul(bank[2 + j][:, 0:P], xw[j][:, k, :], xcT[j][:, KT + k, :],
                                     start=(k == 0), stop=False)
                for k in range(KT):
                    t = nc.tensor.matmul(bank[2 + j][:, 0:P], xcT[j][:, k, :],
                                         w_sim[:, 0, k:k + 1].to_broadcast([P, P]), start=False, stop=(k == KT - 1))
                t.then_inc(s["sim"], 1)

            def attn_transposed(j, b):
                pe.wait_ge(s["attn"], b + 1)
                after(pe, s["attnT_out"], b - 1)
                nc.tensor.transpose(bank[4 + j][:, 0:P], attn[j][:, :], core.ident[:, :]).then_inc(s["attnT"], 1)

            def weighted(j, b):
                pe.wait_ge(s["attnT_out"], b + 1)
                after(pe, s["h_out"], b - 1)
                for k in range(KT):
                    t = nc.tensor.matmul(bank[6 + j][:, k * P:(k + 1) * P], ctx_in[j][:, k * P:(k + 1) * P],
                                         attnT[j][:, :], start=True, stop=True)
                t.then_inc(s["h"], 1)

            def body(j, b, first, last):
                if not last:
                    transposed(1 - j, b + 1)
                attn_transposed(j, b)
                if not last:
                    similarity(1 - j, b + 1)
                weighted(j, b)

            pe.wait_ge(s["weights"], 64)
            transposed(0, 0)
            similarity(0, 0)
            over_batches(pe, body)

        @block.scalar
        def _(act):
            def take_T(j, b):
                act.wait_ge(s["T"], b + 1)
                after(act, s["sim"], b - 1)
                nc.scalar.copy(xcT[j][:, :, :].rearrange("p t c -> p (t c)"), bank[j][:, :]).then_inc(s["T_out"], 1)

            def exp(j, b):
                act.wait_ge(s["neg_max"], b + 1)
                after(act, s["attn"], b - 1)
                nc.scalar.activation(raw[j][:, :], bank[2 + j][:, 0:P], ACT.Exp, bias=cols(neg_max, b, 1),
                                     accum_out=row_sum[j][:, :]).then_inc(s["exped"], 1)

            def take_attnT(j, b):
                act.wait_ge(s["attnT"], b + 1)
                after(act, s["h"], b - 1)
                nc.scalar.copy(attnT[j][:, :], bank[4 + j][:, 0:P]).then_inc(s["attnT_out"], 1)

            def take_h(j, b):
                act.wait_ge(s["h"], b + 1)
                nc.scalar.copy(cols(hT_all, b * D, D), bank[6 + j][:, 0:D]).then_inc(s["h_out"], 1)

            def body(j, b, first, last):
                if not last:
                    take_T(1 - j, b + 1)
                take_attnT(j, b)
                if not last:
                    exp(1 - j, b + 1)
                take_h(j, b)

            finish_norm_scalar(core, act, s, temps)
            take_T(0, 0)
            exp(0, 0)
            over_batches(act, body)

        @block.vector
        def _(dve):
            def prepare(j, b):
                after(dve, s["T"], b - 1)
                normalise(core, xn[j][:, :], b).then_inc(s["xn"], 1)
                dve.wait_ge(s["T_out"], b + 1)
                after(dve, s["sim"], b - 1)
                for k in range(KT):
                    t = nc.vector.tensor_scalar(xw[j][:, k, :], xcT[j][:, k, :], w_sim[:, 2, k:k + 1],
                                                w_sim[:, 1, k:k + 1], ALU.mult, ALU.add)
                t.then_inc(s["xw"], 1)

            def row_max(j, b):
                dve.wait_ge(s["sim"], b + 1)
                nc.vector.tensor_reduce(cols(neg_max, b, 1), bank[2 + j][:, 0:P], AX.X, ALU.max, negate=True
                                        ).then_inc(s["neg_max"], 1)

            def normalise_rows(j, b):
                dve.wait_ge(s["exped"], b + 1)
                nc.vector.reciprocal(inv_row[j][:, :], row_sum[j][:, :]).then_inc(s["inv"], 1)
                dve.wait_ge(s["inv"], b + 1)
                after(dve, s["attnT"], b - 1)
                nc.vector.tensor_scalar(attn[j][:, :], raw[j][:, :], inv_row[j][:, :], None, ALU.mult
                                        ).then_inc(s["attn"], 1)

            def body(j, b, first, last):
                if not last:
                    prepare(1 - j, b + 1)
                    row_max(1 - j, b + 1)
                    normalise_rows(1 - j, b + 1)

            finish_norm_vector(core, dve, s, temps)
            dve.wait_ge(s["weights"], 64)
            prepare(0, 0)
            row_max(0, 0)
            normalise_rows(0, 0)
            over_batches(dve, body)

        phases.close()
        context_weights(core, s_weights=s, neg_max=neg_max, b_sim=b_sim, maxT=maxT, row=row, batt=batt, bank=bank)
        q = core.sems_in("L1o", ["xn", "T", "T_out", "hT", "c", "w_xc", "xh", "out", "updated"])

        block2 = phases.open()

        @block2.tensor
        def _(pe):
            def front(j, b):
                pe.wait_ge(q["xn"], b + 1)
                after(pe, q["T_out"], b - 1)
                after(pe, q["c"], b - 1)
                for k in range(KT):
                    nc.tensor.transpose(bank[j][:, k * P:(k + 1) * P], xn[j][:, k * P:(k + 1) * P], core.ident[:, :])
                for k in range(KT):
                    t = nc.tensor.matmul(bank[2 + j][:, k:k + 1], xn[j][:, k * P:(k + 1) * P], cols(batt, b, 1),
                                         start=True, stop=True)
                t.then_inc(q["T"], 1)

            def project(j, b):
                pe.wait_ge(q["T_out"], b + 1)
                pe.wait_ge(q["hT"], b + 1)
                pe.wait_ge(q["w_xc"], b + 1)
                pe.wait_ge(q["xh"], b + 1)
                after(pe, q["updated"], b - 1)
                dst = bank[4 + j][:, 0:D]
                for k in range(KT):
                    cs = slice(k * P, (k + 1) * P)
                    nc.tensor.matmul(dst, xT[j][:, cs], w_xc[j][:, k, :], start=(k == 0), stop=False)
                    nc.tensor.matmul(dst, hT[j][:, cs], w_qv[:, KT + k, :], start=False, stop=False)
                    nc.tensor.matmul(dst, xh[j][:, cs], w_qv[:, 2 * KT + k, :], start=False, stop=False)
                nc.tensor.matmul(dst, core.ones[0:1, :], b_qv[0:1, :], start=False, stop=True).then_inc(q["out"], 1)

            def body(j, b, first, last):
                if not last:
                    front(1 - j, b + 1)
                project(j, b)

            front(0, 0)
            over_batches(pe, body)

        @block2.scalar
        def _(act):
            def body(j, b, first, last):
                after(act, q["out"], b - 1)
                after(act, q["xh"], b - 1)
                nc.scalar.copy(hT[j][:, :], cols(hT_all, b * D, D)).then_inc(q["hT"], 1)
                act.wait_ge(q["T"], b + 1)
                nc.scalar.copy(xT[j][:, :], bank[j][:, 0:D]).then_inc(q["T_out"], 1)

            over_batches(act, body)

        @block2.vector
        def _(dve):
            def norm(j, b):
                after(dve, q["T"], b - 1)
                normalise(core, xn[j][:, :], b).then_inc(q["xn"], 1)

            def operands(j, b):
                dve.wait_ge(q["T"], b + 1)
                after(dve, q["out"], b - 1)
                nc.vector.tensor_copy(c_col[j][:, :], bank[2 + j][:, 0:KT]).then_inc(q["c"], 1)
                dve.wait_ge(q["T_out"], b + 1)
                dve.wait_ge(q["hT"], b + 1)
                nc.vector.tensor_tensor(xh[j][:, :], xT[j][:, :], hT[j][:, :], ALU.mult).then_inc(q["xh"], 1)
                dve.wait_ge(q["c"], b + 1)
                for k in range(KT):
                    t = nc.vector.scalar_tensor_tensor(w_xc[j][:, k, :], w_qv[:, 3 * KT + k, :], c_col[j][:, k:k + 1],
                                                       w_qv[:, k, :], ALU.mult, ALU.add)
                t.then_inc(q["w_xc"], 1)

            def update(j, b):
                dve.wait_ge(q["out"], b + 1)
                nc.vector.scalar_tensor_tensor(cols(core.x, b * D, D), bank[4 + j][:, 0:D], core.gate(1, 0),
                                               cols(core.x, b * D, D), ALU.mult, ALU.add).then_inc(q["updated"], 1)
                dve.wait_ge(q["updated"], b + 1)
                take_stats(core, b)

            def body(j, b, first, last):
                if not last:
                    norm(1 - j, b + 1)
                    operands(1 - j, b + 1)
                update(j, b)

            norm(0, 0)
            operands(0, 0)
            over_batches(dve, body)

        phases.close()


def context_weights(core, s_weights, neg_max, b_sim, maxT, row, batt, bank):
    nc = core.nc
    s = core.sems_in("L1b", ["step", "T", "max_row", "shifted", "exped", "batt", "back"])
    with nc.Block() as block:
        @block.tensor
        def _(pe):
            pe.wait_ge(s["max_row"], 1)
            nc.tensor.transpose(bank[0][0:B, 0:P], batt[:, :], core.ident[:, :]).then_inc(s["T"], 1)
            pe.wait_ge(s["batt"], 1)
            nc.tensor.transpose(bank[1][:, 0:B], maxT[:, 2, :], core.ident[0:B, 0:B]).then_inc(s["back"], 1)

        @block.scalar
        def _(act):
            act.wait_ge(s["shifted"], 1)
            nc.scalar.activation(maxT[:, 1, :], maxT[:, 0, :], ACT.Exp, accum_out=row[:, 1:2]).then_inc(s["exped"], 1)

        @block.vector
        def _(dve):
            link = chain(dve, s["step"], 0)
            nc.vector.tensor_scalar(batt[:, :], neg_max[:, :], -1.0, b_sim[:, :], ALU.mult, ALU.add
                                    ).then_inc(s["max_row"], 1)
            dve.wait_ge(s["T"], 1)
            link(nc.vector.tensor_reduce(row[:, 0:1], bank[0][0:B, 0:P], AX.X, ALU.max))
            nc.vector.tensor_scalar(maxT[:, 0, :], bank[0][0:B, 0:P], row[:, 0:1], None, ALU.subtract
                                    ).then_inc(s["shifted"], 1)
            dve.wait_ge(s["exped"], 1)
            link(nc.vector.reciprocal(row[:, 2:3], row[:, 1:2]))
            nc.vector.tensor_scalar(maxT[:, 2, :], maxT[:, 1, :], row[:, 2:3], None, ALU.mult).then_inc(s["batt"], 1)
            dve.wait_ge(s["back"], 1)
            nc.vector.tensor_copy(batt[:, :], bank[1][:, 0:B])


def bit_ffn(core):
    nc, ins = core.nc, core.ins
    tag = "L3f"
    F = 1024
    FT = F // P
    MAGIC = 1.5 * 2.0 ** 23
    with ExitStack() as ctx:
        sb = core.sbuf_in(ctx)
        ident_bf = sb("ident_bf", [P, P], BF16)
        w_raw = sb("w_raw", [P, 3, FT * D])
        w_round = sb("w_round", [P, FT * D])
        w_tern = sb("w_tern", [P, 3, FT * D], BF16)
        w_gu = sb("w_gu", [P, KT, 2, F], BF16)
        w_down = sb("w_down", [P, FT, D], BF16)
        w_sum = sb("w_sum", [P, 3])
        w_scale = sb("w_scale", [P, 3])
        w_mean = sb("w_mean", [P, 3])
        temps = sb("L3f_temps", [P, 4, B])
        bank = core.banks_in(ctx, tag)
        p = core.sems_in("L3w", ["ident", "w0", "w1", "w2", "summed", "total", "step", "rounded", "tern", "T", "T_out"])
        names = ("L3_ffn_w_gate", "L3_ffn_w_up", "L3_ffn_w_down")
        phases = Phases(nc)
        block = phases.open()
        tbank = [bank[i][:, :].bitcast(BF16) for i in range(4)]

        @block.sync
        def _(sp):
            for k in range(3):
                sp.dma_start(w_raw[:, k, :].rearrange("p (t n) -> p t n", n=D if k < 2 else F),
                             ins[names[k]].rearrange("(t p) n -> p t n", p=P)).then_inc(p[f"w{k}"], 16)

        @block.vector
        def _(dve):
            for k in range(3):
                dve.wait_ge(p[f"w{k}"], 16)
                nc.vector.tensor_reduce(w_sum[:, k:k + 1], w_raw[:, k, :], AX.X, ALU.add,
                                        apply_absolute_value=True).then_inc(p["summed"], 1)
            dve.wait_ge(p["total"], 1)
            link = chain(dve, p["step"], 0)
            link(nc.vector.tensor_scalar(w_mean[:, :], bank[4][:, 0:3], 1.0 / (F * D), 1e-5, ALU.mult, ALU.max))
            link(nc.vector.reciprocal(w_scale[:, :], w_mean[:, :]))
            for k in range(3):
                link(nc.vector.tensor_scalar(w_round[:, :], w_raw[:, k, :], w_scale[:, k:k + 1], MAGIC,
                                             ALU.mult, ALU.add))
                link(nc.vector.tensor_scalar(w_round[:, :], w_round[:, :], -MAGIC, 1.0, ALU.add, ALU.min))
                link(nc.vector.tensor_scalar(w_tern[:, k, :], w_round[:, :], -1.0, None, ALU.max))
                nc.vector.sem_inc(p["tern"], 1)

        @block.tensor
        def _(pe):
            pe.wait_ge(p["summed"], 3)
            nc.tensor.matmul(bank[4][:, 0:3], core.ones[:, :], w_sum[:, :], start=True, stop=True
                             ).then_inc(p["total"], 1)
            pe.wait_ge(p["ident"], 1)
            for n in range(12):
                k = n // 4
                pe.wait_ge(p["tern"], k + 1)
                after(pe, p["T_out"], n - 3)
                for i in range(4):
                    m = 4 * (n % 4) + i
                    t = nc.tensor.transpose(tbank[n % 4][:, i * P:(i + 1) * P], w_tern[:, k, m * P:(m + 1) * P],
                                            ident_bf[:, :])
                t.then_inc(p["T"], 1)

        @block.scalar
        def _(act):
            nc.scalar.copy(ident_bf[:, :], core.ident[:, :]).then_inc(p["ident"], 1)
            for n in range(12):
                k = n // 4
                act.wait_ge(p["T"], n + 1)
                src = tbank[n % 4][:, 0:4 * P]
                if k < 2:
                    t0 = 2 * (n % 4)
                    dst = w_gu[:, :, k, t0 * P:(t0 + 2) * P].rearrange("p k (t c) -> p t k c", t=2)
                    nc.scalar.copy(dst, src.rearrange("p (t k c) -> p t k c", t=2, k=KT)).then_inc(p["T_out"], 1)
                else:
                    o, i0 = (n % 4) // 2, 4 * (n % 2)
                    nc.scalar.copy(w_down[:, i0:i0 + 4, o * P:(o + 1) * P],
                                   src.rearrange("p (i c) -> p i c", i=4)).then_inc(p["T_out"], 1)

        block_b = phases.open()
        xn = [sb(f"L3f_xn{j}", [P, D]) for j in range(2)]
        amax = [sb(f"amax{j}", [P, 8]) for j in range(2)]
        x_round = sb("x_round", [P, D])
        xq = [sb(f"xq{j}", [P, D], BF16) for j in range(2)]
        xqT = [sb(f"xqT{j}", [P, D], BF16) for j in range(2)]
        silu = [sb(f"silu{j}", [P, F]) for j in range(2)]
        h = [sb(f"h{j}", [P, F]) for j in range(2)]
        hq = [sb(f"hq{j}", [P, F], BF16) for j in range(2)]
        hqT = [sb(f"hqT{j}", [P, F], BF16) for j in range(2)]
        s = core.sems_in(tag, NORM_SEMS + [
            "dve", "xq", "scale_x", "xqT", "xqT_out", "gate", "up", "silu", "gated", "hq", "hqT", "hqT_out", "down",
            "updated"])
        T_bank = bank[0][:, :].bitcast(BF16)
        H_bank = bank[1][:, :].bitcast(BF16)
        G, U, O = bank[2:4], bank[4:6], bank[6:8]

        @block_b.tensor
        def _(pe):
            def front(j, b):
                pe.wait_ge(s["xq"], b + 1)
                after(pe, s["xqT_out"], b)
                for k in range(KT):
                    t = nc.tensor.transpose(T_bank[:, k * P:(k + 1) * P], xq[j][:, k * P:(k + 1) * P],
                                            ident_bf[:, :])
                t.then_inc(s["xqT"], 1)

            def expand(j, b):
                pe.wait_ge(s["xqT_out"], b + 1)
                after(pe, s["silu"], b)
                for half in range(2):
                    for k in range(KT):
                        t = nc.tensor.matmul(G[half][:, :], xqT[j][:, k * P:(k + 1) * P],
                                             w_gu[:, k, 0, half * 512:(half + 1) * 512],
                                             start=(k == 0), stop=(k == KT - 1))
                t.then_inc(s["gate"], 1)
                after(pe, s["gated"], b)
                for half in range(2):
                    for k in range(KT):
                        t = nc.tensor.matmul(U[half][:, :], xqT[j][:, k * P:(k + 1) * P],
                                             w_gu[:, k, 1, half * 512:(half + 1) * 512],
                                             start=(k == 0), stop=(k == KT - 1))
                t.then_inc(s["up"], 1)

            def h_transposed(j, b):
                pe.wait_ge(s["hq"], b + 1)
                after(pe, s["hqT_out"], b)
                for k in range(FT):
                    t = nc.tensor.transpose(H_bank[:, k * P:(k + 1) * P], hq[j][:, k * P:(k + 1) * P],
                                            ident_bf[:, :])
                t.then_inc(s["hqT"], 1)

            def contract(j, b):
                pe.wait_ge(s["hqT_out"], b + 1)
                after(pe, s["updated"], b - 1)
                for k in range(FT):
                    t = nc.tensor.matmul(O[j][:, 0:D], hqT[j][:, k * P:(k + 1) * P], w_down[:, k, :],
                                         start=(k == 0), stop=(k == FT - 1))
                t.then_inc(s["down"], 1)

            def body(j, b, first, last):
                if not last:
                    front(1 - j, b + 1)
                    expand(1 - j, b + 1)
                h_transposed(j, b)
                contract(j, b)

            front(0, 0)
            expand(0, 0)
            over_batches(pe, body)

        @block_b.scalar
        def _(act):
            def front(j, b):
                act.wait_ge(s["xqT"], b + 1)
                after(act, s["up"], b - 1)
                nc.scalar.copy(xqT[j][:, :], T_bank[:, 0:D]).then_inc(s["xqT_out"], 1)
                act.wait_ge(s["gate"], b + 1)
                act.wait_ge(s["scale_x"], b + 1)
                after(act, s["gated"], b - 1)
                for half in range(2):
                    t = nc.scalar.activation(silu[j][:, half * 512:(half + 1) * 512], G[half][:, :], ACT.Silu,
                                             scale=amax[j][:, 2:3])
                t.then_inc(s["silu"], 1)

            def back(j, b):
                act.wait_ge(s["hqT"], b + 1)
                after(act, s["down"], b - 1)
                nc.scalar.copy(hqT[j][:, :], H_bank[:, :]).then_inc(s["hqT_out"], 1)

            def body(j, b, first, last):
                if not last:
                    front(1 - j, b + 1)
                back(j, b)

            finish_norm_scalar(core, act, s, temps)
            front(0, 0)
            over_batches(act, body)

        @block_b.vector
        def _(dve):
            def front(j, b, link):
                a = amax[j]
                after(dve, s["down"], b - 1)
                link(normalise(core, xn[j][:, :], b))
                link(nc.vector.tensor_reduce(a[:, 0:1], xn[j][:, :], AX.X, ALU.max, apply_absolute_value=True))
                link(nc.vector.tensor_scalar(a[:, 0:1], a[:, 0:1], 1e-5, 1.0 / 127.0, ALU.max, ALU.mult))
                link(nc.vector.reciprocal(a[:, 1:2], a[:, 0:1]))
                link(nc.vector.tensor_scalar(x_round[:, :], xn[j][:, :], a[:, 1:2], MAGIC, ALU.mult, ALU.add))
                link(nc.vector.tensor_scalar(x_round[:, :], x_round[:, :], -MAGIC, 127.0, ALU.add, ALU.min))
                nc.vector.tensor_scalar(xq[j][:, :], x_round[:, :], -128.0, None, ALU.max).then_inc(s["xq"], 1)
                nc.vector.tensor_scalar(a[:, 2:4], w_mean[:, 0:2], a[:, 0:1], None, ALU.mult
                                        ).then_inc(s["scale_x"], 1)

            def middle(j, b, link):
                a = amax[j]
                dve.wait_ge(s["up"], b + 1)
                dve.wait_ge(s["silu"], b + 1)
                dve.wait_ge(s["scale_x"], b + 1)
                for half in range(2):
                    t = nc.vector.scalar_tensor_tensor(h[j][:, half * 512:(half + 1) * 512], U[half][:, :],
                                                       a[:, 3:4], silu[j][:, half * 512:(half + 1) * 512],
                                                       ALU.mult, ALU.mult)
                t.then_inc(s["gated"], 1)
                dve.wait_ge(s["gated"], b + 1)
                link(nc.vector.tensor_reduce(a[:, 4:5], h[j][:, :], AX.X, ALU.max, apply_absolute_value=True))
                link(nc.vector.tensor_scalar(a[:, 4:5], a[:, 4:5], 1e-5, 1.0 / 127.0, ALU.max, ALU.mult))
                link(nc.vector.reciprocal(a[:, 5:6], a[:, 4:5]))
                link(nc.vector.tensor_scalar(h[j][:, :], h[j][:, :], a[:, 5:6], MAGIC, ALU.mult, ALU.add))
                link(nc.vector.tensor_scalar(h[j][:, :], h[j][:, :], -MAGIC, 127.0, ALU.add, ALU.min))
                after(dve, s["hqT"], b - 1)
                nc.vector.tensor_scalar(hq[j][:, :], h[j][:, :], -128.0, None, ALU.max).then_inc(s["hq"], 1)
                link(nc.vector.tensor_scalar(a[:, 6:7], a[:, 4:5], w_mean[:, 2:3], None, ALU.mult))
                link(nc.vector.tensor_scalar(a[:, 7:8], a[:, 6:7], core.gate(3, 1), None, ALU.mult))

            def back(j, b, link):
                dve.wait_ge(s["down"], b + 1)
                nc.vector.scalar_tensor_tensor(cols(core.x, b * D, D), O[j][:, 0:D], amax[j][:, 7:8],
                                               cols(core.x, b * D, D), ALU.mult, ALU.add).then_inc(s["updated"], 1)

            def body(j, b, first, last):
                link = chain(dve, s["dve"], b * 13 + 6)
                if not last:
                    front(1 - j, b + 1, link)
                middle(j, b, link)
                back(j, b, link)

            finish_norm_vector(core, dve, s, temps)
            front(0, 0, chain(dve, s["dve"], 0))
            over_batches(dve, body)

        phases.close()


def warped_alignment(core):
    nc, ins = core.nc, core.ins
    tag = "L3x"
    W = P + 1
    NB = 8
    R = P // NB
    UNROLL = 8
    with ExitStack() as ctx:
        sb = core.sbuf_in(ctx)
        temps = sb("L3x_temps", [P, 4, B])
        dist_buf = sb("dist_buf", [P, P * P])
        dist16 = dist_buf[0:B, :]
        cost = sb("cost", [B, W * W])
        low = sb("low", [B, P])
        ctx_in = [sb(f"L3x_ctx{j}", [P, D]) for j in range(2)]
        xn = [sb(f"L3x_xn{j}", [P, D]) for j in range(2)]
        xcT = [sb(f"L3x_xcT{j}", [P, 2 * KT, P]) for j in range(2)]
        x_neg2 = [sb(f"x_neg2{j}", [P, D]) for j in range(2)]
        x_sq = [sb(f"x_sq{j}", [P, D]) for j in range(2)]
        ctx_sq = sb("ctx_sq", [P, D])
        ctx_norm = [sb(f"ctx_norm{j}", [P, 1]) for j in range(2)]
        sq_dist = [sb(f"sq_dist{j}", [P, P]) for j in range(2)]
        dist = [sb(f"dist{j}", [P, P]) for j in range(2)]
        bank = core.banks_in(ctx, tag)
        dist_dram = nc.dram_tensor("dist_dram", (B, P, P), F32, kind="Internal").ap()
        path_dram = nc.dram_tensor("path_dram", (B, P, P), F32, kind="Internal").ap()
        s = core.sems_in(tag, NORM_SEMS + [
            "ctx_in0", "ctx_in1", "passed", "xn", "T", "T_out", "x_neg2", "x_sq", "ctx_norm", "dots", "sq_dist",
            "dist", "stored0", "stored1"])
        phases = Phases(nc)

        block = phases.open()

        @block.sync
        def _(sp):
            def body(j, b, first, last):
                if not isinstance(b, int):
                    sp.wait_ge(s["T"], b - 1)
                    settle(sp, s["passed"])
                    sp.wait_ge(s["ctx_norm"], b - 1)
                    settle(sp, s["passed"])
                sp.dma_start(ctx_in[j][:, :], one(ins["ctx_1024"], b)).then_inc(s[f"ctx_in{j}"], 16)

            load_batches(sp, body)

        @block.tensor
        def _(pe):
            def transposed(j, b):
                pe.wait_ge(s["xn"], b + 1)
                pe.wait_ge(s[f"ctx_in{j}"], loads(b, j))
                after(pe, s["T_out"], b - 1)
                for k in range(KT):
                    nc.tensor.transpose(bank[j][:, k * P:(k + 1) * P], xn[j][:, k * P:(k + 1) * P], core.ident[:, :])
                for k in range(KT):
                    t = nc.tensor.transpose(bank[j][:, (KT + k) * P:(KT + k + 1) * P],
                                            ctx_in[j][:, k * P:(k + 1) * P], core.ident[:, :])
                t.then_inc(s["T"], 1)

            def dots(j, b):
                pe.wait_ge(s["x_neg2"], b + 1)
                pe.wait_ge(s["x_sq"], b + 1)
                after(pe, s["sq_dist"], b - 1)
                for k in range(KT):
                    cs = slice(k * P, (k + 1) * P)
                    nc.tensor.matmul(bank[2 + j][:, 0:P], xcT[j][:, KT + k, :], x_neg2[j][:, cs],
                                     start=(k == 0), stop=False)
                for k in range(KT):
                    cs = slice(k * P, (k + 1) * P)
                    t = nc.tensor.matmul(bank[2 + j][:, 0:P], core.ones[:, :], x_sq[j][:, cs],
                                         start=False, stop=(k == KT - 1))
                t.then_inc(s["dots"], 1)

            def body(j, b, first, last):
                if not last:
                    transposed(1 - j, b + 1)
                dots(j, b)

            transposed(0, 0)
            over_batches(pe, body)

        @block.scalar
        def _(act):
            def front(j, b):
                act.wait_ge(s[f"ctx_in{j}"], loads(b, j))
                after(act, s["sq_dist"], b - 1)
                after(act, s["ctx_norm"], b)
                nc.scalar.activation(ctx_sq[:, :], ctx_in[j][:, :], ACT.Square, accum_out=ctx_norm[j][:, :]
                                     ).then_inc(s["ctx_norm"], 1)
                act.wait_ge(s["T"], b + 1)
                after(act, s["dots"], b - 1)
                nc.scalar.copy(xcT[j][:, :, :].rearrange("p t c -> p (t c)"), bank[j][:, :]).then_inc(s["T_out"], 1)
                act.wait_ge(s["T_out"], b + 1)
                nc.scalar.activation(x_sq[j][:, :], xcT[j][:, 0:KT, :].rearrange("p t c -> p (t c)"), ACT.Square
                                     ).then_inc(s["x_sq"], 1)

            def root(j, b):
                act.wait_ge(s["sq_dist"], b + 1)
                if not (isinstance(b, int) and b < 2):
                    act.wait_ge(s[f"stored{j}"], loads(b, j) - 16)
                nc.scalar.activation(dist[j][:, :], sq_dist[j][:, :], ACT.Sqrt).then_inc(s["dist"], 1)
                act.wait_ge(s["dist"], b + 1)
                act.dma_start(one(dist_dram, b), dist[j][:, :]).then_inc(s[f"stored{j}"], 16)

            def body(j, b, first, last):
                if not last:
                    front(1 - j, b + 1)
                root(j, b)

            finish_norm_scalar(core, act, s, temps)
            front(0, 0)
            over_batches(act, body)

        @block.vector
        def _(dve):
            def front(j, b):
                after(dve, s["T"], b - 1)
                normalise(core, xn[j][:, :], b).then_inc(s["xn"], 1)
                dve.wait_ge(s["T_out"], b + 1)
                after(dve, s["dots"], b - 1)
                nc.vector.tensor_scalar(x_neg2[j][:, :], xcT[j][:, 0:KT, :].rearrange("p t c -> p (t c)"), -2.0, None,
                                        ALU.mult).then_inc(s["x_neg2"], 1)

            def body(j, b, first, last):
                if not last:
                    front(1 - j, b + 1)
                dve.wait_ge(s["dots"], b + 1)
                dve.wait_ge(s["ctx_norm"], b + 1)
                after(dve, s["dist"], b - 1)
                nc.vector.tensor_scalar(sq_dist[j][:, :], bank[2 + j][:, 0:P], ctx_norm[j][:, :], 0.0,
                                        ALU.add, ALU.max).then_inc(s["sq_dist"], 1)

            finish_norm_vector(core, dve, s, temps)
            front(0, 0)
            over_batches(dve, body)

        @block.gpsimd
        def _(pool):
            pool.wait_ge(s["stored0"], 16 * B // 2)
            pool.wait_ge(s["stored1"], 16 * B // 2)

        NQ = 4
        c = core.sems_in("L3c", [f"dist{q}" for q in range(NQ)] + [f"block{k}" for k in range(NB)] +
                         ["border", "rows", "corner", "block_done", "step", "iota", "leave", "leave_in", "enter",
                          "entry", "pathed", "path_out"])
        costs = sb("costs", [P, (R + 1) * W])
        low_b, up, not_left = (dist_buf[:, i * R * P:(i + 1) * R * P].rearrange("p (r j) -> p r j", r=R)
                               for i in range(3))
        left = sb("left", [P, R, W])
        diag = sb("diag", [P, R, W])
        column = sb("column", [P, P])
        leave = [sb(f"leave{i}", [P, W]) for i in range(2)]
        part = [sb(f"part{i}", [P, P]) for i in range(3)]
        leave16 = sb("leave16", [B, NB, P])
        entry16 = sb("entry16", [B, NB])
        entry = sb("entry", [P, 1])
        enters = sb("enters", [P, P])
        path = sb("path", [P, R, W])
        cost3 = cost[:, :].rearrange("b (i j) -> b i j", j=W)
        costs3 = costs[:, :].rearrange("p (i j) -> p i j", j=W)

        block = phases.open()

        @block.sync
        def _(sp):
            rows = P // NQ
            for q in range(NQ):
                sp.dma_start(dist16[:, q * rows * P:(q + 1) * rows * P],
                             dist_dram[:, q * rows:(q + 1) * rows, :].rearrange("b i j -> b (i j)")
                             ).then_inc(c[f"dist{q}"], 16)
            for k in range(NB):
                sp.wait_ge(c["block_done"], k + 1)
                sp.dma_start(costs[k * B:(k + 1) * B, :], cost[:, k * R * W:(k * R + R + 1) * W]
                             ).then_inc(c[f"block{k}"], 16)
            sp.wait_ge(c["leave"], 1)
            for k in range(NB):
                sp.dma_start(leave16[:, k, :], leave[(R - 1) % 2][k * B:(k + 1) * B, 1:W]).then_inc(c["leave_in"], 16)
            sp.wait_ge(c["enter"], 1)
            for k in range(NB):
                sp.dma_start(entry[k * B:(k + 1) * B, :], entry16[:, k:k + 1]).then_inc(c["entry"], 16)
            sp.wait_ge(c["pathed"], 1)
            for k in range(NB):
                sp.dma_start(path_dram[:, k * R:(k + 1) * R, :], path[k * B:(k + 1) * B, :, 0:P]
                             ).then_inc(c["path_out"], 16)
            sp.wait_ge(c["path_out"], 16 * NB)

        @block.gpsimd
        def _(pool):
            nc.gpsimd.iota(column[:, :], [[1, P]], 0, 0, allow_small_or_imprecise_dtypes=True).then_inc(c["iota"], 1)
            nc.gpsimd.memset(cost[:, 0:W], BIG).then_inc(c["border"], 1)
            nc.gpsimd.memset(cost3[:, 1:W, 0], BIG).then_inc(c["border"], 1)
            for t in (left, diag):
                nc.gpsimd.memset(t[:, :, P], 0.0).then_inc(c["iota"], 1)
            nc.gpsimd.memset(path[:, :, P], 0.0).then_inc(c["iota"], 1)
            for t in leave:
                nc.gpsimd.memset(t[:, 0:1], 0.0).then_inc(c["iota"], 1)
            pool.wait_ge(c["border"], 2)
            nc.gpsimd.memset(cost[:, 0:1], 0.0).then_inc(c["border"], 1)
            pool.wait_ge(c["rows"], 3)
            nc.gpsimd.memset(cost[:, 0:1], BIG).then_inc(c["corner"], 1)

        @block.vector
        def _(dve):
            def cost_row(r, done):
                above = bass.ds((r - 1) * W + 1, P)
                above_left = bass.ds((r - 1) * W, P)
                dve.wait_ge(c["rows"], done)
                nc.vector.tensor_tensor(low[:, :], cost[:, above], cost[:, above_left], ALU.min
                                        ).then_inc(c["rows"], 1)
                dve.wait_ge(c["rows"], done + 1)
                nc.vector.tensor_tensor_scan(cost[:, bass.ds(r * W + 1, P)], low[:, :],
                                             dist16[:, bass.ds((r - 1) * P, P)], BIG, ALU.min, ALU.add
                                             ).then_inc(c["rows"], 1)

            dve.wait_ge(c["border"], 3)
            dve.sem_inc(c["rows"], 1)
            for q in range(NQ):
                dve.wait_ge(c[f"dist{q}"], 16)
                for k in range(2 * q, 2 * q + 2):
                    with dve.Fori(0, R // UNROLL) as i:
                        for u in range(UNROLL):
                            r = i * UNROLL + (k * R + u + 1)
                            cost_row(r, i * (2 * UNROLL) + 2 * (k * R + u) + 1)
                    dve.wait_ge(c["rows"], 2 * R * (k + 1) + 1)
                    if k == 0:
                        dve.wait_ge(c["corner"], 1)
                    dve.sem_inc(c["block_done"], 1)

            link = chain(dve, c["step"], 0)
            for k in range(NB):
                dve.wait_ge(c[f"block{k}"], 16)
            dve.wait_ge(c["iota"], 6)
            c_left = costs3[:, 1:R + 1, 0:P]
            c_up = costs3[:, 0:R, 1:W]
            c_diag = costs3[:, 0:R, 0:P]
            nc.vector.tensor_tensor(diag[:, :, 0:P], c_diag, c_up, ALU.is_le)
            link(nc.vector.tensor_tensor(low_b[:, :, :], c_diag, c_up, ALU.min))
            nc.vector.tensor_tensor(left[:, :, 0:P], c_left, low_b[:, :, :], ALU.is_lt)
            link(nc.vector.tensor_tensor(not_left[:, :, :], c_left, low_b[:, :, :], ALU.is_ge))
            link(nc.vector.tensor_tensor(diag[:, :, 0:P], diag[:, :, 0:P], not_left[:, :, :], ALU.mult))
            link(nc.vector.tensor_tensor(up[:, :, :], not_left[:, :, :], diag[:, :, 0:P], ALU.subtract))

            link(nc.vector.tensor_tensor(part[0][:, :], column[:, :], not_left[:, 0, :], ALU.mult))
            link(nc.vector.tensor_tensor(part[2][:, :], part[0][:, :], diag[:, 0, 0:P], ALU.subtract))
            for r in range(R):
                if r:
                    above = leave[(r - 1) % 2]
                    nc.vector.tensor_tensor(part[0][:, :], diag[:, r, 0:P], above[:, 0:P], ALU.mult)
                    link(nc.vector.tensor_tensor(part[1][:, :], up[:, r, :], above[:, 1:W], ALU.mult))
                    link(nc.vector.tensor_tensor(part[2][:, :], part[0][:, :], part[1][:, :], ALU.add))
                link(nc.vector.tensor_tensor_scan(leave[r % 2][:, 1:W], left[:, r, 0:P], part[2][:, :], 0.0,
                                                  ALU.mult, ALU.add))
            dve.sem_inc(c["leave"], 1)

            link(nc.vector.memset(entry16[:, NB - 1:NB], float(P - 1)))
            dve.wait_ge(c["leave_in"], 16 * NB)
            for k in range(NB - 1, 0, -1):
                link(nc.vector.scalar_tensor_tensor(low[:, :], column[0:B, :], entry16[:, k:k + 1], leave16[:, k, :],
                                                    ALU.is_equal, ALU.mult, accum_out=entry16[:, k - 1:k]))
            dve.sem_inc(c["enter"], 1)

            dve.wait_ge(c["entry"], 16 * NB)
            link(nc.vector.tensor_scalar(enters[:, :], column[:, :], entry[:, :], None, ALU.is_equal))
            for r in range(R - 1, -1, -1):
                link(nc.vector.tensor_tensor_scan(path[:, r, 0:P][:, ::-1], left[:, r, 1:W][:, ::-1],
                                                  enters[:, :][:, ::-1], 0.0, ALU.mult, ALU.add))
                if r:
                    nc.vector.tensor_tensor(part[0][:, :], path[:, r, 1:W], diag[:, r, 1:W], ALU.mult)
                    link(nc.vector.tensor_tensor(part[1][:, :], path[:, r, 0:P], up[:, r, :], ALU.mult))
                    link(nc.vector.tensor_tensor(enters[:, :], part[0][:, :], part[1][:, :], ALU.add))
            dve.sem_inc(c["pathed"], 1)

        q = core.sems_in("L3p", ["ctx_in0", "ctx_in1", "path_in0", "path_in1", "passed", "out", "updated"])
        path_in = [sb(f"path_in{j}", [P, P]) for j in range(2)]
        block = phases.open()

        @block.sync
        def _(sp):
            def body(j, b, first, last):
                if not isinstance(b, int):
                    sp.wait_ge(q["out"], b - 1)
                    settle(sp, q["passed"])
                sp.dma_start(ctx_in[j][:, :], one(ins["ctx_1024"], b)).then_inc(q[f"ctx_in{j}"], 16)
                sp.dma_start(path_in[j][:, :], one(path_dram, b)).then_inc(q[f"path_in{j}"], 16)

            load_batches(sp, body)

        @block.tensor
        def _(pe):
            def body(j, b, first, last):
                pe.wait_ge(q[f"ctx_in{j}"], loads(b, j))
                pe.wait_ge(q[f"path_in{j}"], loads(b, j))
                after(pe, q["updated"], b - 1)
                nc.tensor.matmul(bank[j][:, 0:D], path_in[j][:, :], ctx_in[j][:, :], start=True, stop=True
                                 ).then_inc(q["out"], 1)

            over_batches(pe, body)

        @block.vector
        def _(dve):
            def body(j, b, first, last):
                dve.wait_ge(q["out"], b + 1)
                nc.vector.scalar_tensor_tensor(cols(core.x, b * D, D), bank[j][:, 0:D], core.gate(3, 0),
                                               cols(core.x, b * D, D), ALU.mult, ALU.add).then_inc(q["updated"], 1)
                dve.wait_ge(q["updated"], b + 1)
                take_stats(core, b)

            over_batches(dve, body)

        phases.close()


L1_EXPERTS = dict(tag="L1f", layer=1, experts=8, picks=1, hidden=1024, gated=False, router="L1_ffn_gate_w")
L2_EXPERTS = dict(tag="L2f", layer=2, experts=16, picks=4, hidden=256, gated=True, router="L2_ffn_router_w")
MAGIC = 1.5 * 2.0 ** 23


def choose_best(core, dve, link, s, t, logits):
    nc = core.nc
    E = 8
    wide = [P, B, E]
    a, b, c = t["a"], t["b"], t["c"]
    top, total, best = t["col"][0], t["col"][1], t["col"][2]
    link(nc.vector.tensor_reduce(top, logits, AX.X, ALU.max))
    nc.vector.tensor_tensor(a, logits, top[:, :, None].to_broadcast(wide), ALU.subtract).then_inc(s["for_act"], 1)
    link(nc.vector.tensor_tensor(c, logits, top[:, :, None].to_broadcast(wide), ALU.is_equal))
    link(nc.vector.tensor_tensor(c, c, t["countdown"][:, None, :].to_broadcast(wide), ALU.mult))
    link(nc.vector.tensor_reduce(best, c, AX.X, ALU.max))
    link(nc.vector.tensor_tensor(t["chosen"], c, best[:, :, None].to_broadcast(wide), ALU.is_equal))
    dve.wait_ge(s["from_act"], 1)
    link(nc.vector.tensor_reduce(total, b, AX.X, ALU.add))
    link(nc.vector.reciprocal(total, total))
    link(nc.vector.tensor_scalar(total, total, core.gate(1, 1), None, ALU.mult))
    link(nc.vector.tensor_tensor(t["share"], t["chosen"], total[:, :, None].to_broadcast(wide), ALU.mult))


def choose_in_groups(core, dve, link, s, t, logits):
    nc = core.nc
    E, NG, TOP = 16, 4, 4
    wide = [P, B, E]
    a, scores, c = t["a"], t["b"], t["c"]
    dve.wait_ge(s["from_act"], 1)
    link(nc.vector.tensor_tensor(a, scores, t["bias"][:, None, :].to_broadcast(wide), ALU.add))
    member = t["a2"].rearrange("p (n i) -> p n i", i=4)
    gs, pair = t["group"][0], t["group"][1]
    first = True
    for i in range(4):
        for k in range(i + 1, 4):
            if first:
                link(nc.vector.tensor_tensor(gs, member[:, :, i], member[:, :, k], ALU.add))
            else:
                link(nc.vector.tensor_tensor(pair, member[:, :, i], member[:, :, k], ALU.add))
                link(nc.vector.tensor_tensor(gs, gs, pair, ALU.max))
            first = False
    by_g = gs.rearrange("p (b g) -> p b g", g=NG)
    rank = t["group"][2].rearrange("p (b g) -> p b g", g=NG)
    link(nc.vector.memset(t["group"][2], 0.0))
    for g in range(NG):
        for o in range(NG):
            if o != g:
                link(nc.vector.tensor_tensor(t["col"][0], by_g[:, :, o], by_g[:, :, g],
                                             ALU.is_ge if o < g else ALU.is_gt))
                link(nc.vector.tensor_tensor(rank[:, :, g], rank[:, :, g], t["col"][0], ALU.add))
    link(nc.vector.tensor_scalar(t["group"][2], t["group"][2], 2.0, None, ALU.is_lt))
    link(nc.vector.tensor_scalar(t["group"][1], t["group"][2], 1.0, None, ALU.subtract))
    in_group = t["group"][2][:, :, None].to_broadcast([P, B * NG, 4])
    off_group = t["group"][1][:, :, None].to_broadcast([P, B * NG, 4])
    link(nc.vector.tensor_tensor(member, member, in_group, ALU.mult))
    link(nc.vector.tensor_tensor(member, member, off_group, ALU.add))
    for b in range(B):
        last = nc.vector.max(t["sorted"][:, b * 8:b * 8 + 8], t["a2"][:, b * E:(b + 1) * E])
    link(last)
    fourth = t["sorted"].rearrange("p (b k) -> p b k", k=8)[:, :, TOP - 1:TOP].to_broadcast(wide)
    link(nc.vector.tensor_tensor(c, a, fourth, ALU.is_equal))
    link(nc.vector.tensor_tensor(t["chosen"], a, fourth, ALU.is_gt))
    link(nc.vector.tensor_reduce(t["col"][0], t["chosen"], AX.X, ALU.add))
    link(nc.vector.tensor_tensor_scan(t["a2"], t["restart_e2"], t["c2"], 0.0, ALU.mult, ALU.add))
    link(nc.vector.tensor_tensor(a, a, t["col"][0][:, :, None].to_broadcast(wide), ALU.add))
    link(nc.vector.tensor_scalar(a, a, float(TOP), None, ALU.is_le))
    link(nc.vector.tensor_tensor(c, c, a, ALU.mult))
    link(nc.vector.tensor_tensor(t["chosen"], t["chosen"], c, ALU.add))
    link(nc.vector.tensor_tensor(t["share"], scores, t["chosen"], ALU.mult))
    link(nc.vector.tensor_reduce(t["col"][0], t["share"], AX.X, ALU.add))
    link(nc.vector.tensor_scalar(t["col"][0], t["col"][0], 1e-20, None, ALU.add))
    link(nc.vector.reciprocal(t["col"][0], t["col"][0]))
    link(nc.vector.tensor_scalar(t["col"][0], t["col"][0], 2.5, core.gate(2, 1), ALU.mult, ALU.mult))
    link(nc.vector.tensor_tensor(t["share"], t["share"], t["col"][0][:, :, None].to_broadcast(wide), ALU.mult))


def routed_experts(core, spec):
    nc, ins = core.nc, core.ins
    tag, E, K, F, gated = spec["tag"], spec["experts"], spec["picks"], spec["hidden"], spec["gated"]
    FT = F // P
    UP = 2 * F if gated else F
    NU = UP // 512
    S = (B * P * K + E * (P - 1)) // P
    S += S % 2
    N = B * E
    SH = 512
    with ExitStack() as ctx:
        sb = core.sbuf_in(ctx)
        w_up = sb(f"{tag}_w_up", [P, E * KT * UP])
        w_down = sb(f"{tag}_w_down", [P, E * FT * D])
        if gated:
            sh_gu = sb("sh_gu", [P, 2, KT, SH])
            sh_down = sb("sh_down", [P, SH // P, D])
            bias = sb("router_bias", [P, E])
        else:
            b1 = sb("expert_b1", [P, E * F])
            b2 = sb("expert_b2", [1, E * D])
        row_int = sb(f"{tag}_row_int", [P, K * B], U32)
        pick_share = sb(f"{tag}_pick_share", [P, K * B])
        tile_expert = sb(f"{tag}_tile_expert", [P, S], I32)
        xn = [sb(f"{tag}_xn{j}", [P, D]) for j in range(2)]
        xT = [sb(f"{tag}_xT{j}", [P, D]) for j in range(2)]

        def hidden_buffers():
            width = max(F, SH) if gated else F
            return [[sb(f"{tag}_{name}{j}", [P, width]) for j in range(2)] for name in ("h", "hT")]

        if gated:
            h, hT = hidden_buffers()
            gate_h = [sb(f"{tag}_gate_h{j}", [P, SH]) for j in range(2)]
        routing = ctx.enter_context(ExitStack())
        sr = core.sbuf_in(routing)
        router = sr(f"{tag}_router", [P, KT, E])
        temps = sr(f"{tag}_temps", [P, 4, B])
        logits = sr(f"{tag}_logits", [P, N])
        chosen = sr(f"{tag}_chosen", [P, N])
        share = sr(f"{tag}_share", [P, N])
        abc = [sr(f"{tag}_work{i}", [P, N]) for i in range(3)]
        small = sr(f"{tag}_small", [P, 3, B])
        if gated:
            group = sr(f"{tag}_group", [P, 3, 4 * B])
            best8 = sr(f"{tag}_best8", [P, 8 * B])
        restart_b = sr(f"{tag}_restart_b", [P, N])
        restart_e = sr(f"{tag}_restart_e", [P, N])
        countdown = sr(f"{tag}_countdown", [P, E])
        per_e = sr(f"{tag}_per_e", [P, 4, E])
        tile_no = sr(f"{tag}_tile_no", [P, S])
        tile_e = sr(f"{tag}_tile_e", [P, S])
        tile_cmp = sr(f"{tag}_tile_cmp", [P, S * E])
        before = sr(f"{tag}_before", [P, P])
        row = sr(f"{tag}_row", [P, K, B])
        zeros = sr(f"{tag}_zeros", [P, D])
        bank = core.banks_in(ctx, tag)
        sorted_dram = nc.dram_tensor(f"{tag}_sorted", (S * P, D), F32, kind="Internal").ap()
        y_dram = nc.dram_tensor(f"{tag}_y_sorted", (S * P, D), F32, kind="Internal").ap()
        s = core.sems_in(f"{tag}r", NORM_SEMS + ["router", "xn", "T", "T_out", "logits", "logits_out", "w_up",
                                                 "w_down", "extra", "zeros", "zeroed", "consts", "filled"])
        phases = Phases(nc)

        block = phases.open()

        @block.sync
        def _(sp):
            for k in range(KT):
                sp.dma_start(router[:, k, :], ins[spec["router"]][:, k * P:(k + 1) * P].rearrange("e p -> p e"),
                             allow_slow_non_contiguous=True).then_inc(s["router"], 16)
            sp.wait_ge(s["zeros"], 1)
            sp.dma_start(sorted_dram.rearrange("(t p) d -> p t d", p=P), zeros[:, None, :].to_broadcast([P, S, D])
                         ).then_inc(s["zeroed"], 16)
            if gated:
                up4 = w_up[:, :].rearrange("p (e k u f) -> p e k u f", e=E, k=KT, u=2)
                for u, name in enumerate(("L2_ffn_gate_w", "L2_ffn_up_w")):
                    for k in range(KT):
                        sp.dma_start(up4[:, :, k, u, :], ins[name][:, k * P:(k + 1) * P, :].rearrange("e p f -> p e f")
                                     ).then_inc(s["w_up"], 16)
                sp.dma_start(w_down[:, :].rearrange("p (e m d) -> p e m d", e=E, m=FT),
                             ins["L2_ffn_down_w"].rearrange("e (m p) d -> p e m d", p=P)).then_inc(s["w_down"], 16)
                for u, name in enumerate(("L2_ffn_sh_gate_w", "L2_ffn_sh_up_w")):
                    sp.dma_start(sh_gu[:, u, :, :], ins[name].rearrange("(k p) f -> p k f", p=P)
                                 ).then_inc(s["extra"], 16)
                sp.dma_start(sh_down[:, :, :], ins["L2_ffn_sh_down_w"].rearrange("(m p) d -> p m d", p=P)
                             ).then_inc(s["extra"], 16)
                sp.dma_start(bias[:, :], ins["L2_ffn_bias"].rearrange("(a n) -> a n", a=1).to_broadcast([P, E])
                             ).then_inc(s["router"], 16)
            else:
                for k in range(KT):
                    sp.dma_start(w_up[:, :].rearrange("p (e k f) -> p e k f", e=E, k=KT)[:, :, k, :],
                                 ins["L1_ffn_w1"][:, k * P:(k + 1) * P, :].rearrange("e p f -> p e f")
                                 ).then_inc(s["w_up"], 16)
                for e in range(E):
                    sp.dma_start(w_down[:, e * FT * D:(e + 1) * FT * D].rearrange("p (m d) -> p m d", m=FT),
                                 ins["L1_ffn_w2"][e].rearrange("(m p) d -> p m d", p=P)).then_inc(s["w_down"], 16)
                sp.dma_start(b1[:, :], ins["L1_ffn_b1"].rearrange("(a e) f -> a (e f)", a=1).to_broadcast([P, E * F])
                             ).then_inc(s["extra"], 16)
                sp.dma_start(b2[:, :], ins["L1_ffn_b2"].rearrange("(a e) f -> a (e f)", a=1)).then_inc(s["extra"], 16)
        n_up, n_down = (4, 1) if gated else (KT, E)
        n_extra = 3 if gated else 2

        @block.gpsimd
        def _(pool):
            nc.gpsimd.memset(zeros[:, :], 0.0).then_inc(s["zeros"], 1)
            nc.gpsimd.iota(countdown[:, :], [[-1, E]], E, 0, allow_small_or_imprecise_dtypes=True
                           ).then_inc(s["consts"], 1)
            nc.gpsimd.iota(tile_no[:, :], [[1, S]], 0, 0, allow_small_or_imprecise_dtypes=True
                           ).then_inc(s["consts"], 1)
            for t in (restart_b, restart_e, before):
                nc.gpsimd.memset(t[:, :], 1.0).then_inc(s["filled"], 1)
            pool.wait_ge(s["filled"], 3)
            nc.gpsimd.memset(restart_b[:, :].rearrange("p (e b) -> p e b", e=E)[:, :, 0], 0.0).then_inc(s["consts"], 1)
            nc.gpsimd.memset(restart_e[:, :].rearrange("p (b e) -> p b e", e=E)[:, :, 0], 0.0).then_inc(s["consts"], 1)
            nc.gpsimd.affine_select(out=before[:, :], in_=before[:, :], compare_op=ALU.is_gt, fill=0.0, base=0,
                                    pattern=[[1, P]], channel_multiplier=-1).then_inc(s["consts"], 1)

        @block.tensor
        def _(pe):
            def transposed(j, b):
                pe.wait_ge(s["xn"], b + 1)
                after(pe, s["T_out"], b - 1)
                for k in range(KT):
                    t = nc.tensor.transpose(bank[j][:, k * P:(k + 1) * P], xn[j][:, k * P:(k + 1) * P],
                                            core.ident[:, :])
                t.then_inc(s["T"], 1)

            def body(j, b, first, last):
                if not last:
                    transposed(1 - j, b + 1)
                pe.wait_ge(s["T_out"], b + 1)
                after(pe, s["logits_out"], b - 1)
                for k in range(KT):
                    t = nc.tensor.matmul(bank[2 + j][:, 0:E], xT[j][:, k * P:(k + 1) * P], router[:, k, :],
                                         start=(k == 0), stop=(k == KT - 1))
                t.then_inc(s["logits"], 1)

            pe.wait_ge(s["router"], 48 if gated else 32)
            transposed(0, 0)
            over_batches(pe, body)

        @block.scalar
        def _(act):
            def body(j, b, first, last):
                act.wait_ge(s["T"], b + 1)
                after(act, s["logits"], b - 1)
                nc.scalar.copy(xT[j][:, :], bank[j][:, 0:D]).then_inc(s["T_out"], 1)

            finish_norm_scalar(core, act, s, temps)
            over_batches(act, body)

        @block.vector
        def _(dve):
            def norm(j, b):
                after(dve, s["T"], b - 1)
                normalise(core, xn[j][:, :], b).then_inc(s["xn"], 1)

            def body(j, b, first, last):
                if not last:
                    norm(1 - j, b + 1)
                dve.wait_ge(s["logits"], b + 1)
                nc.vector.tensor_copy(cols(logits, b * E, E), bank[2 + j][:, 0:E]).then_inc(s["logits_out"], 1)

            finish_norm_vector(core, dve, s, temps)
            norm(0, 0)
            over_batches(dve, body)

        m = core.sems_in(f"{tag}m", ["for_act", "from_act", "chosen", "counted", "step"])
        block = phases.open()

        @block.scalar
        def _(act):
            if gated:
                nc.scalar.activation(abc[1][:, :], logits[:, :], ACT.Sigmoid).then_inc(m["from_act"], 1)
            else:
                act.wait_ge(m["for_act"], 1)
                nc.scalar.activation(abc[1][:, :], abc[0][:, :], ACT.Exp).then_inc(m["from_act"], 1)

        @block.tensor
        def _(pe):
            pe.wait_ge(m["chosen"], 1)
            nc.tensor.matmul(bank[0][:, 0:N], before[:, :], chosen[:, :], start=True, stop=True)
            nc.tensor.matmul(bank[1][:, 0:N], core.ones[:, :], chosen[:, :], start=True, stop=True
                             ).then_inc(m["counted"], 1)

        @block.vector
        def _(dve):
            link = chain(dve, m["step"], 0)

            def be(t):
                return t[:, :].rearrange("p (b e) -> p b e", e=E)

            def eb(t):
                return t[:, :].rearrange("p (e b) -> p e b", e=E)

            views = dict(a=be(abc[0]), b=be(abc[1]), c=be(abc[2]), a2=abc[0][:, :], c2=abc[2][:, :],
                         chosen=be(chosen), share=be(share), countdown=countdown[:, :],
                         col=[small[:, i, :] for i in range(3)], restart_e2=restart_e[:, :])
            if gated:
                views.update(group=[group[:, i, :] for i in range(3)], sorted=best8[:, :], bias=bias[:, :])
            (choose_in_groups if gated else choose_best)(core, dve, link, m, views, be(logits))
            dve.sem_inc(m["chosen"], 1)
            dve.wait_ge(m["counted"], 1)
            total, cum = abc[0], abc[1]
            link(nc.vector.tensor_copy(eb(total), bank[1][:, 0:N].rearrange("p (b e) -> p e b", e=E)))
            link(nc.vector.tensor_tensor_scan(cum[:, :], restart_b[:, :], total[:, :], 0.0, ALU.mult, ALU.add))
            count, tiles, end, first = (per_e[:, i, :] for i in range(4))
            link(nc.vector.tensor_scalar(tiles, eb(cum)[:, :, B - 1], 1.0 / P, 63.5 / P, ALU.mult, ALU.add))
            link(nc.vector.tensor_scalar(tiles, tiles, MAGIC, None, ALU.add))
            link(nc.vector.tensor_scalar(tiles, tiles, -MAGIC, None, ALU.add))
            link(nc.vector.tensor_tensor_scan(end, core.ones[:, 0:E], tiles, 0.0, ALU.mult, ALU.add))
            link(nc.vector.tensor_tensor(first, end, tiles, ALU.subtract))
            link(nc.vector.tensor_scalar(first, first, float(P), None, ALU.mult))
            link(nc.vector.tensor_tensor(cum[:, :], cum[:, :], total[:, :], ALU.subtract))
            link(nc.vector.tensor_tensor(eb(cum), eb(cum), first[:, :, None].to_broadcast([P, E, B]), ALU.add))
            link(nc.vector.tensor_tensor(be(total), cum[:, :].rearrange("p (e b) -> p b e", e=E),
                                         bank[0][:, 0:N].rearrange("p (b e) -> p b e", e=E), ALU.add))
            place = total
            if K > 1:
                order, one_pick = abc[1], abc[2]
                link(nc.vector.tensor_tensor_scan(order[:, :], restart_e[:, :], chosen[:, :], 0.0, ALU.mult, ALU.add))
            for k in range(K):
                if K > 1:
                    link(nc.vector.scalar_tensor_tensor(one_pick[:, :], order[:, :], float(k + 1), chosen[:, :],
                                                        ALU.is_equal, ALU.mult))
                else:
                    one_pick = chosen
                link(nc.vector.tensor_tensor(logits[:, :], one_pick[:, :], place[:, :], ALU.mult))
                link(nc.vector.tensor_reduce(row[:, k, :], be(logits), AX.X, ALU.add))
                link(nc.vector.tensor_tensor(logits[:, :], one_pick[:, :], share[:, :], ALU.mult))
                link(nc.vector.tensor_reduce(pick_share[:, k * B:(k + 1) * B], be(logits), AX.X, ALU.add))
            nc.vector.tensor_copy(row_int[:, :], row[:, :, :].rearrange("p k b -> p (k b)"))
            link(nc.vector.tensor_tensor(tile_cmp[:, :].rearrange("p (t e) -> p t e", e=E),
                                         tile_no[:, :, None].to_broadcast([P, S, E]),
                                         end[:, None, :].to_broadcast([P, S, E]), ALU.is_ge))
            link(nc.vector.tensor_reduce(tile_e[:, :], tile_cmp[:, :].rearrange("p (t e) -> p t e", e=E), AX.X, ALU.add))
            nc.vector.tensor_scalar(tile_expert[:, :], tile_e[:, :], float(E - 1), None, ALU.min)

        c = core.sems_in(f"{tag}c", ["xn", "sent0", "sent1", "T", "T_out", "up", "silu", "h", "hT", "hT_out",
                                     "down", "updated"])
        block = phases.open()

        @block.gpsimd
        def _(pool):
            pool.wait_ge(s["zeroed"], 16)
            for b in range(B):
                pool.wait_ge(c["xn"], b + 1)
                for k in range(K):
                    pool.indirect_dma_start(
                        out=sorted_dram[:, :],
                        out_offset=bass.IndirectOffsetOnAxis(ap=row_int[:, k * B + b:k * B + b + 1], axis=0),
                        in_=xn[b % 2][:, :], in_offset=None).then_inc(c[f"sent{b % 2}"], 16)
            for j in range(2):
                pool.wait_ge(c[f"sent{j}"], 16 * K * B // 2)

        def sent(eng, j, b):
            if not (isinstance(b, int) and b < 2):
                eng.wait_ge(c[f"sent{j}"], (b - j) * (8 * K))

        if gated:
            @block.tensor
            def _(pe):
                def front(j, b):
                    pe.wait_ge(c["xn"], b + 1)
                    after(pe, c["T_out"], b)
                    for k in range(KT):
                        t = nc.tensor.transpose(bank[0][:, k * P:(k + 1) * P], xn[j][:, k * P:(k + 1) * P],
                                                core.ident[:, :])
                    t.then_inc(c["T"], 1)
                    pe.wait_ge(c["T_out"], b + 1)
                    after(pe, c["h"], b - 1)
                    for u in range(2):
                        for k in range(KT):
                            t = nc.tensor.matmul(bank[2 + 2 * j + u][:, :], xT[j][:, k * P:(k + 1) * P],
                                                 sh_gu[:, u, k, :], start=(k == 0), stop=(k == KT - 1))
                    t.then_inc(c["up"], 1)

                def body(j, b, first, last):
                    if not last:
                        front(1 - j, b + 1)
                    pe.wait_ge(c["h"], b + 1)
                    after(pe, c["hT_out"], b)
                    for k in range(SH // P):
                        t = nc.tensor.transpose(bank[1][:, k * P:(k + 1) * P], h[j][:, k * P:(k + 1) * P],
                                                core.ident[:, :])
                    t.then_inc(c["hT"], 1)
                    pe.wait_ge(c["hT_out"], b + 1)
                    after(pe, c["updated"], b - 1)
                    for k in range(SH // P):
                        t = nc.tensor.matmul(bank[6 + j][:, 0:D], hT[j][:, k * P:(k + 1) * P], sh_down[:, k, :],
                                             start=(k == 0), stop=(k == SH // P - 1))
                    t.then_inc(c["down"], 1)

                pe.wait_ge(s["extra"], 16 * n_extra)
                front(0, 0)
                over_batches(pe, body)

            @block.scalar
            def _(act):
                def front(j, b):
                    act.wait_ge(c["T"], b + 1)
                    after(act, c["up"], b - 1)
                    nc.scalar.copy(xT[j][:, :], bank[0][:, 0:D]).then_inc(c["T_out"], 1)
                    act.wait_ge(c["up"], b + 1)
                    after(act, c["h"], b - 1)
                    nc.scalar.activation(gate_h[j][:, :], bank[2 + 2 * j][:, :], ACT.Silu).then_inc(c["silu"], 1)

                def body(j, b, first, last):
                    if not last:
                        front(1 - j, b + 1)
                    act.wait_ge(c["hT"], b + 1)
                    after(act, c["down"], b - 1)
                    nc.scalar.copy(hT[j][:, :], bank[1][:, :]).then_inc(c["hT_out"], 1)

                front(0, 0)
                over_batches(act, body)

        @block.vector
        def _(dve):
            def front(j, b):
                sent(dve, j, b)
                if gated:
                    after(dve, c["T"], b - 1)
                normalise(core, xn[j][:, :], b).then_inc(c["xn"], 1)
                if gated:
                    dve.wait_ge(c["silu"], b + 1)
                    after(dve, c["hT"], b - 1)
                    nc.vector.tensor_tensor(h[j][:, :], gate_h[j][:, :], bank[3 + 2 * j][:, :], ALU.mult
                                            ).then_inc(c["h"], 1)

            def body(j, b, first, last):
                if not last:
                    front(1 - j, b + 1)
                if gated:
                    dve.wait_ge(c["down"], b + 1)
                    nc.vector.scalar_tensor_tensor(cols(core.x, b * D, D), bank[6 + j][:, 0:D],
                                                   core.gate(spec["layer"], 1), cols(core.x, b * D, D),
                                                   ALU.mult, ALU.add).then_inc(c["updated"], 1)

            front(0, 0)
            over_batches(dve, body)

        phases.close()
        routing.close()
        rows = [sb(f"{tag}_rows{j}", [P, D]) for j in range(2)]
        if gated:
            y = [sb(f"{tag}_y{j}", [P, D]) for j in range(2)]
        else:
            h, hT = hidden_buffers()
            y = xn
        q = core.sems_in(f"{tag}q", ["rows0", "rows1", "passed", "T", "T_out", "up", "silu", "h", "hT", "hT_out",
                                     "down", "y", "stored0", "stored1"])
        block = phases.open()

        def dram_rows(ap, t):
            return ap[bass.ds(t * P, P), :]

        @block.sync
        def _(sp):
            def load(j, t):
                sp.dma_start(rows[j][:, :], dram_rows(sorted_dram, t)).then_inc(q[f"rows{j}"], 16)

            def body(j, t, first, last):
                if not (isinstance(t, int) and t + 2 >= S):
                    sp.wait_ge(q["T"], t + 1)
                    settle(sp, q["passed"])
                    load(j, t + 2)
                sp.wait_ge(q["y"], t + 1)
                settle(sp, q["passed"])
                sp.dma_start(dram_rows(y_dram, t), y[j][:, :]).then_inc(q[f"stored{j}"], 16)

            load(0, 0)
            load(1, 1)
            over_batches(sp, body, S)
            for j in range(2):
                sp.wait_ge(q[f"stored{j}"], 16 * S // 2)

        def expert_of(eng, t):
            return eng.value_load(tile_expert[0:1, bass.ds(t, 1)], min_val=0, max_val=E - 1)

        @block.tensor
        def _(pe):
            def front(j, t):
                pe.wait_ge(q[f"rows{j}"], loads(t, j))
                after(pe, q["T_out"], t)
                for k in range(KT):
                    x = nc.tensor.transpose(bank[0][:, k * P:(k + 1) * P], rows[j][:, k * P:(k + 1) * P],
                                            core.ident[:, :])
                x.then_inc(q["T"], 1)
                e = expert_of(pe, t)
                pe.wait_ge(q["T_out"], t + 1)
                after(pe, q["h"], t if NU == 2 else t - 1)
                for n in range(NU):
                    for k in range(KT):
                        x = nc.tensor.matmul(bank[2 + n if NU == 2 else 2 + j][:, :], xT[j][:, k * P:(k + 1) * P],
                                             cols(w_up, e * (KT * UP) + (k * UP + n * 512), 512),
                                             start=(k == 0), stop=(k == KT - 1))
                x.then_inc(q["up"], 1)

            def body(j, t, first, last):
                if not last:
                    front(1 - j, t + 1)
                pe.wait_ge(q["h"], t + 1)
                after(pe, q["hT_out"], t)
                for k in range(FT):
                    x = nc.tensor.transpose(bank[4 + k // 4][:, (k % 4) * P:(k % 4 + 1) * P],
                                            h[j][:, k * P:(k + 1) * P], core.ident[:, :])
                x.then_inc(q["hT"], 1)
                e = expert_of(pe, t)
                pe.wait_ge(q["hT_out"], t + 1)
                after(pe, q["y"], t - 1)
                for k in range(FT):
                    x = nc.tensor.matmul(bank[6 + j][:, 0:D], hT[j][:, k * P:(k + 1) * P],
                                         cols(w_down, e * (FT * D) + k * D, D),
                                         start=(k == 0), stop=(k == FT - 1 and gated))
                if not gated:
                    x = nc.tensor.matmul(bank[6 + j][:, 0:D], core.ones[0:1, :], cols(b2, e * D, D),
                                         start=False, stop=True)
                x.then_inc(q["down"], 1)

            pe.wait_ge(s["w_up"], 16 * n_up)
            pe.wait_ge(s["w_down"], 16 * n_down)
            pe.wait_ge(s["extra"], 16 * n_extra)
            front(0, 0)
            over_batches(pe, body, S)

        @block.scalar
        def _(act):
            def front(j, t):
                act.wait_ge(q["T"], t + 1)
                after(act, q["up"], t - 1)
                nc.scalar.copy(xT[j][:, :], bank[0][:, 0:D]).then_inc(q["T_out"], 1)
                if gated:
                    act.wait_ge(q["up"], t + 1)
                    after(act, q["h"], t - 1)
                    nc.scalar.activation(gate_h[j][:, 0:F], bank[2 + j][:, 0:F], ACT.Silu).then_inc(q["silu"], 1)

            def body(j, t, first, last):
                if not last:
                    front(1 - j, t + 1)
                act.wait_ge(q["hT"], t + 1)
                after(act, q["down"], t - 1)
                for n in range((F + 511) // 512):
                    w = min(512, F - n * 512)
                    x = nc.scalar.activation(hT[j][:, n * 512:n * 512 + w], bank[4 + n][:, 0:w],
                                             ACT.Copy if gated else ACT.Relu)
                x.then_inc(q["hT_out"], 1)

            front(0, 0)
            over_batches(act, body, S)

        @block.vector
        def _(dve):
            def front(j, t):
                if gated:
                    dve.wait_ge(q["silu"], t + 1)
                    after(dve, q["hT"], t - 1)
                    nc.vector.tensor_tensor(h[j][:, 0:F], gate_h[j][:, 0:F], bank[2 + j][:, F:2 * F], ALU.mult
                                            ).then_inc(q["h"], 1)
                else:
                    e = expert_of(dve, t)
                    dve.wait_ge(q["up"], t + 1)
                    after(dve, q["hT"], t - 1)
                    for n in range(NU):
                        x = nc.vector.tensor_tensor(h[j][:, n * 512:(n + 1) * 512], bank[2 + n][:, :],
                                                    cols(b1, e * F + n * 512, 512), ALU.add)
                    x.then_inc(q["h"], 1)

            def body(j, t, first, last):
                if not last:
                    front(1 - j, t + 1)
                dve.wait_ge(q["down"], t + 1)
                if not (isinstance(t, int) and t < 2):
                    dve.wait_ge(q[f"stored{j}"], loads(t, j) - 16)
                nc.vector.tensor_copy(y[j][:, :], bank[6 + j][:, 0:D]).then_inc(q["y"], 1)

            if not gated:
                dve.wait_ge(s["extra"], 16 * n_extra)
            front(0, 0)
            over_batches(dve, body, S)

        g = core.sems_in(f"{tag}g", ["got0", "got1", "got2", "got3", "added"])
        got = [rows[0], rows[1], xn[0], xn[1]]
        NP = B * K
        block = phases.open()

        @block.gpsimd
        def _(pool):
            for n in range(NP):
                b, k = n // K, n % K
                after(pool, g["added"], n - 3)
                pool.indirect_dma_start(
                    out=got[n % 4][:, :], out_offset=None, in_=y_dram[:, :],
                    in_offset=bass.IndirectOffsetOnAxis(ap=row_int[:, k * B + b:k * B + b + 1], axis=0)
                ).then_inc(g[f"got{n % 4}"], 16)

        @block.vector
        def _(dve):
            with dve.Fori(0, NP // 4) as i:
                for r in range(4):
                    b, col = (i, i + r * B) if K == 4 else (i * 4 + r, i * 4 + r)
                    dve.wait_ge(g[f"got{r}"], i * 16 + 16)
                    if K == 4 and r:
                        dve.wait_ge(g["added"], i * 4 + r)
                    nc.vector.scalar_tensor_tensor(cols(core.x, b * D, D), got[r][:, :], cols(pick_share, col, 1),
                                                   cols(core.x, b * D, D), ALU.mult, ALU.add).then_inc(g["added"], 1)
            dve.wait_ge(g["added"], NP)
            for b in range(B):
                take_stats(core, b)

        phases.close()


def flamingo_stack(nc, ins, out):
    with ExitStack() as ctx:
        core = Core(nc, ins, out, ctx)
        sublayers = [
            lambda: attention(core, "L0x", 0, 16, "mask_Bx1xSxS2_ik1", L0_MASK, L0_X, False),
            lambda: depth_routed_block(core),
            lambda: bidirectional_attention(core),
            lambda: routed_experts(core, L1_EXPERTS),
            lambda: attention(core, "L2x", 2, 64, "mask_BxSxS2_ik0", L2_MASK, L2_X, True),
            lambda: routed_experts(core, L2_EXPERTS),
            lambda: warped_alignment(core),
            lambda: bit_ffn(core),
        ]
        load_and_prepare(core)
        for sublayer in sublayers:
            sublayer()
            core.give_back_sems()
        store_result(core)


_INS = ['x', 'ctx_1024', 'mask_Bx1xSxS2_ik1', 'mask_BxSxS2_ik0', 'g_xattn', 'g_ffn',
        'L0_xattn_wq', 'L0_xattn_wk', 'L0_xattn_wv', 'L0_xattn_wo', 'L0_xattn_bo',
        'L0_ffn_attention_mask', 'L0_ffn_position_ids', 'L0_ffn_router_w', 'L0_ffn_router_b',
        'L0_ffn_wq', 'L0_ffn_wk', 'L0_ffn_wv', 'L0_ffn_wo', 'L0_ffn_w1', 'L0_ffn_w2', 'L0_ffn_ln1', 'L0_ffn_ln2',
        'L1_xattn_w_sim', 'L1_xattn_b_sim', 'L1_xattn_W_qv', 'L1_xattn_b_qv',
        'L1_ffn_gate_w', 'L1_ffn_w1', 'L1_ffn_b1', 'L1_ffn_w2', 'L1_ffn_b2',
        'L2_xattn_Wq', 'L2_xattn_bq', 'L2_xattn_Wk', 'L2_xattn_bk', 'L2_xattn_Wv', 'L2_xattn_bv',
        'L2_xattn_Wo', 'L2_xattn_bo',
        'L2_ffn_router_w', 'L2_ffn_bias', 'L2_ffn_gate_w', 'L2_ffn_up_w', 'L2_ffn_down_w',
        'L2_ffn_sh_gate_w', 'L2_ffn_sh_up_w', 'L2_ffn_sh_down_w',
        'L3_ffn_w_gate', 'L3_ffn_w_up', 'L3_ffn_w_down']


def kernel(**inputs):
    import concourse.bacc as bacc
    from concourse.bass_utils import run_bass_kernel_spmd

    nc = bacc.Bacc("TRN2", target_bir_lowering=False, num_devices=1)
    arrays, ins = {}, {}
    for name in _INS:
        a = np.ascontiguousarray(inputs[name])
        arrays[f"in_{name}"] = a
        ins[name] = nc.dram_tensor(f"in_{name}", a.shape, mybir.dt.from_np(a.dtype), kind="ExternalInput").ap()
    out = nc.dram_tensor("out_x", (B, P, D), F32, kind="ExternalOutput").ap()
    flamingo_stack(nc, ins, out)
    r = run_bass_kernel_spmd(nc, [arrays], core_ids=[0])
    return r.results[0]["out_x"]
```

```python
from contextlib import ExitStack

import numpy as np

import concourse.bass as bass
from concourse import mybir



F32 = mybir.dt.float32
U32 = mybir.dt.uint32
BF16 = mybir.dt.bfloat16
I32 = mybir.dt.int32
ALU = mybir.AluOpType
ACT = mybir.ActivationFunctionType
AX = mybir.AxisListType

P = 128
B = 16
D = 256
KT = D // P
LN_EPS = 1e-5
BIG = 1e30
MAGIC = 1.5 * 2.0 ** 23


def after(eng, sem, count):
    if isinstance(count, int) and count <= 0:
        return
    eng.wait_ge(sem, count)


def loads(b, j):
    return (b - j) * 8 + 16


def settle(eng, sem):
    eng.sem_inc(sem, 1)


def over_batches(eng, body, n=B):
    body(0, 0, True, False)
    body(1, 1, False, False)
    with eng.Fori(0, (n - 4) // 2) as i:
        body(0, i * 2 + 2, False, False)
        body(1, i * 2 + 3, False, False)
    body(0, n - 2, False, False)
    body(1, n - 1, False, True)


def two_left(b):
    return isinstance(b, int) and b + 2 >= B


def over_batches_by_four(eng, body):
    body(0, 0, True, False)
    body(1, 1, False, False)
    with eng.Fori(0, (B - 4) // 4) as i:
        for u in range(4):
            body((2 + u) % 4, i * 4 + (2 + u), False, False)
    body((B - 2) % 4, B - 2, False, False)
    body((B - 1) % 4, B - 1, False, True)


def chain(eng, sem, base):
    count = [0]

    def link(ins):
        ins.then_inc(sem, 1)
        count[0] += 1
        eng.wait_ge(sem, base + count[0])

    link.count = count
    return link


def cols(t, start, n):
    return t[:, bass.ds(start, n)]


class Phases:

    def __init__(self, nc):
        self.nc, self.stack = nc, None

    def open(self):
        self.close()
        self.stack = ExitStack()
        return self.stack.enter_context(self.nc.Block())

    def close(self):
        if self.stack is not None:
            self.stack.close()
        self.stack = None


class Core:

    def __init__(self, nc, ins, out, ctx):
        self.nc, self.ins, self.out, self.ctx = nc, ins, out, ctx
        self.sems = []
        sb = self.sbuf_in(ctx)
        self.x = sb("x", [P, B * D])
        self.stats = sb("stats", [P, B * 6])
        self.rstd = sb("rstd", [P, B])
        self.neg_mean_rstd = sb("neg_mean_rstd", [P, B])
        self.ident = sb("ident", [P, P])
        self.ones = sb("ones", [P, P])
        self.gates = sb("gates", [P, 8])

    def sbuf_in(self, ctx):
        return lambda name, shape, dt=F32: ctx.enter_context(self.nc.sbuf_tensor(name, shape, dt))

    def banks_in(self, ctx, tag):
        return [ctx.enter_context(self.nc.psum_tensor(f"{tag}_bank{i}", [P, 512], F32)) for i in range(8)]

    def sems_in(self, tag, names):
        made = {n: self.nc.alloc_semaphore(name=f"{tag}_{n}") for n in names}
        self.sems.extend(made.values())
        return made

    def give_back_sems(self):
        self.nc.clear_and_free_semaphores(self.sems)
        self.nc.all_engine_barrier()
        self.sems = []

    def gate(self, layer, ffn):
        k = 4 * ffn + layer
        return self.gates[:, k:k + 1]


def load_and_prepare(core):
    nc, ins = core.nc, core.ins
    with ExitStack() as ctx:
        s = core.sems_in("prep", ["x_loaded", "gates_loaded", "cleared"])

        block = ctx.enter_context(nc.Block())

        @block.sync
        def _(sp):
            for b in range(0, B, 4):
                sp.dma_start(core.x[:, b * D:(b + 4) * D].rearrange("p (b d) -> p b d", d=D),
                             ins["x"][b:b + 4].rearrange("b s d -> s b d")).then_inc(s["x_loaded"], 16)

        @block.scalar
        def _(act):
            for k, name in enumerate(("g_xattn", "g_ffn")):
                act.dma_start(core.gates[:, 4 * k:4 * k + 4],
                              ins[name].rearrange("(a n) -> a n", a=1).to_broadcast([P, 4])
                              ).then_inc(s["gates_loaded"], 16)
            act.wait_ge(s["gates_loaded"], 32)
            nc.scalar.activation(core.gates[:, :], core.gates[:, :], ACT.Tanh)

        @block.gpsimd
        def _(pool):
            nc.gpsimd.memset(core.ident[:, :], 0.0).then_inc(s["cleared"], 1)
            nc.gpsimd.memset(core.ones[:, :], 1.0)
            pool.wait_ge(s["cleared"], 1)
            nc.gpsimd.affine_select(out=core.ident[:, :], in_=core.ident[:, :], compare_op=ALU.not_equal,
                                    fill=1.0, base=0, pattern=[[-1, P]],
                                    channel_multiplier=1).then_inc(s["cleared"], 1)

        @block.vector
        def _(dve):
            for b in range(B):
                if b == 0:
                    dve.wait_ge(s["x_loaded"], 64)
                nc.vector.bn_stats(core.stats[:, 6 * b:6 * b + 6], core.x[:, b * D:(b + 1) * D])


def finish_norm_vector(core, dve, s, temps):
    nc = core.nc
    st = core.stats[:, :].rearrange("p (b k) -> p b k", k=6)
    mean_e, var_e, mean_o, var_o = st[:, :, 1], st[:, :, 2], st[:, :, 4], st[:, :, 5]
    half, var, mean, root = (temps[:, k, :] for k in range(4))
    link = chain(dve, s["norm_step"], 0)
    link(nc.vector.tensor_tensor(half, mean_e, mean_o, ALU.subtract))
    link(nc.vector.tensor_tensor(var, var_e, var_o, ALU.add))
    link(nc.vector.tensor_tensor(half, half, half, ALU.mult))
    link(nc.vector.tensor_scalar(var, var, 1.0 / D, LN_EPS, ALU.mult, ALU.add))
    nc.vector.scalar_tensor_tensor(var, half, 0.25, var, ALU.mult, ALU.add).then_inc(s["norm_var"], 1)
    link(nc.vector.tensor_tensor(mean, mean_e, mean_o, ALU.add))
    dve.wait_ge(s["norm_root"], 1)
    link(nc.vector.reciprocal(core.rstd[:, :], root))
    link(nc.vector.scalar_tensor_tensor(core.neg_mean_rstd[:, :], mean, -0.5, core.rstd[:, :], ALU.mult, ALU.mult))


def finish_norm_scalar(core, act, s, temps):
    act.wait_ge(s["norm_var"], 1)
    core.nc.scalar.activation(temps[:, 3, :], temps[:, 1, :], ACT.Sqrt).then_inc(s["norm_root"], 1)


NORM_SEMS = ["norm_step", "norm_var", "norm_root"]


def normalise(core, out, b):
    return core.nc.vector.tensor_scalar(out, cols(core.x, b * D, D), cols(core.rstd, b, 1),
                                        cols(core.neg_mean_rstd, b, 1), ALU.mult, ALU.add)


def take_stats(core, b):
    return core.nc.vector.bn_stats(cols(core.stats, b * 6, 6), cols(core.x, b * D, D))


def store_result(core):
    nc = core.nc
    s = core.sems_in("store", ["stored"])
    with nc.Block() as block:
        @block.sync
        def _(sp):
            for b in range(0, B, 4):
                sp.dma_start(core.out[b:b + 4].rearrange("b s d -> s b d"),
                             core.x[:, b * D:(b + 4) * D].rearrange("p (b d) -> p b d", d=D)
                             ).then_inc(s["stored"], 16)
            sp.wait_ge(s["stored"], 64)


def attention(core, tag, layer, head_dim, mask_name, mask_of, wname, biased, ahead=None):
    nc, ins = core.nc, core.ins
    H = 16
    E = H * head_dim
    small = head_dim == 16
    QT = 4 if small else E // P
    KTL = E // P
    VW = head_dim + 1
    scale = head_dim ** -0.5
    with ExitStack() as ctx:
        sb = core.sbuf_in(ctx)
        wq = sb(f"{tag}_wq", [P, KT, QT * P])
        wk = sb(f"{tag}_wk", [P, KT, E])
        wv = sb(f"{tag}_wv", [P, KT, E])
        wo = sb(f"{tag}_wo", [P, KTL, D])
        bo = sb(f"{tag}_bo", [P, D])
        gated_bias = sb(f"{tag}_gated_bias", [P, D])
        if biased:
            bq = sb(f"{tag}_bq", [P, KTL])
            bk = sb(f"{tag}_bk", [P, KTL])
            bv = sb(f"{tag}_bv", [P, KTL])
            bv_wo = [sb(f"{tag}_bv_wo{i}", [P, D]) for i in range(2)]
        mask_diag = sb(f"{tag}_mask_diag", [P, P], BF16)
        temps = sb(f"{tag}_temps", [P, 4, B])
        ctx_in = [sb(f"{tag}_ctx{j}", [P, D]) for j in range(2)]
        mask_in = [sb(f"{tag}_mask{j}", [P, P], I32) for j in range(2)]
        mask_add = [sb(f"{tag}_mask_add{j}", [P, P], BF16) for j in range(2)]
        xn = [sb(f"{tag}_xn{j}", [P, D]) for j in range(2)]
        xcT = [sb(f"{tag}_xcT{j}", [P, 2 * KT, P]) for j in range(2)]
        qT = [sb(f"{tag}_qT{j}", [P, QT, P]) for j in range(2)]
        kT = [sb(f"{tag}_kT{j}", [P, KTL, P]) for j in range(2)]
        v1 = [sb(f"{tag}_v1{j}", [P, H, VW]) for j in range(2)]
        top = sb(f"{tag}_top", [P, 2, 4])
        shifted = [sb(f"{tag}_shifted{j}", [P, 4, P]) for j in range(2)]
        probs = [sb(f"{tag}_probs{j}", [P, 4, P]) for j in range(2)]
        probsT = [sb(f"{tag}_probsT{j}", [P, 4, P]) for j in range(2)]
        inv_sum = sb(f"{tag}_inv_sum", [P, 2, 4])
        heads = [sb(f"{tag}_heads{j}", [P, E]) for j in range(2)]
        headsT = sb(f"{tag}_headsT", [P, KTL, P])
        bank = core.banks_in(ctx, tag)
        front_bank, score_bank, pT_bank, out_bank, back_bank = bank[0:2], bank[2:4], bank[4:6], bank[6], bank[7]
        s = core.sems_in(tag, NORM_SEMS + [
            "w_q", "w_k", "w_v", "w_o", "biases", "diag", "ctx_in0", "ctx_in1", "mask_in0", "mask_in1", "mask_add", "xn",
            "filled", "evicted_act", "evicted_dve",
            "scores", "maxed", "shifted", "exped", "pT", "pT_out", "pv", "inv", "normed", "ones_col",
            "headsT", "headsT_out", "projected", "updated", "passed",
            "bv_wo", "bv_row", "gated_bias", "x_biased"])

        if small:
            fills = ["T", "Q0", "KV"]
            slots = [[0], [1, 2], [], []]
        else:
            fills = ["T", "Q0", "Q1", "K0", "K1", "V0", "V1"]
            slots = [[0, 1], [2, 3, 4], [5, 6], []]
        NF = len(fills)
        by_dve = [f[0] in "QK" and biased for f in fills]
        NA, ND = NF - sum(by_dve), sum(by_dve)
        TB = (KTL + 3) // 4

        def evicted(eng, b, f):
            if by_dve[f]:
                after(eng, s["evicted_dve"], b * ND + sum(by_dve[:f + 1]))
            else:
                after(eng, s["evicted_act"], b * NA + f + 1 - sum(by_dve[:f + 1]))

        def head_of(g, i):
            return 2 * g + 8 * (i // 2) + i % 2 if small else 8 * (g // 2) + 2 * i + g % 2

        def head_at(h):
            if small:
                i, odd = h // 2, h % 2
                return 2 * odd + i // 4, i // 4, slice(32 * (i % 4), 32 * (i % 4) + 32)
            return h // 2, h // 2, slice(64 * (h % 2), 64 * (h % 2) + 64)

        def of_unit(t, g):
            if small:
                return t.rearrange("p (a r o c) -> p r a o c", a=2, r=4, o=2)[:, g]
            return t.rearrange("p (m i s c) -> p m i s c", m=2, i=4, s=2)[:, g // 2, :, g % 2:g % 2 + 1]

        n_wq = 2 * KT if small else KT

        block = ctx.enter_context(nc.Block())

        @block.sync
        def _(sp):
            def w2d(name):
                w = ins[wname[name]]
                return w if len(w.shape) == 2 else w.rearrange("d n h -> d (n h)")

            def loaded(dst, src, which, scattered=False):
                sp.dma_start(dst, src, allow_slow_non_contiguous=scattered).then_inc(s[which], 16)

            mask = ins[mask_name]
            if len(mask.shape) == 4:
                mask = mask.rearrange("b a q k -> b (a q) k")

            def load_inputs(j, b):
                sp.dma_start(ctx_in[j][:, :], one(ins["ctx_1024"], b)).then_inc(s[f"ctx_in{j}"], 16)
                sp.dma_start(mask_in[j][:, :], one(mask, b)).then_inc(s[f"mask_in{j}"], 16)

            for b in range(2):
                load_inputs(b, b)
            if biased:
                for name, dst in (("bq", bq), ("bk", bk), ("bv", bv)):
                    flat = ins[wname[name]].rearrange("n h -> (n h)")
                    loaded(dst[:, :], flat.rearrange("(t p) -> p t", p=P), "biases", True)
            if small:
                sp.wait_ge(s["diag"], 2)
                for k in range(KT):
                    for odd in range(2):
                        dst = wq[:, k, odd * D:(odd + 1) * D].rearrange("p (i o c) -> p i o c", o=2, c=16)
                        src = w2d("wq")[k * P:(k + 1) * P, :].rearrange("p (i o c) -> p i o c", o=2, c=16)
                        loaded(dst[:, :, odd, :], src[:, :, odd, :], "w_q")
            else:
                for k in range(KT):
                    loaded(wq[:, k, :], w2d("wq")[k * P:(k + 1) * P, :], "w_q")
            for dst, name in ((wk, "wk"), (wv, "wv")):
                for k in range(KT):
                    loaded(dst[:, k, :], w2d(name)[k * P:(k + 1) * P, :], "w_" + name[1])
            wo_d = ins[wname["wo"]]
            wo_d = wo_d if len(wo_d.shape) == 2 else wo_d.rearrange("n h d -> (n h) d")
            loaded(wo[:, :, :], wo_d.rearrange("(t p) d -> p t d", p=P), "w_o")
            loaded(bo[:, :], ins[wname["bo"]].rearrange("(a n) -> a n", a=1).to_broadcast([P, D]), "w_o")
            if ahead:
                sp.wait_ge(ahead.sems["zeros"], 1)
                for b in range(2):
                    ahead.part(sp, b)

            def body(j, b):
                evicted(sp, b - 2, 0)
                settle(sp, s["passed"])
                sp.wait_ge(s["mask_add"], b - 1)
                settle(sp, s["passed"])
                load_inputs(j, b)
                if ahead:
                    ahead.part(sp, b)

            with sp.Fori(1, B // 2) as i:
                for j in range(2):
                    body(j, i * 2 + j)
            if ahead:
                ahead.all_in(sp)

        @block.gpsimd
        def _(pool):
            if ahead:
                ahead.make_zeros()
            nc.gpsimd.memset(mask_diag[:, :], 0.0).then_inc(s["diag"], 1)
            if small:
                nc.gpsimd.memset(wq[:, :, :], 0.0).then_inc(s["diag"], 1)
            for j in range(2):
                nc.gpsimd.memset(v1[j][:, :, head_dim], 1.0).then_inc(s["ones_col"], 1)
            pool.wait_ge(s["diag"], 2 if small else 1)
            nc.gpsimd.affine_select(out=mask_diag[:, :], in_=mask_diag[:, :], compare_op=ALU.not_equal,
                                    fill=mask_of["diag"], base=0, pattern=[[-1, P]],
                                    channel_multiplier=1).then_inc(s["diag"], 1)

            def add_bias(j, b, first, last):
                pool.wait_ge(s["xn"], b + 1)
                nc.gpsimd.tensor_tensor(cols(core.x, b * D, D), cols(core.x, b * D, D), gated_bias[:, :], ALU.add
                                        ).then_inc(s["x_biased"], 1)

            pool.wait_ge(s["gated_bias"], 1)
            over_batches(pool, add_bias)

        @block.tensor
        def _(pe):
            def front(j, b, f):
                kind = fills[f]
                n = j * NF + f
                dst = front_bank[n % 2]
                if not (isinstance(b, int) and b * NF + f < 2):
                    if f >= 2:
                        evicted(pe, b, f - 2)
                    else:
                        evicted(pe, b - 1, NF - 2 + f)
                if kind == "T":
                    pe.wait_ge(s["xn"], b + 1)
                    pe.wait_ge(s[f"ctx_in{j}"], loads(b, j))
                    for k in range(KT):
                        nc.tensor.transpose(dst[:, k * P:(k + 1) * P], xn[j][:, k * P:(k + 1) * P], core.ident[:, :])
                    for k in range(KT):
                        last = nc.tensor.transpose(dst[:, (KT + k) * P:(KT + k + 1) * P],
                                                   ctx_in[j][:, k * P:(k + 1) * P], core.ident[:, :])
                    last.then_inc(s["filled"], 1)
                    return
                evicted(pe, b, 0)
                if kind[0] in "QK":
                    w, of = (wq, 0) if kind[0] == "Q" else (wk, KT)
                    tiles = range(4 * int(kind[1]), 4 * int(kind[1]) + 4) if kind != "KV" else range(KTL)
                    for i, t in enumerate(tiles):
                        for k in range(KT):
                            last = nc.tensor.matmul(dst[:, i * P:(i + 1) * P], w[:, k, t * P:(t + 1) * P],
                                                    xcT[j][:, of + k, :], start=(k == 0), stop=(k == KT - 1))
                if kind in ("KV", "V0", "V1"):
                    at, w0, nw = (D, 0, E) if kind == "KV" else (0, 512 * int(kind[1]), 512)
                    for k in range(KT):
                        last = nc.tensor.matmul(dst[:, at:at + nw], xcT[j][:, KT + k, :], wv[:, k, w0:w0 + nw],
                                                start=(k == 0), stop=(k == KT - 1))
                last.then_inc(s["filled"], 1)

            def scores(j, b, g):
                u = b * 4 + g
                dst = score_bank[g % 2]
                if g == 0:
                    if ND:
                        pe.wait_ge(s["evicted_dve"], b * ND + ND)
                    else:
                        pe.wait_ge(s["evicted_act"], b * NA + NA)
                    pe.wait_ge(s["mask_add"], b + 1)
                after(pe, s["shifted"], u - 1)
                nc.tensor.matmul(dst[:, :].rearrange("p (h k) -> p h k", h=4), mask_diag[:, :],
                                 mask_add[j][:, None, :].to_broadcast([P, 4, P]), start=True, stop=False)
                for i in range(4):
                    tq, tk, rows = head_at(head_of(g, i))
                    last = nc.tensor.matmul(dst[:, i * P:(i + 1) * P], qT[j][rows, tq, :], kT[j][rows, tk, :],
                                            start=False, stop=(i == 3))
                last.then_inc(s["scores"], 1)

            def transposed(j, b, g):
                u = b * 4 + g
                pe.wait_ge(s["exped"], u + 1)
                after(pe, s["pT_out"], u - 1)
                for i in range(4):
                    last = nc.tensor.transpose(pT_bank[g % 2][:, i * P:(i + 1) * P], probs[g % 2][:, i, :],
                                               core.ident[:, :])
                last.then_inc(s["pT"], 1)

            def weighted(j, b, g):
                u = b * 4 + g
                if g == 0:
                    pe.wait_ge(s["evicted_act"], b * NA + NA)
                pe.wait_ge(s["pT_out"], u + 1)
                after(pe, s["normed"], u)
                for i in range(4):
                    last = nc.tensor.matmul(out_bank[:, i * VW:(i + 1) * VW], probsT[g % 2][:, i, :],
                                            v1[j][:, head_of(g, i), :], start=True, stop=True)
                last.then_inc(s["pv"], 1)

            def back_transpose(j, b, t):
                pe.wait_ge(s["normed"], 4 * b + 4)
                if t == 0:
                    after(pe, s["updated"], b)
                else:
                    pe.wait_ge(s["headsT_out"], b * TB + t)
                for i in range(4 * t, min(4 * t + 4, KTL)):
                    last = nc.tensor.transpose(back_bank[:, (i - 4 * t) * P:(i - 4 * t + 1) * P],
                                               heads[j][:, i * P:(i + 1) * P], core.ident[:, :])
                last.then_inc(s["headsT"], 1)

            def back_project(j, b):
                pe.wait_ge(s["headsT_out"], (b + 1) * TB)
                for i in range(KTL):
                    last = nc.tensor.matmul(back_bank[:, 0:D], headsT[:, i, :], wo[:, i, :],
                                            start=(i == 0), stop=(i == KTL - 1))
                last.then_inc(s["projected"], 1)

            def body(j, b, first, last):
                for g in range(4):
                    if g:
                        weighted(j, b, g - 1)
                    elif not first:
                        weighted(1 - j, b - 1, 3)
                    transposed(j, b, g)
                    if g < 2:
                        scores(j, b, g + 2)
                    elif not last:
                        scores(1 - j, b + 1, g - 2)
                    if not last:
                        for f in slots[g]:
                            front(1 - j, b + 1, f)
                    if not first and 1 <= g <= TB:
                        back_transpose(1 - j, b - 1, g - 1)
                    if not first and g == TB + 1:
                        back_project(1 - j, b - 1)

            pe.wait_ge(s["diag"], 3 if small else 2)
            pe.wait_ge(s["ones_col"], 2)
            for f in range(NF):
                if fills[f] == "Q0":
                    pe.wait_ge(s["w_q"], 16 * n_wq)
                if fills[f] in ("K0", "KV"):
                    pe.wait_ge(s["w_k"], 16 * KT)
                if fills[f] in ("V0", "KV"):
                    pe.wait_ge(s["w_v"], 16 * KT)
                front(0, 0, f)
            scores(0, 0, 0)
            scores(0, 0, 1)
            if biased:
                pe.wait_ge(s["bv_wo"], KTL)
                nc.tensor.matmul(back_bank[:, 0:D], core.ones[:, :], bv_wo[(KTL - 1) % 2][:, :], start=True, stop=True
                                 ).then_inc(s["bv_row"], 1)
            pe.wait_ge(s["w_o"], 32)
            over_batches(pe, body)
            weighted(1, B - 1, 3)
            for t in range(TB):
                back_transpose(1, B - 1, t)
            back_project(1, B - 1)

        @block.scalar
        def _(act):
            def take(j, b, f):
                if by_dve[f]:
                    return
                n = j * NF + f
                src = front_bank[n % 2]
                kind = fills[f]
                act.wait_ge(s["filled"], b * NF + f + 1)
                after(act, s["pv"], 4 * (b - 1))
                if kind == "T":
                    nc.scalar.copy(xcT[j][:, :, :].rearrange("p t c -> p (t c)"), src[:, :]
                                   ).then_inc(s["evicted_act"], 1)
                elif kind[0] == "Q":
                    t0 = 4 * int(kind[1])
                    nc.scalar.copy(qT[j][:, t0:t0 + 4, :].rearrange("p t c -> p (t c)"), src[:, :]
                                   ).then_inc(s["evicted_act"], 1)
                elif kind == "KV":
                    nc.scalar.copy(kT[j][:, :, :].rearrange("p t c -> p (t c)"), src[:, 0:E])
                    nc.scalar.copy(v1[j][:, :, 0:head_dim], src[:, D:D + E].rearrange("p (h c) -> p h c", c=head_dim)
                                   ).then_inc(s["evicted_act"], 1)
                else:
                    h0 = 8 * int(kind[1])
                    nc.scalar.copy(v1[j][:, h0:h0 + 8, 0:head_dim],
                                   src[:, :].rearrange("p (h c) -> p h c", c=head_dim)).then_inc(s["evicted_act"], 1)

            def exp(b, g):
                u = b * 4 + g
                act.wait_ge(s["shifted"], u + 1)
                after(act, s["pT"], u - 1)
                nc.scalar.activation(probs[g % 2][:, :, :], shifted[g % 2][:, :, :], ACT.Exp, scale=scale
                                     ).then_inc(s["exped"], 1)

            def take_pT(b, g):
                u = b * 4 + g
                act.wait_ge(s["pT"], u + 1)
                after(act, s["pv"], u - 1)
                nc.scalar.copy(probsT[g % 2][:, :, :].rearrange("p h q -> p (h q)"), pT_bank[g % 2][:, :]
                               ).then_inc(s["pT_out"], 1)

            def take_headsT(b, t):
                act.wait_ge(s["headsT"], b * TB + t + 1)
                after(act, s["projected"], b)
                n = min(4, KTL - 4 * t)
                nc.scalar.copy(headsT[:, 4 * t:4 * t + n, :].rearrange("p t c -> p (t c)"), back_bank[:, 0:n * P]
                               ).then_inc(s["headsT_out"], 1)

            def body(j, b, first, last):
                for g in range(4):
                    take_pT(b, g)
                    if g < 3:
                        exp(b, g + 1)
                    if not last:
                        for f in slots[g]:
                            take(1 - j, b + 1, f)
                    if not first and 1 <= g <= TB:
                        take_headsT(b - 1, g - 1)
                    if g == 3 and not last:
                        exp(b + 1, 0)

            finish_norm_scalar(core, act, s, temps)
            for f in range(NF):
                take(0, 0, f)
            exp(0, 0)
            over_batches(act, body)
            for t in range(TB):
                take_headsT(B - 1, t)

        @block.vector
        def _(dve):
            def prepare(j, b):
                if not isinstance(b, int) or b >= 2:
                    evicted(dve, b - 2, 0)
                normalise(core, xn[j][:, :], b).then_inc(s["xn"], 1)
                dve.wait_ge(s[f"mask_in{j}"], loads(b, j))
                after(dve, s["scores"], 4 * (b - 1))
                nc.vector.tensor_scalar(mask_add[j][:, :], mask_in[j][:, :], mask_of["compare"], mask_of["times"],
                                        mask_of["op"], ALU.mult).then_inc(s["mask_add"], 1)

            def take(j, b, f):
                if not by_dve[f]:
                    return
                src = front_bank[(j * NF + f) % 2]
                kind = fills[f]
                dst, bias = (qT, bq) if kind[0] == "Q" else (kT, bk)
                t0 = 4 * int(kind[1])
                dve.wait_ge(s["filled"], b * NF + f + 1)
                after(dve, s["scores"], 4 * (b - 1))
                nc.vector.tensor_tensor(dst[j][:, t0:t0 + 4, :], src[:, :].rearrange("p (t c) -> p t c", t=4),
                                        bias[:, t0:t0 + 4, None].to_broadcast([P, 4, P]), ALU.add
                                        ).then_inc(s["evicted_dve"], 1)

            def shift(b, g):
                u = b * 4 + g
                src = score_bank[g % 2][:, :].rearrange("p (h k) -> p h k", h=4)
                dve.wait_ge(s["scores"], u + 1)
                nc.vector.tensor_reduce(top[:, g % 2, :], src, AX.X, ALU.max).then_inc(s["maxed"], 1)
                dve.wait_ge(s["maxed"], u + 1)
                after(dve, s["exped"], u - 1)
                nc.vector.tensor_tensor(shifted[g % 2][:, :, :], src,
                                        top[:, g % 2, :][:, :, None].to_broadcast([P, 4, P]), ALU.subtract
                                        ).then_inc(s["shifted"], 1)

            def norm(j, b, g):
                u = b * 4 + g
                pairs = dict(a=2, o=2) if small else dict(a=4, o=1)
                src = out_bank[:, 0:4 * VW].rearrange("p (h c) -> p h c", h=4)
                src4 = out_bank[:, 0:4 * VW].rearrange("p (a o c) -> p a o c", **pairs)
                inv4 = inv_sum[:, g % 2, :].rearrange("p (a o) -> p a o", **pairs)
                dve.wait_ge(s["pv"], u + 1)
                nc.vector.reciprocal(inv_sum[:, g % 2, :], src[:, :, head_dim]).then_inc(s["inv"], 1)
                dve.wait_ge(s["inv"], u + 1)
                after(dve, s["projected"], b - 1)
                nc.vector.tensor_tensor(of_unit(heads[j][:, :], g), src4[:, :, :, 0:head_dim],
                                        inv4[:, :, :, None].to_broadcast([P, pairs["a"], pairs["o"], head_dim]),
                                        ALU.mult
                                        ).then_inc(s["normed"], 1)

            def make_bias():
                dve.wait_ge(s["w_o"], 32)
                if biased:
                    for i in range(KTL):
                        after(dve, s["bv_wo"], i)
                        if i == 0:
                            t = nc.vector.tensor_scalar(bv_wo[0][:, :], wo[:, 0, :], bv[:, 0:1], None, ALU.mult)
                        else:
                            t = nc.vector.scalar_tensor_tensor(bv_wo[i % 2][:, :], wo[:, i, :], bv[:, i:i + 1],
                                                               bv_wo[(i - 1) % 2][:, :], ALU.mult, ALU.add)
                        t.then_inc(s["bv_wo"], 1)
                    dve.wait_ge(s["bv_row"], 1)
                    nc.vector.tensor_tensor(bo[:, :], bo[:, :], back_bank[:, 0:D], ALU.add).then_inc(s["bv_row"], 1)
                    dve.wait_ge(s["bv_row"], 2)
                nc.vector.tensor_scalar(gated_bias[:, :], bo[:, :], core.gate(layer, 0), None, ALU.mult
                                        ).then_inc(s["gated_bias"], 1)

            def update(b):
                dve.wait_ge(s["projected"], b + 1)
                dve.wait_ge(s["x_biased"], b + 1)
                nc.vector.scalar_tensor_tensor(cols(core.x, b * D, D), back_bank[:, 0:D], core.gate(layer, 0),
                                               cols(core.x, b * D, D), ALU.mult, ALU.add).then_inc(s["updated"], 1)
                dve.wait_ge(s["updated"], b + 1)
                take_stats(core, b)

            def body(j, b, first, last):
                for g in range(4):
                    if g:
                        norm(j, b, g - 1)
                    elif not first:
                        norm(1 - j, b - 1, 3)
                    if g == 0 and not last:
                        prepare(1 - j, b + 1)
                    if g < 2:
                        shift(b, g + 2)
                    elif not last:
                        shift(b + 1, g - 2)
                    if not last:
                        for f in slots[g]:
                            take(1 - j, b + 1, f)
                    if not first and g == TB + 1:
                        update(b - 1)

            finish_norm_vector(core, dve, s, temps)
            prepare(0, 0)
            if biased:
                dve.wait_ge(s["biases"], 48)
            for f in range(NF):
                take(0, 0, f)
            shift(0, 0)
            shift(0, 1)
            make_bias()
            over_batches(dve, body)
            norm(1, B - 1, 3)
            update(B - 1)


def one(ap, b):
    return ap[bass.ds(b, 1)].rearrange("a p d -> (a p) d")


def load_batches(sp, body):
    body(0, 0, True, False)
    body(1, 1, False, False)
    with sp.Fori(1, B // 2) as i:
        body(0, i * 2, False, False)
        body(1, i * 2 + 1, False, False)


L0_X = dict(wq="L0_xattn_wq", wk="L0_xattn_wk", wv="L0_xattn_wv", wo="L0_xattn_wo", bo="L0_xattn_bo")
L2_X = dict(wq="L2_xattn_Wq", wk="L2_xattn_Wk", wv="L2_xattn_Wv", wo="L2_xattn_Wo", bo="L2_xattn_bo",
            bq="L2_xattn_bq", bk="L2_xattn_bk", bv="L2_xattn_bv")
L0_MASK = dict(compare=0.0, times=-1e10, op=ALU.is_equal, diag=1.0)
L2_MASK = dict(compare=1.0, times=800.0, op=ALU.subtract, diag=100.0)


def depth_routed_block(core):
    nc, ins = core.nc, core.ins
    tag = "L0f"
    H, HD = 16, 16
    KEEP = 15
    SLOTS = 16
    G = 2
    F = 1024
    FT = F // P
    XW = D + 2
    OFF = -1e30
    TWO_PI = 2 * np.pi
    with ExitStack() as ctx:
        sb = core.sbuf_in(ctx)
        router_w = sb("router_w", [P, KT])
        router_b = sb("router_b", [P, 1])
        ln1 = sb("ln1", [P, D])
        ln2 = sb("ln2", [P, D])
        w4 = sb("L0f_w4", [P, 4, KT, D])
        w1 = sb("L0f_w1", [P, KT, F])
        w2 = sb("L0f_w2", [P, FT, D])
        attn_mask = sb("attn_mask", [P, 4, P])
        pos_in = sb("pos_in", [P, 4], I32)
        pos = sb("pos", [P, B])
        temps = sb("L0f_temps", [P, 4, B])
        column = sb("L0f_column", [P, P])
        earlier = sb("earlier", [P, P])
        first_slot = sb("first_slot", [P, B])
        apart = sb("apart", [P, P])
        weight = sb("weight", [P, B])
        above = sb("above", [P, B])
        equal = sb("equal", [P, B])
        at_least = sb("at_least", [P, B])
        slot = sb("slot", [P, B])
        unchosen = sb("unchosen", [P, B])
        xn = [sb(f"L0f_xn{j}", [P, D]) for j in range(2)]
        xT = [sb(f"L0f_xT{j}", [P, D]) for j in range(2)]
        x_aug = [sb(f"x_aug{j}", [P, XW]) for j in range(2)]
        spread = [sb(f"spread{j}", [P, P]) for j in range(2)]
        junk = [sb(f"L0f_junk{j}", [P, P]) for j in range(3)]
        pick = [sb(f"pick{j}", [P, P]) for j in range(2)]
        masked = [sb(f"masked{j}", [P, P]) for j in range(2)]
        zero_row = sb("zero_row", [1, XW])
        chosen = sb("chosen", [P, G, XW])
        mask = sb("L0f_mask", [P, G, P])
        result = sb("L0f_result", [P, G, D])
        bank = core.banks_in(ctx, tag)
        s = core.sems_in(tag, NORM_SEMS + [
            "router", "weights", "small", "consts", "xn", "T", "T_out", "w", "w_out", "spread", "row", "counted",
            "step", "aug", "pick", "U", "U_out", "gathered", "mask_in"])
        phases = Phases(nc)

        block = phases.open()

        @block.sync
        def _(sp):
            sp.dma_start(router_w[:, :], ins["L0_ffn_router_w"].rearrange("(k p) a -> p (k a)", p=P),
                         allow_slow_non_contiguous=True).then_inc(s["router"], 16)
            sp.dma_start(router_b[:, :], ins["L0_ffn_router_b"].rearrange("(a n) -> a n", a=1).to_broadcast([P, 1])
                         ).then_inc(s["router"], 16)
            sp.dma_start(pos_in[:, :], ins["L0_ffn_position_ids"][:, 0:P].rearrange("b s -> s b"),
                         allow_slow_non_contiguous=True).then_inc(s["router"], 16)
            sp.dma_start(attn_mask[:, :, :], ins["L0_ffn_attention_mask"][:, 0, 0:P, 0:P].rearrange("b q k -> q b k")
                         ).then_inc(s["mask_in"], 16)
            for n, name in enumerate(("wq", "wk", "wv", "wo")):
                sp.dma_start(w4[:, n, :, :], ins[f"L0_ffn_{name}"].rearrange("(k p) n -> p k n", p=P)
                             ).then_inc(s["weights"], 16)
            sp.dma_start(w1[:, :, :], ins["L0_ffn_w1"].rearrange("(k p) n -> p k n", p=P)).then_inc(s["weights"], 16)
            sp.dma_start(w2[:, :, :], ins["L0_ffn_w2"].rearrange("(k p) n -> p k n", p=P)).then_inc(s["weights"], 16)
            for name, dst in (("ln1", ln1), ("ln2", ln2)):
                sp.dma_start(dst[:, :], ins[f"L0_ffn_{name}"].rearrange("(a n) -> a n", a=1).to_broadcast([P, D])
                             ).then_inc(s["weights"], 16)
            sp.wait_ge(s["weights"], 16 * 8)

        @block.gpsimd
        def _(pool):
            nc.gpsimd.iota(column[:, :], [[1, P]], 0, 0, allow_small_or_imprecise_dtypes=True).then_inc(s["consts"], 1)
            nc.gpsimd.memset(zero_row[:, :], 0.0).then_inc(s["consts"], 1)
            nc.gpsimd.iota(first_slot[:, :], [[0, G], [SLOTS, B // G]], 0, 0, allow_small_or_imprecise_dtypes=True
                           ).then_inc(s["consts"], 1)
            nc.gpsimd.memset(earlier[:, :], 1.0).then_inc(s["small"], 1)
            nc.gpsimd.memset(apart[:, :], 0.0).then_inc(s["small"], 1)
            pool.wait_ge(s["small"], 2)
            nc.gpsimd.affine_select(out=earlier[:, :], in_=earlier[:, :], compare_op=ALU.is_gt, fill=0.0, base=0,
                                    pattern=[[-1, P]], channel_multiplier=1).then_inc(s["consts"], 1)
            blocks = apart[:, :].rearrange("p (k c) -> p k c", c=SLOTS)
            nc.gpsimd.affine_select(out=blocks, in_=blocks, compare_op=ALU.is_ge, fill=OFF, base=0,
                                    pattern=[[-SLOTS, P // SLOTS], [0, SLOTS]], channel_multiplier=1
                                    ).then_inc(s["small"], 1)
            pool.wait_ge(s["small"], 3)
            nc.gpsimd.affine_select(out=blocks, in_=blocks, compare_op=ALU.is_ge, fill=OFF, base=SLOTS - 1,
                                    pattern=[[SLOTS, P // SLOTS], [0, SLOTS]], channel_multiplier=-1
                                    ).then_inc(s["small"], 1)
            pool.wait_ge(s["small"], 4)
            nc.gpsimd.memset(blocks[:, :, KEEP], OFF).then_inc(s["consts"], 1)

        @block.tensor
        def _(pe):
            def transposed(j, b):
                pe.wait_ge(s["xn"], b + 1)
                after(pe, s["T_out"], b - 1)
                for k in range(KT):
                    t = nc.tensor.transpose(bank[j][:, k * P:(k + 1) * P], xn[j][:, k * P:(k + 1) * P],
                                            core.ident[:, :])
                t.then_inc(s["T"], 1)

            def route(j, b, first, last):
                if not last:
                    transposed(1 - j, b + 1)
                pe.wait_ge(s["T_out"], b + 1)
                after(pe, s["w_out"], b - 1)
                for k in range(KT):
                    t = nc.tensor.matmul(bank[2 + j][:, 0:1], xT[j][:, k * P:(k + 1) * P], router_w[:, k:k + 1],
                                         start=(k == 0), stop=(k == KT - 1))
                t.then_inc(s["w"], 1)

            def row(j, b, first, last):
                pe.wait_ge(s["spread"], b + 1)
                after(pe, s["counted"], b - 1)
                nc.tensor.matmul(bank[j][:, 0:P], core.ones[:, :], spread[j][:, :], start=True, stop=True
                                 ).then_inc(s["row"], 1)

            def gather(j, b, m, tile):
                pe.wait_ge(s["pick"], b + 1)
                after(pe, s["U_out"], b - 1)
                nc.tensor.matmul(bank[j][:, 0:P], attn_mask[:, m, :], pick[j][:, :], start=True, stop=True
                                 ).then_inc(s["U"], 1)
                pe.wait_ge(s["aug"], b + 1)
                nc.tensor.matmul(bank[4 + tile][:, 0:XW], pick[j][:, :], x_aug[j][:, :], start=False, stop=False)
                pe.wait_ge(s["U_out"], b + 1)
                nc.tensor.matmul(bank[6 + tile][:, 0:P], masked[j][:, :], pick[j][:, :], start=False, stop=False
                                 ).then_inc(s["gathered"], 1)

            def zero(tile, start, stop):
                nc.tensor.matmul(bank[4 + tile][:, 0:XW], zero_row[0:1, 0:P], zero_row[0:1, :],
                                 start=start, stop=stop)
                nc.tensor.matmul(bank[6 + tile][:, 0:P], zero_row[0:1, 0:P], zero_row[0:1, 0:P],
                                 start=start, stop=stop)

            pe.wait_ge(s["router"], 48)
            pe.wait_ge(s["consts"], 5)
            transposed(0, 0)
            over_batches(pe, route)
            over_batches(pe, row)
            pe.wait_ge(s["mask_in"], 16)
            for tile in range(G):
                zero(tile, True, False)
            for b in range(4):
                gather(b % 2, b, b, 0)
            with pe.Fori(2, 4) as i:
                for j in range(2):
                    gather(j, i * 2 + j, 3, 0)
            with pe.Fori(4, 8) as i:
                for j in range(2):
                    gather(j, i * 2 + j, 3, 1)
            for tile in range(G):
                zero(tile, False, True)

        @block.scalar
        def _(act):
            def take_T(j, b, first, last):
                act.wait_ge(s["T"], b + 1)
                after(act, s["w"], b - 1)
                nc.scalar.copy(xT[j][:, :], bank[j][:, 0:D]).then_inc(s["T_out"], 1)

            def take_U(j, b, first, last):
                act.wait_ge(s["U"], b + 1)
                after(act, s["gathered"], b - 1)
                nc.scalar.copy(masked[j][:, :], bank[j][:, 0:P]).then_inc(s["U_out"], 1)

            finish_norm_scalar(core, act, s, temps)
            over_batches(act, take_T)
            over_batches(act, take_U)

        @block.vector
        def _(dve):
            def norm(j, b):
                after(dve, s["T"], b - 1)
                normalise(core, xn[j][:, :], b).then_inc(s["xn"], 1)

            def route(j, b, first, last):
                if not two_left(b):
                    norm(j, b + 2)
                dve.wait_ge(s["w"], b + 1)
                nc.vector.tensor_tensor(cols(weight, b, 1), bank[2 + j][:, 0:1], router_b[:, :], ALU.add
                                        ).then_inc(s["w_out"], 1)

            def diagonal(j, b):
                after(dve, s["row"], b - 1)
                nc.vector.tensor_scalar(spread[j][:, :], core.ident[:, :], cols(weight, b, 1), None, ALU.mult
                                        ).then_inc(s["spread"], 1)

            def count(j, b, first, last):
                if not last:
                    diagonal(1 - j, b + 1)
                dve.wait_ge(s["row"], b + 1)
                src = bank[j][:, 0:P]
                after(dve, s["counted"], b)
                nc.vector.tensor_scalar(junk[0][:, :], src, cols(weight, b, 1), 0.0, ALU.is_gt, ALU.add,
                                        accum_out=cols(above, b, 1))
                nc.vector.scalar_tensor_tensor(junk[1][:, :], src, cols(weight, b, 1), earlier[:, :],
                                               ALU.is_equal, ALU.mult, accum_out=cols(equal, b, 1))
                nc.vector.tensor_scalar(junk[2][:, :], src, cols(weight, b, 1), 0.0, ALU.is_ge, ALU.add,
                                        accum_out=cols(at_least, b, 1)).then_inc(s["counted"], 1)

            def pick_tokens(j, b, first, last):
                after(dve, s["gathered"], b - 1)
                nc.vector.tensor_scalar(pick[j][:, :], column[:, :], cols(slot, b, 1), None, ALU.is_equal
                                        ).then_inc(s["pick"], 1)
                nc.vector.tensor_copy(x_aug[j][:, D:D + 1], cols(pos, b, 1))
                nc.vector.tensor_copy(x_aug[j][:, D + 1:D + 2], cols(weight, b, 1))
                normalise(core, x_aug[j][:, 0:D], b).then_inc(s["aug"], 1)

            finish_norm_vector(core, dve, s, temps)
            dve.wait_ge(s["router"], 48)
            dve.wait_ge(s["consts"], 5)
            norm(0, 0)
            norm(1, 1)
            over_batches(dve, route)
            dve.wait_ge(s["w_out"], B)
            diagonal(0, 0)
            over_batches(dve, count)
            dve.wait_ge(s["counted"], B)
            link = chain(dve, s["step"], 0)
            link(nc.vector.tensor_copy(pos[:, 0:4], pos_in[:, :]))
            link(nc.vector.tensor_copy(pos[:, 4:B], pos[:, 3:4].to_broadcast([P, B - 4])))
            link(nc.vector.tensor_tensor(slot[:, :], above[:, :], equal[:, :], ALU.add))
            link(nc.vector.tensor_scalar(equal[:, :], slot[:, :], float(KEEP), 1000.0, ALU.is_ge, ALU.mult))
            link(nc.vector.tensor_tensor(slot[:, :], slot[:, :], equal[:, :], ALU.add))
            link(nc.vector.tensor_tensor(slot[:, :], slot[:, :], first_slot[:, :], ALU.add))
            link(nc.vector.tensor_scalar(unchosen[:, :], at_least[:, :], float(KEEP), None, ALU.is_gt))
            over_batches(dve, pick_tokens)

        t1 = core.sems_in("L0t", [
            "zeros", "chosen", "sq", "ss", "root", "inv", "hn", "hT", "hT_out", "qkv", "v_out", "angle", "sin",
            "rope", "spread_q", "qkT", "qkT_out", "scores", "masked", "exped", "pT", "pT_out", "pv", "normed", "oT",
            "oT_out", "o", "x1", "up", "gelu", "down", "step"])
        freq = sb("freq", [P, HD // 2])
        ang = sb("ang", [P, G, 2, HD // 2])
        turns = sb("turns", [P, G, 2, HD // 2])
        sincos = sb("sincos", [P, G, 2, HD // 2])
        ss = sb("ss", [P, 4, G])
        hn = sb("hn", [P, G, D])
        hT = sb("hT", [P, G, KT, P])
        rot = [sb(f"rot{i}", [P, 2 * D]) for i in range(2)]
        qk = sb("qk", [P, G, 2 * D])
        q_eo = sb("q_eo", [P, G, 2, D])
        v1 = sb("L0f_v1", [P, G, H, HD + 1])
        qT = sb("L0f_qT", [P, G, 4, P])
        kT = sb("L0f_kT", [P, G, KT, P])
        top = sb("L0f_top", [P, 2, 4])
        shifted = [sb(f"L0f_shifted{j}", [P, 4, P]) for j in range(2)]
        probs = [sb(f"L0f_probs{j}", [P, 4, P]) for j in range(2)]
        probsT = [sb(f"L0f_probsT{j}", [P, 4, P]) for j in range(2)]
        inv_sum = sb("L0f_inv", [P, 2, 4])
        heads = sb("L0f_heads", [P, G, D])
        x1 = sb("x1", [P, G, D])
        hid = sb("hid", [P, FT, G * P])
        inv_freq = [float(np.float32(1.0) / np.float32(10000.0) ** (np.float32(2 * i) / np.float32(HD)))
                    for i in range(HD // 2)]

        block = phases.open()

        @block.gpsimd
        def _(pool):
            nc.gpsimd.memset(q_eo[:, :, :, :], 0.0).then_inc(t1["zeros"], 1)
            for g in range(G):
                nc.gpsimd.memset(v1[:, g, :, HD], 1.0).then_inc(t1["zeros"], 1)
            for i, f in enumerate(inv_freq):
                nc.gpsimd.memset(freq[:, i:i + 1], f).then_inc(t1["zeros"], 1)

        def head_at(h):
            i, odd = h // 2, h % 2
            return 2 * odd + i // 4, i // 4, slice(32 * (i % 4), 32 * (i % 4) + 32)

        @block.tensor
        def _(pe):
            def transpose_rows(src, n):
                for g in range(G):
                    for k in range(KT):
                        t = nc.tensor.transpose(bank[0][:, (g * KT + k) * P:(g * KT + k + 1) * P],
                                                src[:, g, k * P:(k + 1) * P], core.ident[:, :])
                t.then_inc(t1["hT"], 1)

            pe.wait_ge(t1["hn"], 1)
            transpose_rows(hn, 0)
            pe.wait_ge(t1["hT_out"], 1)
            for g in range(G):
                for n in range(3):
                    dst = bank[1 + g][:, n * D:(n + 1) * D] if n < 2 else bank[3][:, g * D:(g + 1) * D]
                    for k in range(KT):
                        t = nc.tensor.matmul(dst, hT[:, g, k, :], w4[:, n, k, :], start=(k == 0), stop=(k == KT - 1))
            t.then_inc(t1["qkv"], 1)
            pe.wait_ge(t1["spread_q"], 1)
            for g in range(G):
                after(pe, t1["qkT_out"], 2 * g)
                for i in range(4):
                    nc.tensor.transpose(bank[4][:, i * P:(i + 1) * P],
                                        q_eo[:, g, i // 2, (i % 2) * P:(i % 2 + 1) * P], core.ident[:, :])
                for k in range(KT):
                    t = nc.tensor.transpose(bank[5][:, k * P:(k + 1) * P],
                                            qk[:, g, D + k * P:D + (k + 1) * P], core.ident[:, :])
                t.then_inc(t1["qkT"], 1)
            pe.wait_ge(t1["qkT_out"], 4)
            pe.wait_ge(t1["v_out"], 1)

            def scores(u):
                g, r = u // 4, u % 4
                after(pe, t1["masked"], u - 1)
                for i in range(4):
                    tq, tk, rows = head_at(2 * r + 8 * (i // 2) + i % 2)
                    t = nc.tensor.matmul(bank[6 + u % 2][:, i * P:(i + 1) * P], qT[rows, g, tq, :], kT[rows, g, tk, :],
                                         start=True, stop=True)
                t.then_inc(t1["scores"], 1)

            scores(0)
            for u in range(8):
                g, r = u // 4, u % 4
                if u < 7:
                    scores(u + 1)
                pe.wait_ge(t1["exped"], u + 1)
                after(pe, t1["pT_out"], u - 1)
                for i in range(4):
                    t = nc.tensor.transpose(bank[4 + u % 2][:, i * P:(i + 1) * P], probs[u % 2][:, i, :],
                                            core.ident[:, :])
                t.then_inc(t1["pT"], 1)
                pe.wait_ge(t1["pT_out"], u + 1)
                after(pe, t1["normed"], u)
                for i in range(4):
                    t = nc.tensor.matmul(bank[1][:, i * (HD + 1):(i + 1) * (HD + 1)], probsT[u % 2][:, i, :],
                                         v1[:, g, 2 * r + 8 * (i // 2) + i % 2, :], start=True, stop=True)
                t.then_inc(t1["pv"], 1)
            pe.wait_ge(t1["normed"], 8)
            transpose_rows(heads, 1)
            pe.wait_ge(t1["hT_out"], 2)
            for g in range(G):
                for k in range(KT):
                    t = nc.tensor.matmul(bank[2][:, g * D:(g + 1) * D], hT[:, g, k, :], w4[:, 3, k, :],
                                         start=(k == 0), stop=(k == KT - 1))
            t.then_inc(t1["o"], 1)
            pe.wait_ge(t1["hn"], 2)
            transpose_rows(hn, 2)
            pe.wait_ge(t1["hT_out"], 3)
            for m in range(FT):
                for k in range(KT):
                    t = nc.tensor.matmul(bank[4 + m // 2][:, (m % 2) * G * P:(m % 2 + 1) * G * P]
                                         .rearrange("p (g c) -> p g c", g=G), w1[:, k, m * P:(m + 1) * P],
                                         hT[:, :, k, :], start=(k == 0), stop=(k == KT - 1))
                if m % 2:
                    t.then_inc(t1["up"], 1)
            pe.wait_ge(t1["gelu"], 4)
            for g in range(G):
                for m in range(FT):
                    t = nc.tensor.matmul(bank[3][:, g * D:(g + 1) * D], hid[:, m, g * P:(g + 1) * P], w2[:, m, :],
                                         start=(m == 0), stop=(m == FT - 1))
            t.then_inc(t1["down"], 1)

        @block.scalar
        def _(act):
            def square(src, n):
                for g in range(G):
                    t = nc.scalar.activation(hn[:, g, :], src[:, g, 0:D], ACT.Square, accum_out=ss[:, 0, g:g + 1])
                t.then_inc(t1["sq"], 1)
                act.wait_ge(t1["ss"], n + 1)
                nc.scalar.activation(ss[:, 2, :], ss[:, 1, :], ACT.Sqrt).then_inc(t1["root"], 1)

            def take_hT(n):
                act.wait_ge(t1["hT"], n + 1)
                nc.scalar.copy(hT[:, :, :, :].rearrange("p g k c -> p (g k c)"), bank[0][:, :]
                               ).then_inc(t1["hT_out"], 1)

            act.wait_ge(t1["chosen"], 1)
            square(chosen, 0)
            act.wait_ge(t1["angle"], 1)
            nc.scalar.activation(sincos[:, :, :, :].rearrange("p g t i -> p (g t i)"),
                                 ang[:, :, :, :].rearrange("p g t i -> p (g t i)"), ACT.Sin).then_inc(t1["sin"], 1)
            take_hT(0)
            act.wait_ge(t1["qkv"], 1)
            act.wait_ge(t1["zeros"], 3)
            for g in range(G):
                t = nc.scalar.copy(v1[:, g, :, 0:HD], bank[3][:, g * D:(g + 1) * D].rearrange("p (h c) -> p h c", c=HD))
            t.then_inc(t1["v_out"], 1)
            act.wait_ge(t1["rope"], 2)
            act.wait_ge(t1["zeros"], 1)
            for g in range(G):
                for odd in range(2):
                    dst = q_eo[:, g, odd, :].rearrange("p (i o c) -> p i o c", o=2, c=HD)
                    src = qk[:, g, 0:D].rearrange("p (i o c) -> p i o c", o=2, c=HD)
                    t = nc.scalar.copy(dst[:, :, odd, :], src[:, :, odd, :])
            t.then_inc(t1["spread_q"], 1)
            for g in range(G):
                act.wait_ge(t1["qkT"], g + 1)
                nc.scalar.copy(qT[:, g, :, :].rearrange("p t c -> p (t c)"), bank[4][:, :]).then_inc(t1["qkT_out"], 1)
                nc.scalar.copy(kT[:, g, :, :].rearrange("p t c -> p (t c)"), bank[5][:, 0:D]).then_inc(t1["qkT_out"], 1)

            def exp(u):
                act.wait_ge(t1["masked"], u + 1)
                after(act, t1["pT"], u - 1)
                nc.scalar.activation(probs[u % 2][:, :, :], shifted[u % 2][:, :, :], ACT.Exp).then_inc(t1["exped"], 1)

            exp(0)
            for u in range(8):
                if u < 7:
                    exp(u + 1)
                act.wait_ge(t1["pT"], u + 1)
                after(act, t1["pv"], u - 1)
                nc.scalar.copy(probsT[u % 2][:, :, :].rearrange("p h c -> p (h c)"), bank[4 + u % 2][:, :]
                               ).then_inc(t1["pT_out"], 1)
            take_hT(1)
            act.wait_ge(t1["x1"], 1)
            square(x1, 1)
            take_hT(2)
            for m in range(FT // 2):
                act.wait_ge(t1["up"], m + 1)
                nc.scalar.activation(hid[:, 2 * m:2 * m + 2, :].rearrange("p m c -> p (m c)"), bank[4 + m][:, :],
                                     ACT.Gelu_apprx_tanh).then_inc(t1["gelu"], 1)

        @block.vector
        def _(dve):
            link = chain(dve, t1["step"], 0)

            def rms(src, ln, n):
                dve.wait_ge(t1["sq"], n + 1)
                nc.vector.tensor_scalar(ss[:, 1, :], ss[:, 0, :], 1.0 / D, 1e-6, ALU.mult, ALU.add
                                        ).then_inc(t1["ss"], 1)
                dve.wait_ge(t1["root"], n + 1)
                link(nc.vector.reciprocal(ss[:, 3, :], ss[:, 2, :]))
                for g in range(G):
                    t = nc.vector.scalar_tensor_tensor(hn[:, g, :], src[:, g, 0:D], ss[:, 3, g:g + 1], ln[:, :],
                                                       ALU.mult, ALU.mult)
                t.then_inc(t1["hn"], 1)

            for g in range(G):
                t = nc.vector.tensor_copy(chosen[:, g, :], bank[4 + g][:, 0:XW])
            t.then_inc(t1["chosen"], 1)
            for g in range(G):
                nc.vector.tensor_tensor(mask[:, g, :], bank[6 + g][:, 0:P], apart[:, :], ALU.add)
            dve.wait_ge(t1["chosen"], 1)
            dve.wait_ge(t1["zeros"], 11)
            for g in range(G):
                link(nc.vector.tensor_scalar(ang[:, g, 0, :], freq[:, :], chosen[:, g, D:D + 1], None, ALU.mult))
            turn_hi = 6.28125
            turn_mid = float(np.float32(np.floor((TWO_PI - turn_hi) * 2.0 ** 21) / 2.0 ** 21))
            turn_lo = float(np.float32(TWO_PI - turn_hi - turn_mid))
            link(nc.vector.tensor_scalar(turns[:, :, 0, :], ang[:, :, 0, :], 1.0 / TWO_PI, MAGIC, ALU.mult, ALU.add))
            link(nc.vector.tensor_scalar(turns[:, :, 0, :], turns[:, :, 0, :], -MAGIC, None, ALU.add))
            link(nc.vector.tensor_scalar(turns[:, :, 1, :], ang[:, :, 0, :], 1.0 / TWO_PI, 0.25, ALU.mult, ALU.add))
            link(nc.vector.tensor_scalar(turns[:, :, 1, :], turns[:, :, 1, :], MAGIC, None, ALU.add))
            link(nc.vector.tensor_scalar(turns[:, :, 1, :], turns[:, :, 1, :], -MAGIC, None, ALU.add))
            link(nc.vector.tensor_copy(ang[:, :, 1, :], ang[:, :, 0, :]))
            ang2 = ang[:, :, :, :].rearrange("p g t i -> p (g t i)")
            turns2 = turns[:, :, :, :].rearrange("p g t i -> p (g t i)")
            for part in (turn_hi, turn_mid, turn_lo):
                link(nc.vector.scalar_tensor_tensor(ang2, turns2, -part, ang2, ALU.mult, ALU.add))
            link(nc.vector.tensor_scalar(ang[:, :, 1, :], ang[:, :, 1, :], float(np.pi / 2), None, ALU.add))
            link(nc.vector.tensor_scalar(ang2, ang2, -3.14159, 3.14159, ALU.max, ALU.min))
            dve.sem_inc(t1["angle"], 1)
            rms(chosen, ln1, 0)
            dve.wait_ge(t1["qkv"], 1)
            dve.wait_ge(t1["sin"], 1)
            HH = HD // 2
            for g in range(G):
                src = bank[1 + g][:, :].rearrange("p (h t i) -> p h t i", t=2, i=HH)
                dst = qk[:, g, :].rearrange("p (h t i) -> p h t i", t=2, i=HH)
                a = rot[0][:, :].rearrange("p (t h i) -> p t h i", t=2, i=HH)
                c = rot[1][:, :].rearrange("p (t h i) -> p t h i", t=2, i=HH)
                sin = sincos[:, g, 0, None, :].to_broadcast([P, 2 * H, HH])
                cos = sincos[:, g, 1, None, :].to_broadcast([P, 2 * H, HH])
                for t in range(2):
                    nc.vector.tensor_tensor(a[:, t], src[:, :, t, :], cos, ALU.mult)
                    link(nc.vector.tensor_tensor(c[:, t], src[:, :, 1 - t, :], sin, ALU.mult))
                nc.vector.tensor_tensor(dst[:, :, 0, :], a[:, 0], c[:, 0], ALU.subtract)
                link(nc.vector.tensor_tensor(dst[:, :, 1, :], a[:, 1], c[:, 1], ALU.add))
                dve.sem_inc(t1["rope"], 1)

            def shift(u):
                g, j = u // 4, u % 2
                src = bank[6 + j][:, :].rearrange("p (h k) -> p h k", h=4)
                dve.wait_ge(t1["scores"], u + 1)
                after(dve, t1["exped"], u - 1)
                link(nc.vector.scalar_tensor_tensor(shifted[j][:, :, :], src, HD ** -0.5,
                                                    mask[:, g, None, :].to_broadcast([P, 4, P]), ALU.mult, ALU.add))
                link(nc.vector.tensor_reduce(top[:, j, :], shifted[j][:, :, :], AX.X, ALU.max))
                nc.vector.tensor_tensor(shifted[j][:, :, :], shifted[j][:, :, :],
                                        top[:, j, :][:, :, None].to_broadcast([P, 4, P]), ALU.subtract
                                        ).then_inc(t1["masked"], 1)

            shift(0)
            for u in range(8):
                g, r = u // 4, u % 4
                if u < 7:
                    shift(u + 1)
                dve.wait_ge(t1["pv"], u + 1)
                src = bank[1][:, 0:4 * (HD + 1)].rearrange("p (h c) -> p h c", h=4)
                src4 = bank[1][:, 0:4 * (HD + 1)].rearrange("p (a o c) -> p a o c", a=2, o=2)
                link(nc.vector.reciprocal(inv_sum[:, u % 2, :], src[:, :, HD]))
                inv4 = inv_sum[:, u % 2, :].rearrange("p (a o) -> p a o", a=2)
                dst = heads[:, g, :].rearrange("p (a r o c) -> p r a o c", a=2, r=4, o=2)[:, r]
                nc.vector.tensor_tensor(dst, src4[:, :, :, 0:HD],
                                        inv4[:, :, :, None].to_broadcast([P, 2, 2, HD]), ALU.mult
                                        ).then_inc(t1["normed"], 1)
            dve.wait_ge(t1["o"], 1)
            for g in range(G):
                t = nc.vector.tensor_tensor(x1[:, g, :], chosen[:, g, 0:D], bank[2][:, g * D:(g + 1) * D], ALU.add)
            t.then_inc(t1["x1"], 1)
            dve.wait_ge(t1["x1"], 1)
            rms(x1, ln2, 1)
            dve.wait_ge(t1["down"], 1)
            for g in range(G):
                link(nc.vector.tensor_tensor(x1[:, g, :], x1[:, g, :], bank[3][:, g * D:(g + 1) * D], ALU.add))
                nc.vector.tensor_scalar(result[:, g, :], x1[:, g, :], chosen[:, g, D + 1:D + 2], None, ALU.mult)

        q = core.sems_in("L0b", ["pick", "xn", "pickT", "pickT_out", "out", "mixed", "updated"])
        pickT = masked
        block = phases.open()

        @block.tensor
        def _(pe):
            def transposed(j, b):
                pe.wait_ge(q["pick"], b + 1)
                after(pe, q["pickT_out"], b - 1)
                nc.tensor.transpose(bank[j][:, 0:P], pick[j][:, :], core.ident[:, :]).then_inc(q["pickT"], 1)

            def scatter(j, b, tile):
                pe.wait_ge(q["pickT_out"], b + 1)
                after(pe, q["mixed"], b - 1)
                nc.tensor.matmul(bank[2 + j][:, 0:D], pickT[j][:, :], result[:, tile, :], start=True, stop=True
                                 ).then_inc(q["out"], 1)

            def pair(i, tile, more=True):
                transposed(1, i * 2 + 1)
                scatter(0, i * 2, tile)
                if more:
                    transposed(0, i * 2 + 2)
                scatter(1, i * 2 + 1, tile)

            transposed(0, 0)
            pair(0, 0)
            with pe.Fori(1, 4) as i:
                pair(i, 0)
            with pe.Fori(4, 7) as i:
                pair(i, 1)
            pair(7, 1, False)

        @block.scalar
        def _(act):
            def body(j, b, first, last):
                act.wait_ge(q["pickT"], b + 1)
                after(act, q["out"], b - 1)
                nc.scalar.copy(pickT[j][:, :], bank[j][:, 0:P]).then_inc(q["pickT_out"], 1)

            over_batches(act, body)

        @block.vector
        def _(dve):
            def front(j, b):
                after(dve, q["pickT"], b - 1)
                after(dve, q["mixed"], b - 1)
                nc.vector.tensor_scalar(pick[j][:, :], column[:, :], cols(slot, b, 1), None, ALU.is_equal
                                        ).then_inc(q["pick"], 1)
                normalise(core, xn[j][:, :], b).then_inc(q["xn"], 1)

            def body(j, b, first, last):
                if not last:
                    front(1 - j, b + 1)
                dve.wait_ge(q["out"], b + 1)
                dve.wait_ge(q["xn"], b + 1)
                nc.vector.scalar_tensor_tensor(xT[j][:, :], xn[j][:, :], cols(unchosen, b, 1), bank[2 + j][:, 0:D],
                                               ALU.mult, ALU.add).then_inc(q["mixed"], 1)
                dve.wait_ge(q["mixed"], b + 1)
                nc.vector.scalar_tensor_tensor(cols(core.x, b * D, D), xT[j][:, :], core.gate(0, 1),
                                               cols(core.x, b * D, D), ALU.mult, ALU.add).then_inc(q["updated"], 1)
                dve.wait_ge(q["updated"], b + 1)
                take_stats(core, b)

            front(0, 0)
            over_batches(dve, body)

        phases.close()


def bidirectional_attention(core, ahead):
    nc, ins = core.nc, core.ins
    tag = "L1x"
    with ExitStack() as ctx:
        sb = core.sbuf_in(ctx)
        w_sim = sb("w_sim", [P, 3, KT])
        b_sim = sb("b_sim", [P, 1])
        w_qv = sb("w_qv", [P, 4 * KT, D])
        b_qv = sb("b_qv", [1, D])
        temps = sb("L1x_temps", [P, 4, B])
        neg_max = sb("neg_max", [P, B])
        hT_all = sb("hT_all", [P, B * D])
        ctx_in = [sb(f"L1x_ctx{j}", [P, D]) for j in range(4)]
        xn = [sb(f"L1x_xn{j}", [P, D]) for j in range(2)]
        xcT = [sb(f"L1x_xcT{j}", [P, 2 * KT, P]) for j in range(2)]
        xw = [sb(f"xw{j}", [P, KT, P]) for j in range(2)]
        raw = [sb(f"raw{j}", [P, P]) for j in range(2)]
        row_sum = [sb(f"row_sum{j}", [P, 1]) for j in range(2)]
        inv_row = [sb(f"inv_row{j}", [P, 1]) for j in range(2)]
        attn = [sb(f"attn{j}", [P, P]) for j in range(2)]
        attnT = [sb(f"attnT{j}", [P, P]) for j in range(2)]
        maxT = sb("maxT", [B, 4, P])
        row = sb("row", [B, 4])
        batt = sb("batt", [P, B])
        hT = [sb(f"hT{j}", [P, D]) for j in range(2)]
        xT = [sb(f"xT{j}", [P, D]) for j in range(2)]
        xh = [sb(f"xh{j}", [P, D]) for j in range(2)]
        c_col = [sb(f"c_col{j}", [P, KT]) for j in range(2)]
        w_xc = [sb(f"w_xc{j}", [P, KT, D]) for j in range(2)]
        bank = core.banks_in(ctx, tag)
        s = core.sems_in(tag, NORM_SEMS + [
            "weights", "ctx_in0", "ctx_in1", "ctx_in2", "ctx_in3", "passed", "xn", "T", "T_out", "xw", "sim",
            "neg_max", "exped", "inv",
            "attn", "attnT", "attnT_out", "h", "h_out"])

        phases = Phases(nc)
        block = phases.open()

        @block.sync
        def _(sp):
            for b in range(4):
                sp.dma_start(ctx_in[b][:, :], one(ins["ctx_1024"], b)).then_inc(s[f"ctx_in{b}"], 16)
            sp.dma_start(w_sim[:, :, :], ins["L1_xattn_w_sim"].rearrange("(w k p) -> p w k", w=3, p=P),
                         allow_slow_non_contiguous=True).then_inc(s["weights"], 16)
            sp.dma_start(b_sim[:, :], ins["L1_xattn_b_sim"].rearrange("(a n) -> a n", a=1).to_broadcast([P, 1])
                         ).then_inc(s["weights"], 16)
            sp.dma_start(w_qv[:, :, :], ins["L1_xattn_W_qv"].rearrange("(t p) n -> p t n", p=P)
                         ).then_inc(s["weights"], 16)
            sp.dma_start(b_qv[:, :], ins["L1_xattn_b_qv"].rearrange("(a n) -> a n", a=1)).then_inc(s["weights"], 16)

            def body(j, b):
                sp.wait_ge(s["h"], b - 3)
                settle(sp, s["passed"])
                sp.dma_start(ctx_in[j][:, :], one(ins["ctx_1024"], b)).then_inc(s[f"ctx_in{j}"], 16)
                ahead.part(sp, b)

            sp.wait_ge(ahead.sems["zeros"], 1)
            for b in range(4):
                ahead.part(sp, b)
            with sp.Fori(1, B // 4) as i:
                for j in range(4):
                    body(j, i * 4 + j)

        @block.gpsimd
        def _(pool):
            ahead.make_zeros()

        @block.tensor
        def _(pe):
            def transposed(j4, b):
                j = j4 % 2
                pe.wait_ge(s["xn"], b + 1)
                pe.wait_ge(s[f"ctx_in{j4}"], (b - j4) * 4 + 16)
                after(pe, s["T_out"], b - 1)
                for k in range(KT):
                    nc.tensor.transpose(bank[j][:, k * P:(k + 1) * P], xn[j][:, k * P:(k + 1) * P], core.ident[:, :])
                for k in range(KT):
                    t = nc.tensor.transpose(bank[j][:, (KT + k) * P:(KT + k + 1) * P],
                                            ctx_in[j4][:, k * P:(k + 1) * P], core.ident[:, :])
                t.then_inc(s["T"], 1)

            def similarity(j, b):
                pe.wait_ge(s["T_out"], b + 1)
                pe.wait_ge(s["xw"], b + 1)
                after(pe, s["exped"], b - 1)
                for k in range(KT):
                    nc.tensor.matmul(bank[2 + j][:, 0:P], xw[j][:, k, :], xcT[j][:, KT + k, :],
                                     start=(k == 0), stop=False)
                for k in range(KT):
                    t = nc.tensor.matmul(bank[2 + j][:, 0:P], xcT[j][:, k, :],
                                         w_sim[:, 0, k:k + 1].to_broadcast([P, P]), start=False, stop=(k == KT - 1))
                t.then_inc(s["sim"], 1)

            def attn_transposed(j, b):
                pe.wait_ge(s["attn"], b + 1)
                after(pe, s["attnT_out"], b - 1)
                nc.tensor.transpose(bank[4 + j][:, 0:P], attn[j][:, :], core.ident[:, :]).then_inc(s["attnT"], 1)

            def weighted(j4, b):
                j = j4 % 2
                pe.wait_ge(s["attnT_out"], b + 1)
                after(pe, s["h_out"], b - 1)
                for k in range(KT):
                    t = nc.tensor.matmul(bank[6 + j][:, k * P:(k + 1) * P], ctx_in[j4][:, k * P:(k + 1) * P],
                                         attnT[j][:, :], start=True, stop=True)
                t.then_inc(s["h"], 1)

            def body(j, b, first, last):
                if not two_left(b):
                    transposed((j + 2) % 4, b + 2)
                if not last:
                    similarity((j + 1) % 2, b + 1)
                attn_transposed(j % 2, b)
                weighted(j, b)

            pe.wait_ge(s["weights"], 64)
            transposed(0, 0)
            transposed(1, 1)
            similarity(0, 0)
            over_batches_by_four(pe, body)

        @block.scalar
        def _(act):
            def take_T(j, b):
                act.wait_ge(s["T"], b + 1)
                after(act, s["sim"], b - 1)
                nc.scalar.copy(xcT[j][:, :, :].rearrange("p t c -> p (t c)"), bank[j][:, :]).then_inc(s["T_out"], 1)

            def exp(j, b):
                act.wait_ge(s["neg_max"], b + 1)
                after(act, s["attn"], b - 1)
                nc.scalar.activation(raw[j][:, :], bank[2 + j][:, 0:P], ACT.Exp, bias=cols(neg_max, b, 1),
                                     accum_out=row_sum[j][:, :]).then_inc(s["exped"], 1)

            def take_attnT(j, b):
                act.wait_ge(s["attnT"], b + 1)
                after(act, s["h"], b - 1)
                nc.scalar.copy(attnT[j][:, :], bank[4 + j][:, 0:P]).then_inc(s["attnT_out"], 1)

            def take_h(j, b):
                act.wait_ge(s["h"], b + 1)
                nc.scalar.copy(cols(hT_all, b * D, D), bank[6 + j][:, 0:D]).then_inc(s["h_out"], 1)

            def body(j, b, first, last):
                exp(j, b)
                if not two_left(b):
                    take_T(j, b + 2)
                take_attnT(j, b)
                take_h(j, b)

            finish_norm_scalar(core, act, s, temps)
            take_T(0, 0)
            take_T(1, 1)
            over_batches(act, body)

        @block.vector
        def _(dve):
            def norm(j, b):
                after(dve, s["T"], b - 1)
                normalise(core, xn[j][:, :], b).then_inc(s["xn"], 1)

            def weigh(j, b):
                dve.wait_ge(s["T_out"], b + 1)
                after(dve, s["sim"], b - 1)
                for k in range(KT):
                    t = nc.vector.tensor_scalar(xw[j][:, k, :], xcT[j][:, k, :], w_sim[:, 2, k:k + 1],
                                                w_sim[:, 1, k:k + 1], ALU.mult, ALU.add)
                t.then_inc(s["xw"], 1)

            def row_max(j, b):
                dve.wait_ge(s["sim"], b + 1)
                nc.vector.tensor_reduce(cols(neg_max, b, 1), bank[2 + j][:, 0:P], AX.X, ALU.max, negate=True
                                        ).then_inc(s["neg_max"], 1)

            def normalise_rows(j, b):
                dve.wait_ge(s["exped"], b + 1)
                nc.vector.reciprocal(inv_row[j][:, :], row_sum[j][:, :]).then_inc(s["inv"], 1)
                dve.wait_ge(s["inv"], b + 1)
                after(dve, s["attnT"], b - 1)
                nc.vector.tensor_scalar(attn[j][:, :], raw[j][:, :], inv_row[j][:, :], None, ALU.mult
                                        ).then_inc(s["attn"], 1)

            def body(j, b, first, last):
                row_max(j, b)
                if not two_left(b):
                    norm(j, b + 2)
                if not last:
                    weigh(1 - j, b + 1)
                normalise_rows(j, b)

            finish_norm_vector(core, dve, s, temps)
            norm(0, 0)
            norm(1, 1)
            dve.wait_ge(s["weights"], 64)
            weigh(0, 0)
            over_batches(dve, body)

        phases.close()
        context_weights(core, neg_max=neg_max, b_sim=b_sim, maxT=maxT, row=row, batt=batt, bank=bank)
        q = core.sems_in("L1o", ["xn", "T", "T_out", "hT", "c", "w_xc", "xh", "out", "updated"])

        block2 = phases.open()

        @block2.tensor
        def _(pe):
            def front(j, b):
                pe.wait_ge(q["xn"], b + 1)
                after(pe, q["T_out"], b - 1)
                after(pe, q["c"], b - 1)
                for k in range(KT):
                    nc.tensor.transpose(bank[j][:, k * P:(k + 1) * P], xn[j][:, k * P:(k + 1) * P], core.ident[:, :])
                for k in range(KT):
                    t = nc.tensor.matmul(bank[2 + j][:, k:k + 1], xn[j][:, k * P:(k + 1) * P], cols(batt, b, 1),
                                         start=True, stop=True)
                t.then_inc(q["T"], 1)

            def project(j, b):
                pe.wait_ge(q["T_out"], b + 1)
                pe.wait_ge(q["hT"], b + 1)
                pe.wait_ge(q["w_xc"], b + 1)
                pe.wait_ge(q["xh"], b + 1)
                after(pe, q["updated"], b - 1)
                dst = bank[4 + j][:, 0:D]
                for k in range(KT):
                    cs = slice(k * P, (k + 1) * P)
                    nc.tensor.matmul(dst, xT[j][:, cs], w_xc[j][:, k, :], start=(k == 0), stop=False)
                    nc.tensor.matmul(dst, hT[j][:, cs], w_qv[:, KT + k, :], start=False, stop=False)
                    nc.tensor.matmul(dst, xh[j][:, cs], w_qv[:, 2 * KT + k, :], start=False, stop=False)
                nc.tensor.matmul(dst, core.ones[0:1, :], b_qv[0:1, :], start=False, stop=True).then_inc(q["out"], 1)

            def body(j, b, first, last):
                if not last:
                    front(1 - j, b + 1)
                project(j, b)

            front(0, 0)
            over_batches(pe, body)

        @block2.scalar
        def _(act):
            def body(j, b, first, last):
                after(act, q["out"], b - 1)
                after(act, q["xh"], b - 1)
                nc.scalar.copy(hT[j][:, :], cols(hT_all, b * D, D)).then_inc(q["hT"], 1)
                act.wait_ge(q["T"], b + 1)
                nc.scalar.copy(xT[j][:, :], bank[j][:, 0:D]).then_inc(q["T_out"], 1)

            over_batches(act, body)

        @block2.sync
        def _(sp):
            ahead.all_in(sp)

        @block2.vector
        def _(dve):
            def norm(j, b):
                after(dve, q["T"], b - 1)
                normalise(core, xn[j][:, :], b).then_inc(q["xn"], 1)

            def operands(j, b):
                dve.wait_ge(q["T"], b + 1)
                after(dve, q["out"], b - 1)
                nc.vector.tensor_copy(c_col[j][:, :], bank[2 + j][:, 0:KT]).then_inc(q["c"], 1)
                dve.wait_ge(q["T_out"], b + 1)
                dve.wait_ge(q["hT"], b + 1)
                nc.vector.tensor_tensor(xh[j][:, :], xT[j][:, :], hT[j][:, :], ALU.mult).then_inc(q["xh"], 1)
                dve.wait_ge(q["c"], b + 1)
                for k in range(KT):
                    t = nc.vector.scalar_tensor_tensor(w_xc[j][:, k, :], w_qv[:, 3 * KT + k, :], c_col[j][:, k:k + 1],
                                                       w_qv[:, k, :], ALU.mult, ALU.add)
                t.then_inc(q["w_xc"], 1)

            def update(j, b):
                dve.wait_ge(q["out"], b + 1)
                nc.vector.scalar_tensor_tensor(cols(core.x, b * D, D), bank[4 + j][:, 0:D], core.gate(1, 0),
                                               cols(core.x, b * D, D), ALU.mult, ALU.add).then_inc(q["updated"], 1)
                dve.wait_ge(q["updated"], b + 1)
                take_stats(core, b)

            def body(j, b, first, last):
                if not last:
                    operands(1 - j, b + 1)
                if not two_left(b):
                    norm(j, b + 2)
                update(j, b)

            norm(0, 0)
            norm(1, 1)
            operands(0, 0)
            over_batches(dve, body)

        phases.close()


def context_weights(core, neg_max, b_sim, maxT, row, batt, bank):
    nc = core.nc
    s = core.sems_in("L1b", ["step", "T", "max_row", "shifted", "exped", "batt", "back"])
    with nc.Block() as block:
        @block.tensor
        def _(pe):
            pe.wait_ge(s["max_row"], 1)
            nc.tensor.transpose(bank[0][0:B, 0:P], batt[:, :], core.ident[:, :]).then_inc(s["T"], 1)
            pe.wait_ge(s["batt"], 1)
            nc.tensor.transpose(bank[1][:, 0:B], maxT[:, 2, :], core.ident[0:B, 0:B]).then_inc(s["back"], 1)

        @block.scalar
        def _(act):
            act.wait_ge(s["shifted"], 1)
            nc.scalar.activation(maxT[:, 1, :], maxT[:, 0, :], ACT.Exp, accum_out=row[:, 1:2]).then_inc(s["exped"], 1)

        @block.vector
        def _(dve):
            link = chain(dve, s["step"], 0)
            nc.vector.tensor_scalar(batt[:, :], neg_max[:, :], -1.0, b_sim[:, :], ALU.mult, ALU.add
                                    ).then_inc(s["max_row"], 1)
            dve.wait_ge(s["T"], 1)
            link(nc.vector.tensor_reduce(row[:, 0:1], bank[0][0:B, 0:P], AX.X, ALU.max))
            nc.vector.tensor_scalar(maxT[:, 0, :], bank[0][0:B, 0:P], row[:, 0:1], None, ALU.subtract
                                    ).then_inc(s["shifted"], 1)
            dve.wait_ge(s["exped"], 1)
            link(nc.vector.reciprocal(row[:, 2:3], row[:, 1:2]))
            nc.vector.tensor_scalar(maxT[:, 2, :], maxT[:, 1, :], row[:, 2:3], None, ALU.mult).then_inc(s["batt"], 1)
            dve.wait_ge(s["back"], 1)
            nc.vector.tensor_copy(batt[:, :], bank[1][:, 0:B])


class TernaryWeights:

    F = 1024

    def __init__(self, core, ctx):
        self.core = core
        self.FT = self.F // P
        sb = core.sbuf_in(ctx)
        self.gate_up = sb("w_gu", [P, KT, 2, self.F], BF16)
        self.down = sb("w_down", [P, self.FT, D], BF16)
        self.mean = sb("w_mean", [P, 3])
        self.ident_bf = sb("ident_bf", [P, P], BF16)
        self.scratch = ctx.enter_context(ExitStack())
        sb = core.sbuf_in(self.scratch)
        self.raw = sb("w_raw", [P, 3, self.FT * D])
        self.tern = sb("w_tern", [P, self.FT * D], BF16)
        self.sum = sb("w_sum", [P, 3])
        self.scale = sb("w_scale", [P, 3])
        self.sems = core.sems_in("L3w", ["loaded", "ident", "summed", "total", "scale", "round", "tern", "T", "T_out"])

    def load(self, sp):
        for k, name in enumerate(("L3_ffn_w_gate", "L3_ffn_w_up", "L3_ffn_w_down")):
            sp.dma_start(self.raw[:, k, :].rearrange("p (t n) -> p t n", n=D if k < 2 else self.F),
                         self.core.ins[name].rearrange("(t p) n -> p t n", p=P)).then_inc(self.sems["loaded"], 16)

    def on_scalar(self, act, bank):
        nc, p = self.core.nc, self.sems
        nc.scalar.copy(self.ident_bf[:, :], self.core.ident[:, :]).then_inc(p["ident"], 1)
        act.wait_ge(p["loaded"], 48)
        for k in range(3):
            after(act, p["summed"], k)
            nc.scalar.activation(self.tern[:, :], self.raw[:, k, :], ACT.Abs, accum_out=self.sum[:, k:k + 1]
                                 ).then_inc(p["summed"], 1)
        for n in range(12):
            k, src = n // 4, bank[n % 4][:, :].bitcast(BF16)[:, 0:4 * P]
            act.wait_ge(p["T"], n + 1)
            if k < 2:
                t0 = 2 * (n % 4)
                dst = self.gate_up[:, :, k, t0 * P:(t0 + 2) * P].rearrange("p k (t c) -> p t k c", t=2)
                nc.scalar.copy(dst, src.rearrange("p (t k c) -> p t k c", t=2, k=KT)).then_inc(p["T_out"], 1)
            else:
                o, i0 = (n % 4) // 2, 4 * (n % 2)
                nc.scalar.copy(self.down[:, i0:i0 + 4, o * P:(o + 1) * P],
                               src.rearrange("p (i c) -> p i c", i=4)).then_inc(p["T_out"], 1)

    def on_tensor(self, pe, bank):
        nc, p = self.core.nc, self.sems
        pe.wait_ge(p["summed"], 3)
        nc.tensor.matmul(bank[4][:, 0:3], self.core.ones[:, :], self.sum[:, :], start=True, stop=True
                         ).then_inc(p["total"], 1)
        pe.wait_ge(p["ident"], 1)
        for n in range(12):
            pe.wait_ge(p["tern"], n // 4 + 1)
            after(pe, p["T_out"], n - 3)
            for i in range(4):
                m = 4 * (n % 4) + i
                t = nc.tensor.transpose(bank[n % 4][:, :].bitcast(BF16)[:, i * P:(i + 1) * P],
                                        self.tern[:, m * P:(m + 1) * P], self.ident_bf[:, :])
            t.then_inc(p["T"], 1)

    def scales(self, dve, bank):
        nc, p = self.core.nc, self.sems
        dve.wait_ge(p["total"], 1)
        nc.vector.tensor_scalar(self.mean[:, :], bank[4][:, 0:3], 1.0 / (self.F * D), 1e-5, ALU.mult, ALU.max
                                ).then_inc(p["scale"], 1)
        dve.wait_ge(p["scale"], 1)
        nc.vector.reciprocal(self.scale[:, :], self.mean[:, :]).then_inc(p["scale"], 1)

    def on_gpsimd(self, pool):
        nc, p = self.core.nc, self.sems
        pool.wait_ge(p["scale"], 2)
        for k in range(3):
            w = self.raw[:, k, :]
            nc.gpsimd.tensor_scalar(w, w, self.scale[:, k:k + 1], MAGIC, ALU.mult, ALU.add).then_inc(p["round"], 1)
            pool.wait_ge(p["round"], 2 * k + 1)
            nc.gpsimd.tensor_scalar(w, w, -MAGIC, 1.0, ALU.add, ALU.min).then_inc(p["round"], 1)
            pool.wait_ge(p["round"], 2 * k + 2)
            after(pool, p["T"], 4 * k)
            nc.gpsimd.tensor_scalar(self.tern[:, :], w, -1.0, None, ALU.max).then_inc(p["tern"], 1)


def bit_ffn(core, weights):
    nc = core.nc
    tag = "L3f"
    F, FT = weights.F, weights.FT
    w_gu, w_down, w_mean, ident_bf = weights.gate_up, weights.down, weights.mean, weights.ident_bf
    with ExitStack() as ctx:
        sb = core.sbuf_in(ctx)
        temps = sb("L3f_temps", [P, 4, B])
        bank = core.banks_in(ctx, tag)
        phases = Phases(nc)
        block_b = phases.open()
        neg_magic = sb("neg_magic", [P, 1])
        xn = [sb(f"L3f_xn{j}", [P, D]) for j in range(2)]
        amax = [sb(f"amax{j}", [P, 8]) for j in range(2)]
        x_round = [sb(f"x_round{j}", [P, D]) for j in range(2)]
        xq = [sb(f"xq{j}", [P, D], BF16) for j in range(2)]
        xqT = [sb(f"xqT{j}", [P, D], BF16) for j in range(2)]
        silu = [sb(f"silu{j}", [P, F]) for j in range(2)]
        h = [sb(f"h{j}", [P, F]) for j in range(2)]
        hq = [sb(f"hq{j}", [P, F], BF16) for j in range(2)]
        hqT = [sb(f"hqT{j}", [P, F], BF16) for j in range(2)]
        s = core.sems_in(tag, NORM_SEMS + [
            "x_step", "h_step", "neg_magic", "x_clamped", "h_clamped", "xq", "scale_x", "xqT", "xqT_out",
            "gate", "up", "silu", "gated", "hq", "hqT", "hqT_out", "down",
            "updated"])
        T_bank = bank[0][:, :].bitcast(BF16)
        H_bank = bank[1][:, :].bitcast(BF16)
        G, U, O = bank[2:4], bank[4:6], bank[6:8]

        @block_b.tensor
        def _(pe):
            def front(j, b):
                pe.wait_ge(s["xq"], b + 1)
                after(pe, s["xqT_out"], b)
                for k in range(KT):
                    t = nc.tensor.transpose(T_bank[:, k * P:(k + 1) * P], xq[j][:, k * P:(k + 1) * P],
                                            ident_bf[:, :])
                t.then_inc(s["xqT"], 1)

            def expand(j, b):
                pe.wait_ge(s["xqT_out"], b + 1)
                after(pe, s["silu"], b)
                for half in range(2):
                    for k in range(KT):
                        t = nc.tensor.matmul(G[half][:, :], xqT[j][:, k * P:(k + 1) * P],
                                             w_gu[:, k, 0, half * 512:(half + 1) * 512],
                                             start=(k == 0), stop=(k == KT - 1))
                t.then_inc(s["gate"], 1)
                after(pe, s["gated"], b)
                for half in range(2):
                    for k in range(KT):
                        t = nc.tensor.matmul(U[half][:, :], xqT[j][:, k * P:(k + 1) * P],
                                             w_gu[:, k, 1, half * 512:(half + 1) * 512],
                                             start=(k == 0), stop=(k == KT - 1))
                t.then_inc(s["up"], 1)

            def h_transposed(j, b):
                pe.wait_ge(s["hq"], b + 1)
                after(pe, s["hqT_out"], b)
                for k in range(FT):
                    t = nc.tensor.transpose(H_bank[:, k * P:(k + 1) * P], hq[j][:, k * P:(k + 1) * P],
                                            ident_bf[:, :])
                t.then_inc(s["hqT"], 1)

            def contract(j, b):
                pe.wait_ge(s["hqT_out"], b + 1)
                after(pe, s["updated"], b - 1)
                for k in range(FT):
                    t = nc.tensor.matmul(O[j][:, 0:D], hqT[j][:, k * P:(k + 1) * P], w_down[:, k, :],
                                         start=(k == 0), stop=(k == FT - 1))
                t.then_inc(s["down"], 1)

            def body(j, b, first, last):
                if not last:
                    expand(1 - j, b + 1)
                h_transposed(j, b)
                if not two_left(b):
                    front(j, b + 2)
                contract(j, b)

            front(0, 0)
            front(1, 1)
            expand(0, 0)
            over_batches(pe, body)

        @block_b.scalar
        def _(act):
            def quantised_x(j, b):
                act.wait_ge(s["x_clamped"], b + 1)
                after(act, s["xqT"], b - 1)
                nc.scalar.activation(xq[j][:, :], x_round[j][:, :], ACT.Identity, bias=neg_magic[:, :]
                                     ).then_inc(s["xq"], 1)

            def take_xqT(j, b):
                act.wait_ge(s["xqT"], b + 1)
                after(act, s["up"], b - 1)
                nc.scalar.copy(xqT[j][:, :], T_bank[:, 0:D]).then_inc(s["xqT_out"], 1)

            def silu_of_gate(j, b):
                act.wait_ge(s["gate"], b + 1)
                act.wait_ge(s["scale_x"], b + 1)
                after(act, s["gated"], b - 1)
                for half in range(2):
                    t = nc.scalar.activation(silu[j][:, half * 512:(half + 1) * 512], G[half][:, :], ACT.Silu,
                                             scale=amax[j][:, 2:3])
                t.then_inc(s["silu"], 1)

            def quantised_h(j, b):
                act.wait_ge(s["h_clamped"], b + 1)
                after(act, s["hqT"], b - 1)
                nc.scalar.activation(hq[j][:, :], h[j][:, :], ACT.Identity, bias=neg_magic[:, :]
                                     ).then_inc(s["hq"], 1)

            def take_hqT(j, b):
                act.wait_ge(s["hqT"], b + 1)
                after(act, s["down"], b - 1)
                nc.scalar.copy(hqT[j][:, :], H_bank[:, :]).then_inc(s["hqT_out"], 1)

            def body(j, b, first, last):
                if not last:
                    silu_of_gate(1 - j, b + 1)
                quantised_h(j, b)
                if not two_left(b):
                    quantised_x(j, b + 2)
                take_hqT(j, b)
                if not two_left(b):
                    take_xqT(j, b + 2)

            finish_norm_scalar(core, act, s, temps)
            act.wait_ge(s["neg_magic"], 1)
            for b in range(2):
                quantised_x(b, b)
                take_xqT(b, b)
            silu_of_gate(0, 0)
            over_batches(act, body)

        @block_b.gpsimd
        def _(pool):
            nc.gpsimd.memset(neg_magic[:, :], -MAGIC).then_inc(s["neg_magic"], 1)

        @block_b.vector
        def _(dve):
            def clamp(t):
                return nc.vector.tensor_scalar(t, t, MAGIC + 127.0, MAGIC - 128.0, ALU.min, ALU.max)

            def x_step(j, b, n):
                a = amax[j]
                if n == 0:
                    after(dve, s["xqT"], b - 1)
                    t = normalise(core, xn[j][:, :], b)
                else:
                    dve.wait_ge(s["x_step"], b * 5 + n)
                if n == 1:
                    t = nc.vector.tensor_reduce(a[:, 0:1], xn[j][:, :], AX.X, ALU.max, apply_absolute_value=True)
                if n == 2:
                    t = nc.vector.tensor_scalar(a[:, 0:1], a[:, 0:1], 1e-5, 1.0 / 127.0, ALU.max, ALU.mult)
                if n == 3:
                    t = nc.vector.reciprocal(a[:, 1:2], a[:, 0:1])
                if n == 4:
                    after(dve, s["xq"], b - 1)
                    t = nc.vector.tensor_scalar(x_round[j][:, :], xn[j][:, :], a[:, 1:2], MAGIC, ALU.mult, ALU.add)
                if n < 5:
                    t.then_inc(s["x_step"], 1)
                    return
                clamp(x_round[j][:, :]).then_inc(s["x_clamped"], 1)
                nc.vector.tensor_scalar(a[:, 2:4], w_mean[:, 0:2], a[:, 0:1], None, ALU.mult
                                        ).then_inc(s["scale_x"], 1)

            def h_step(j, b, n):
                a = amax[j]
                if n == 0:
                    dve.wait_ge(s["up"], b + 1)
                    dve.wait_ge(s["silu"], b + 1)
                    dve.wait_ge(s["scale_x"], b + 1)
                    after(dve, s["hq"], b - 1)
                    for half in range(2):
                        t = nc.vector.scalar_tensor_tensor(h[j][:, half * 512:(half + 1) * 512], U[half][:, :],
                                                           a[:, 3:4], silu[j][:, half * 512:(half + 1) * 512],
                                                           ALU.mult, ALU.mult)
                    t.then_inc(s["gated"], 1)
                    return
                if n == 1:
                    dve.wait_ge(s["gated"], b + 1)
                    t = nc.vector.tensor_reduce(a[:, 4:5], h[j][:, :], AX.X, ALU.max, apply_absolute_value=True)
                else:
                    dve.wait_ge(s["h_step"], b * 6 + n - 1)
                if n == 2:
                    t = nc.vector.tensor_scalar(a[:, 4:5], a[:, 4:5], 1e-5, 1.0 / 127.0, ALU.max, ALU.mult)
                if n == 3:
                    t = nc.vector.reciprocal(a[:, 5:6], a[:, 4:5])
                if n == 4:
                    t = nc.vector.tensor_scalar(h[j][:, :], h[j][:, :], a[:, 5:6], MAGIC, ALU.mult, ALU.add)
                if n == 5:
                    clamp(h[j][:, :]).then_inc(s["h_clamped"], 1)
                    t = nc.vector.tensor_scalar(a[:, 6:7], a[:, 4:5], w_mean[:, 2:3], None, ALU.mult)
                if n == 6:
                    t = nc.vector.tensor_scalar(a[:, 7:8], a[:, 6:7], core.gate(3, 1), None, ALU.mult)
                t.then_inc(s["h_step"], 1)

            def update(j, b):
                dve.wait_ge(s["down"], b + 1)
                dve.wait_ge(s["h_step"], b * 6 + 6)
                nc.vector.scalar_tensor_tensor(cols(core.x, b * D, D), O[j][:, 0:D], amax[j][:, 7:8],
                                               cols(core.x, b * D, D), ALU.mult, ALU.add).then_inc(s["updated"], 1)

            def body(j, b, first, last):
                for n in range(6):
                    h_step(j, b, n)
                    if not two_left(b):
                        x_step(j, b + 2, n)
                if not first:
                    update(1 - j, b - 1)
                h_step(j, b, 6)

            finish_norm_vector(core, dve, s, temps)
            for b in range(2):
                for n in range(6):
                    x_step(b, b, n)
            over_batches(dve, body)
            update(1, B - 1)

        phases.close()


def warped_alignment(core, weights):
    nc, ins = core.nc, core.ins
    tag = "L3x"
    W = P + 1
    NB = 8
    R = P // NB
    with ExitStack() as ctx:
        sb = core.sbuf_in(ctx)
        temps = sb("L3x_temps", [P, 4, B])
        dist_buf = sb("dist_buf", [P, P * P])
        dist16 = dist_buf[0:B, :]
        cost = sb("cost", [B, W * W])
        low = sb("low", [B, P])
        ctx_in = [sb(f"L3x_ctx{j}", [P, D]) for j in range(2)]
        distances = ctx.enter_context(ExitStack())
        sd = core.sbuf_in(distances)
        xn = [sd(f"L3x_xn{j}", [P, D]) for j in range(2)]
        xcT = [sd(f"L3x_xcT{j}", [P, 2 * KT, P]) for j in range(2)]
        x_neg2 = [sd(f"x_neg2{j}", [P, D]) for j in range(2)]
        x_sq = [sd(f"x_sq{j}", [P, D]) for j in range(2)]
        ctx_sq = sd("ctx_sq", [P, D])
        ctx_norm = [sd(f"ctx_norm{j}", [P, 1]) for j in range(2)]
        sq_dist = [sd(f"sq_dist{j}", [P, P]) for j in range(2)]
        dist = [sd(f"dist{j}", [P, P]) for j in range(2)]
        bank = core.banks_in(ctx, tag)
        dist_dram = nc.dram_tensor("dist_dram", (B, P, P), F32, kind="Internal").ap()
        path_dram = nc.dram_tensor("path_dram", (B, P, P), F32, kind="Internal").ap()
        s = core.sems_in(tag, NORM_SEMS + [
            "ctx_in0", "ctx_in1", "passed", "xn", "T", "T_out", "x_neg2", "x_sq", "ctx_norm", "dots", "sq_dist",
            "dist", "stored0", "stored1"])
        phases = Phases(nc)

        block = phases.open()

        @block.sync
        def _(sp):
            def body(j, b, first, last):
                if not isinstance(b, int):
                    sp.wait_ge(s["T"], b - 1)
                    settle(sp, s["passed"])
                    sp.wait_ge(s["ctx_norm"], b - 1)
                    settle(sp, s["passed"])
                sp.dma_start(ctx_in[j][:, :], one(ins["ctx_1024"], b)).then_inc(s[f"ctx_in{j}"], 16)

            load_batches(sp, body)
            weights.load(sp)

        @block.tensor
        def _(pe):
            def transposed(j, b):
                pe.wait_ge(s["xn"], b + 1)
                pe.wait_ge(s[f"ctx_in{j}"], loads(b, j))
                after(pe, s["T_out"], b - 1)
                for k in range(KT):
                    nc.tensor.transpose(bank[j][:, k * P:(k + 1) * P], xn[j][:, k * P:(k + 1) * P], core.ident[:, :])
                for k in range(KT):
                    t = nc.tensor.transpose(bank[j][:, (KT + k) * P:(KT + k + 1) * P],
                                            ctx_in[j][:, k * P:(k + 1) * P], core.ident[:, :])
                t.then_inc(s["T"], 1)

            def dots(j, b):
                pe.wait_ge(s["x_neg2"], b + 1)
                pe.wait_ge(s["x_sq"], b + 1)
                after(pe, s["sq_dist"], b - 1)
                for k in range(KT):
                    cs = slice(k * P, (k + 1) * P)
                    nc.tensor.matmul(bank[2 + j][:, 0:P], xcT[j][:, KT + k, :], x_neg2[j][:, cs],
                                     start=(k == 0), stop=False)
                for k in range(KT):
                    cs = slice(k * P, (k + 1) * P)
                    t = nc.tensor.matmul(bank[2 + j][:, 0:P], core.ones[:, :], x_sq[j][:, cs],
                                         start=False, stop=(k == KT - 1))
                t.then_inc(s["dots"], 1)

            def body(j, b, first, last):
                if not last:
                    transposed(1 - j, b + 1)
                dots(j, b)

            transposed(0, 0)
            over_batches(pe, body)

        @block.scalar
        def _(act):
            def front(j, b):
                act.wait_ge(s[f"ctx_in{j}"], loads(b, j))
                after(act, s["sq_dist"], b - 1)
                after(act, s["ctx_norm"], b)
                nc.scalar.activation(ctx_sq[:, :], ctx_in[j][:, :], ACT.Square, accum_out=ctx_norm[j][:, :]
                                     ).then_inc(s["ctx_norm"], 1)
                act.wait_ge(s["T"], b + 1)
                after(act, s["dots"], b - 1)
                nc.scalar.copy(xcT[j][:, :, :].rearrange("p t c -> p (t c)"), bank[j][:, :]).then_inc(s["T_out"], 1)
                act.wait_ge(s["T_out"], b + 1)
                nc.scalar.activation(x_sq[j][:, :], xcT[j][:, 0:KT, :].rearrange("p t c -> p (t c)"), ACT.Square
                                     ).then_inc(s["x_sq"], 1)

            def root(j, b):
                act.wait_ge(s["sq_dist"], b + 1)
                if not (isinstance(b, int) and b < 2):
                    act.wait_ge(s[f"stored{j}"], loads(b, j) - 16)
                nc.scalar.activation(dist[j][:, :], sq_dist[j][:, :], ACT.Sqrt).then_inc(s["dist"], 1)
                act.wait_ge(s["dist"], b + 1)
                act.dma_start(one(dist_dram, b), dist[j][:, :]).then_inc(s[f"stored{j}"], 16)

            def body(j, b, first, last):
                if not last:
                    front(1 - j, b + 1)
                root(j, b)

            finish_norm_scalar(core, act, s, temps)
            front(0, 0)
            over_batches(act, body)

        @block.vector
        def _(dve):
            def norm(j, b):
                after(dve, s["T"], b - 1)
                normalise(core, xn[j][:, :], b).then_inc(s["xn"], 1)

            def front(j, b):
                dve.wait_ge(s["T_out"], b + 1)
                after(dve, s["dots"], b - 1)
                nc.vector.tensor_scalar(x_neg2[j][:, :], xcT[j][:, 0:KT, :].rearrange("p t c -> p (t c)"), -2.0, None,
                                        ALU.mult).then_inc(s["x_neg2"], 1)

            def body(j, b, first, last):
                if not two_left(b):
                    norm(j, b + 2)
                if not last:
                    front(1 - j, b + 1)
                dve.wait_ge(s["dots"], b + 1)
                dve.wait_ge(s["ctx_norm"], b + 1)
                after(dve, s["dist"], b - 1)
                nc.vector.tensor_scalar(sq_dist[j][:, :], bank[2 + j][:, 0:P], ctx_norm[j][:, :], 0.0,
                                        ALU.add, ALU.max).then_inc(s["sq_dist"], 1)

            finish_norm_vector(core, dve, s, temps)
            norm(0, 0)
            norm(1, 1)
            front(0, 0)
            over_batches(dve, body)

        @block.gpsimd
        def _(pool):
            pool.wait_ge(s["stored0"], 16 * B // 2)
            pool.wait_ge(s["stored1"], 16 * B // 2)

        phases.close()
        distances.close()
        NQ = 4
        c = core.sems_in("L3c", [f"dist{q}" for q in range(NQ)] + [f"block{k}" for k in range(NB)] +
                         ["border", "rows", "corner", "block_done", "step", "iota", "leave", "leave_in", "enter",
                          "entry", "pathed", "path_out"])
        costs = sb("costs", [P, (R + 1) * W])
        low_b, up, not_left = (dist_buf[:, i * R * P:(i + 1) * R * P].rearrange("p (r j) -> p r j", r=R)
                               for i in range(3))
        left, diag, path = (dist_buf[:, 3 * R * P + i * R * W:3 * R * P + (i + 1) * R * W]
                            .rearrange("p (r j) -> p r j", r=R) for i in range(3))
        column = sb("column", [P, P])
        leave = [sb(f"leave{i}", [P, W]) for i in range(2)]
        part = [sb(f"part{i}", [P, P]) for i in range(3)]
        leave16 = sb("leave16", [B, NB, P])
        entry16 = sb("entry16", [B, NB])
        entry = sb("entry", [P, 1])
        enters = sb("enters", [P, P])
        cost3 = cost[:, :].rearrange("b (i j) -> b i j", j=W)
        costs3 = costs[:, :].rearrange("p (i j) -> p i j", j=W)

        block = phases.open()

        @block.sync
        def _(sp):
            rows = P // NQ
            for q in range(NQ):
                sp.dma_start(dist16[:, q * rows * P:(q + 1) * rows * P],
                             dist_dram[:, q * rows:(q + 1) * rows, :].rearrange("b i j -> b (i j)")
                             ).then_inc(c[f"dist{q}"], 16)
            for k in range(NB):
                sp.wait_ge(c["block_done"], k + 1)
                sp.dma_start(costs[k * B:(k + 1) * B, :], cost[:, k * R * W:(k * R + R + 1) * W]
                             ).then_inc(c[f"block{k}"], 16)
            sp.wait_ge(c["leave"], 1)
            for k in range(NB):
                sp.dma_start(leave16[:, k, :], leave[(R - 1) % 2][k * B:(k + 1) * B, 1:W]).then_inc(c["leave_in"], 16)
            sp.wait_ge(c["enter"], 1)
            for k in range(NB):
                sp.dma_start(entry[k * B:(k + 1) * B, :], entry16[:, k:k + 1]).then_inc(c["entry"], 16)
            sp.wait_ge(c["pathed"], 1)
            for k in range(NB):
                sp.dma_start(path_dram[:, k * R:(k + 1) * R, :], path[k * B:(k + 1) * B, :, 0:P]
                             ).then_inc(c["path_out"], 16)
            sp.wait_ge(c["path_out"], 16 * NB)

        @block.gpsimd
        def _(pool):
            nc.gpsimd.iota(column[:, :], [[1, P]], 0, 0, allow_small_or_imprecise_dtypes=True).then_inc(c["iota"], 1)
            nc.gpsimd.memset(cost[:, 0:W], BIG).then_inc(c["border"], 1)
            nc.gpsimd.memset(cost3[:, 1:W, 0], BIG).then_inc(c["border"], 1)
            for t in leave:
                nc.gpsimd.memset(t[:, 0:1], 0.0).then_inc(c["iota"], 1)
            pool.wait_ge(c["border"], 2)
            nc.gpsimd.memset(cost[:, 0:1], 0.0).then_inc(c["border"], 1)
            pool.wait_ge(c["rows"], 3)
            nc.gpsimd.memset(cost[:, 0:1], BIG).then_inc(c["corner"], 1)
            weights.on_gpsimd(pool)

        @block.scalar
        def _(act):
            weights.on_scalar(act, bank)

        @block.tensor
        def _(pe):
            weights.on_tensor(pe, bank)

        @block.vector
        def _(dve):
            def cost_row(r, done):
                above = bass.ds((r - 1) * W + 1, P)
                above_left = bass.ds((r - 1) * W, P)
                dve.wait_ge(c["rows"], done)
                nc.vector.tensor_tensor(low[:, :], cost[:, above], cost[:, above_left], ALU.min
                                        ).then_inc(c["rows"], 1)
                dve.wait_ge(c["rows"], done + 1)
                nc.vector.tensor_tensor_scan(cost[:, bass.ds(r * W + 1, P)], low[:, :],
                                             dist16[:, bass.ds((r - 1) * P, P)], BIG, ALU.min, ALU.add
                                             ).then_inc(c["rows"], 1)

            dve.wait_ge(c["border"], 3)
            dve.sem_inc(c["rows"], 1)
            for q in range(NQ):
                if q == 1:
                    weights.scales(dve, bank)
                dve.wait_ge(c[f"dist{q}"], 16)
                for k in range(2 * q, 2 * q + 2):
                    for r in range(k * R + 1, (k + 1) * R + 1):
                        cost_row(r, 2 * r - 1)
                    dve.wait_ge(c["rows"], 2 * R * (k + 1) + 1)
                    if k == 0:
                        dve.wait_ge(c["corner"], 1)
                    dve.sem_inc(c["block_done"], 1)

            link = chain(dve, c["step"], 0)
            for k in range(NB):
                dve.wait_ge(c[f"block{k}"], 16)
            dve.wait_ge(c["iota"], 3)
            for t in (left, diag, path):
                link(nc.vector.memset(t[:, :, P], 0.0))
            c_left = costs3[:, 1:R + 1, 0:P]
            c_up = costs3[:, 0:R, 1:W]
            c_diag = costs3[:, 0:R, 0:P]
            nc.vector.tensor_tensor(diag[:, :, 0:P], c_diag, c_up, ALU.is_le)
            link(nc.vector.tensor_tensor(low_b[:, :, :], c_diag, c_up, ALU.min))
            nc.vector.tensor_tensor(left[:, :, 0:P], c_left, low_b[:, :, :], ALU.is_lt)
            link(nc.vector.tensor_tensor(not_left[:, :, :], c_left, low_b[:, :, :], ALU.is_ge))
            link(nc.vector.tensor_tensor(diag[:, :, 0:P], diag[:, :, 0:P], not_left[:, :, :], ALU.mult))
            link(nc.vector.tensor_tensor(up[:, :, :], not_left[:, :, :], diag[:, :, 0:P], ALU.subtract))

            link(nc.vector.tensor_tensor(part[0][:, :], column[:, :], not_left[:, 0, :], ALU.mult))
            link(nc.vector.tensor_tensor(part[2][:, :], part[0][:, :], diag[:, 0, 0:P], ALU.subtract))
            for r in range(R):
                if r:
                    above = leave[(r - 1) % 2]
                    nc.vector.tensor_tensor(part[0][:, :], diag[:, r, 0:P], above[:, 0:P], ALU.mult)
                    link(nc.vector.tensor_tensor(part[1][:, :], up[:, r, :], above[:, 1:W], ALU.mult))
                    link(nc.vector.tensor_tensor(part[2][:, :], part[0][:, :], part[1][:, :], ALU.add))
                link(nc.vector.tensor_tensor_scan(leave[r % 2][:, 1:W], left[:, r, 0:P], part[2][:, :], 0.0,
                                                  ALU.mult, ALU.add))
            dve.sem_inc(c["leave"], 1)

            link(nc.vector.memset(entry16[:, NB - 1:NB], float(P - 1)))
            dve.wait_ge(c["leave_in"], 16 * NB)
            for k in range(NB - 1, 0, -1):
                link(nc.vector.scalar_tensor_tensor(low[:, :], column[0:B, :], entry16[:, k:k + 1], leave16[:, k, :],
                                                    ALU.is_equal, ALU.mult, accum_out=entry16[:, k - 1:k]))
            dve.sem_inc(c["enter"], 1)

            dve.wait_ge(c["entry"], 16 * NB)
            link(nc.vector.tensor_scalar(enters[:, :], column[:, :], entry[:, :], None, ALU.is_equal))
            for r in range(R - 1, -1, -1):
                link(nc.vector.tensor_tensor_scan(path[:, r, 0:P][:, ::-1], left[:, r, 1:W][:, ::-1],
                                                  enters[:, :][:, ::-1], 0.0, ALU.mult, ALU.add))
                if r:
                    nc.vector.tensor_tensor(part[0][:, :], path[:, r, 1:W], diag[:, r, 1:W], ALU.mult)
                    link(nc.vector.tensor_tensor(part[1][:, :], path[:, r, 0:P], up[:, r, :], ALU.mult))
                    link(nc.vector.tensor_tensor(enters[:, :], part[0][:, :], part[1][:, :], ALU.add))
            dve.sem_inc(c["pathed"], 1)

        q = core.sems_in("L3p", ["ctx_in0", "ctx_in1", "path_in0", "path_in1", "passed", "out", "updated"])
        path_in = [sb(f"path_in{j}", [P, P]) for j in range(2)]
        block = phases.open()

        @block.sync
        def _(sp):
            def body(j, b, first, last):
                if not isinstance(b, int):
                    sp.wait_ge(q["out"], b - 1)
                    settle(sp, q["passed"])
                sp.dma_start(ctx_in[j][:, :], one(ins["ctx_1024"], b)).then_inc(q[f"ctx_in{j}"], 16)
                sp.dma_start(path_in[j][:, :], one(path_dram, b)).then_inc(q[f"path_in{j}"], 16)

            load_batches(sp, body)

        @block.tensor
        def _(pe):
            def body(j, b, first, last):
                pe.wait_ge(q[f"ctx_in{j}"], loads(b, j))
                pe.wait_ge(q[f"path_in{j}"], loads(b, j))
                after(pe, q["updated"], b - 1)
                nc.tensor.matmul(bank[j][:, 0:D], path_in[j][:, :], ctx_in[j][:, :], start=True, stop=True
                                 ).then_inc(q["out"], 1)

            over_batches(pe, body)

        @block.vector
        def _(dve):
            def body(j, b, first, last):
                dve.wait_ge(q["out"], b + 1)
                nc.vector.scalar_tensor_tensor(cols(core.x, b * D, D), bank[j][:, 0:D], core.gate(3, 0),
                                               cols(core.x, b * D, D), ALU.mult, ALU.add).then_inc(q["updated"], 1)
                dve.wait_ge(q["updated"], b + 1)
                take_stats(core, b)

            over_batches(dve, body)

        phases.close()


L1_EXPERTS = dict(tag="L1f", layer=1, experts=8, picks=1, hidden=1024, gated=False, router="L1_ffn_gate_w")
L2_EXPERTS = dict(tag="L2f", layer=2, experts=16, picks=4, hidden=256, gated=True, router="L2_ffn_router_w")


def choose_best(core, dve, link, s, t, logits):
    nc = core.nc
    E = 8
    wide = [P, B, E]
    a, b, c = t["a"], t["b"], t["c"]
    top, total, best = t["col"][0], t["col"][1], t["col"][2]
    link(nc.vector.tensor_reduce(top, logits, AX.X, ALU.max))
    nc.vector.tensor_tensor(a, logits, top[:, :, None].to_broadcast(wide), ALU.subtract).then_inc(s["for_act"], 1)
    link(nc.vector.tensor_tensor(c, logits, top[:, :, None].to_broadcast(wide), ALU.is_equal))
    link(nc.vector.tensor_tensor(c, c, t["countdown"][:, None, :].to_broadcast(wide), ALU.mult))
    link(nc.vector.tensor_reduce(best, c, AX.X, ALU.max))
    link(nc.vector.tensor_tensor(t["chosen"], c, best[:, :, None].to_broadcast(wide), ALU.is_equal))
    dve.wait_ge(s["from_act"], 1)
    link(nc.vector.tensor_reduce(total, b, AX.X, ALU.add))
    link(nc.vector.reciprocal(total, total))
    link(nc.vector.tensor_scalar(total, total, core.gate(1, 1), None, ALU.mult))
    link(nc.vector.tensor_tensor(t["share"], t["chosen"], total[:, :, None].to_broadcast(wide), ALU.mult))


def choose_in_groups(core, dve, link, s, t, logits):
    nc = core.nc
    E, NG, TOP = 16, 4, 4
    wide = [P, B, E]
    a, scores, c = t["a"], t["b"], t["c"]
    dve.wait_ge(s["from_act"], 1)
    link(nc.vector.tensor_tensor(a, scores, t["bias"][:, None, :].to_broadcast(wide), ALU.add))
    member = t["a2"].rearrange("p (n i) -> p n i", i=4)
    gs, pair = t["group"][0], t["group"][1]
    first = True
    for i in range(4):
        for k in range(i + 1, 4):
            if first:
                link(nc.vector.tensor_tensor(gs, member[:, :, i], member[:, :, k], ALU.add))
            else:
                link(nc.vector.tensor_tensor(pair, member[:, :, i], member[:, :, k], ALU.add))
                link(nc.vector.tensor_tensor(gs, gs, pair, ALU.max))
            first = False
    by_g = gs.rearrange("p (b g) -> p b g", g=NG)
    rank = t["group"][2].rearrange("p (b g) -> p b g", g=NG)
    link(nc.vector.memset(t["group"][2], 0.0))
    for g in range(NG):
        for o in range(NG):
            if o != g:
                link(nc.vector.tensor_tensor(t["col"][0], by_g[:, :, o], by_g[:, :, g],
                                             ALU.is_ge if o < g else ALU.is_gt))
                link(nc.vector.tensor_tensor(rank[:, :, g], rank[:, :, g], t["col"][0], ALU.add))
    link(nc.vector.tensor_scalar(t["group"][2], t["group"][2], 2.0, None, ALU.is_lt))
    link(nc.vector.tensor_scalar(t["group"][1], t["group"][2], 1.0, None, ALU.subtract))
    in_group = t["group"][2][:, :, None].to_broadcast([P, B * NG, 4])
    off_group = t["group"][1][:, :, None].to_broadcast([P, B * NG, 4])
    link(nc.vector.tensor_tensor(member, member, in_group, ALU.mult))
    link(nc.vector.tensor_tensor(member, member, off_group, ALU.add))
    for b in range(B):
        last = nc.vector.max(t["sorted"][:, b * 8:b * 8 + 8], t["a2"][:, b * E:(b + 1) * E])
    link(last)
    fourth = t["sorted"].rearrange("p (b k) -> p b k", k=8)[:, :, TOP - 1:TOP].to_broadcast(wide)
    link(nc.vector.tensor_tensor(c, a, fourth, ALU.is_equal))
    link(nc.vector.tensor_tensor(t["chosen"], a, fourth, ALU.is_gt))
    link(nc.vector.tensor_reduce(t["col"][0], t["chosen"], AX.X, ALU.add))
    link(nc.vector.tensor_tensor_scan(t["a2"], t["restart_e2"], t["c2"], 0.0, ALU.mult, ALU.add))
    link(nc.vector.tensor_tensor(a, a, t["col"][0][:, :, None].to_broadcast(wide), ALU.add))
    link(nc.vector.tensor_scalar(a, a, float(TOP), None, ALU.is_le))
    link(nc.vector.tensor_tensor(c, c, a, ALU.mult))
    link(nc.vector.tensor_tensor(t["chosen"], t["chosen"], c, ALU.add))
    link(nc.vector.tensor_tensor(t["share"], scores, t["chosen"], ALU.mult))
    link(nc.vector.tensor_reduce(t["col"][0], t["share"], AX.X, ALU.add))
    link(nc.vector.tensor_scalar(t["col"][0], t["col"][0], 1e-20, None, ALU.add))
    link(nc.vector.reciprocal(t["col"][0], t["col"][0]))
    link(nc.vector.tensor_scalar(t["col"][0], t["col"][0], 2.5, core.gate(2, 1), ALU.mult, ALU.mult))
    link(nc.vector.tensor_tensor(t["share"], t["share"], t["col"][0][:, :, None].to_broadcast(wide), ALU.mult))


class ExpertLoads:

    def __init__(self, core, spec, ctx):
        self.core, self.spec = core, spec
        tag, E, K, F = spec["tag"], spec["experts"], spec["picks"], spec["hidden"]
        sb = core.sbuf_in(ctx)
        self.tiles = (B * P * K + E * (P - 1)) // P
        self.tiles += self.tiles % 2
        self.up_ahead = not spec["gated"]
        if self.up_ahead:
            self.w_up = sb(f"{tag}_w_up", [P, E * KT * F])
        self.w_down = sb(f"{tag}_w_down", [P, E * (F // P) * D])
        self.zeros_scope = ctx.enter_context(ExitStack())
        self.zeros = core.sbuf_in(self.zeros_scope)(f"{tag}_zeros", [P, self.tiles * D // B])
        self.sorted_dram = core.nc.dram_tensor(f"{tag}_sorted", (self.tiles * P, D), F32, kind="Internal").ap()
        self.sems = core.sems_in(tag, ["zeros", "ahead"])
        self.total = 16 * B * (3 if self.up_ahead else 2)

    def all_in(self, sp):
        sp.wait_ge(self.sems["ahead"], self.total)

    def make_zeros(self):
        self.core.nc.gpsimd.memset(self.zeros[:, :], 0.0).then_inc(self.sems["zeros"], 1)

    def part(self, sp, b):
        ins, loaded = self.core.ins, self.sems["ahead"]
        E, F = self.spec["experts"], self.spec["hidden"]
        flat = self.sorted_dram.rearrange("t d -> (t d)").rearrange("(i p r) -> i p r", i=B, p=P)
        sp.dma_start(one(flat, b), self.zeros[:, :]).then_inc(loaded, 16)
        if self.up_ahead:
            sp.dma_start(cols(self.w_up, b * F, F), one(ins["L1_ffn_w1"].rearrange("e (k p) f -> (e k) p f", p=P), b)
                         ).then_inc(loaded, 16)
            down = ins["L1_ffn_w2"].rearrange("e (h m p) d -> (e h) p m d", h=B // E, p=P)
        else:
            down = ins["L2_ffn_down_w"].rearrange("e (m p) d -> e p m d", p=P)
        per = E * F // P // B
        sp.dma_start(cols(self.w_down, b * (per * D), per * D).rearrange("p (m d) -> p m d", d=D),
                     down[bass.ds(b, 1)].rearrange("a p m d -> (a p) m d")).then_inc(loaded, 16)


def routed_experts(core, spec, ahead):
    nc, ins = core.nc, core.ins
    tag, E, K, F, gated = spec["tag"], spec["experts"], spec["picks"], spec["hidden"], spec["gated"]
    FT = F // P
    UP = 2 * F if gated else F
    S = ahead.tiles
    N = B * E
    SH = 512
    with ExitStack() as ctx:
        sb = core.sbuf_in(ctx)
        w_up = ahead.w_up if ahead.up_ahead else sb(f"{tag}_w_up", [P, E * KT * UP])
        w_down, sorted_dram = ahead.w_down, ahead.sorted_dram
        if gated:
            sh_gu = sb("sh_gu", [P, 2, KT, SH])
            sh_down = sb("sh_down", [P, SH // P, D])
            bias = sb("router_bias", [P, E])
        else:
            b1 = sb("expert_b1", [P, E * FT])
            b2 = sb("expert_b2", [P, E * D])
        row_int = sb(f"{tag}_row_int", [P, K * B], U32)
        pick_share = sb(f"{tag}_pick_share", [P, K * B])
        tile_expert = sb(f"{tag}_tile_expert", [P, S], I32)
        xn = [sb(f"{tag}_xn{j}", [P, D]) for j in range(2)]
        xT = [sb(f"{tag}_xT{j}", [P, D]) for j in range(2)]

        if gated:
            hT = [sb(f"{tag}_hT{j}", [P, SH]) for j in range(2)]
            gate_h = [sb(f"{tag}_gate_h{j}", [P, SH]) for j in range(2)]
        routing = ctx.enter_context(ExitStack())
        sr = core.sbuf_in(routing)
        router = sr(f"{tag}_router", [P, KT, E])
        temps = sr(f"{tag}_temps", [P, 4, B])
        logits = sr(f"{tag}_logits", [P, N])
        chosen = sr(f"{tag}_chosen", [P, N])
        share = sr(f"{tag}_share", [P, N])
        abc = [sr(f"{tag}_work{i}", [P, N]) for i in range(3)]
        small = sr(f"{tag}_small", [P, 3, B])
        if gated:
            group = sr(f"{tag}_group", [P, 3, 4 * B])
            best8 = sr(f"{tag}_best8", [P, 8 * B])
        restart_b = sr(f"{tag}_restart_b", [P, N])
        restart_e = sr(f"{tag}_restart_e", [P, N])
        countdown = sr(f"{tag}_countdown", [P, E])
        per_e = sr(f"{tag}_per_e", [P, 4, E])
        tile_no = sr(f"{tag}_tile_no", [P, S])
        tile_e = sr(f"{tag}_tile_e", [P, S])
        tile_cmp = sr(f"{tag}_tile_cmp", [P, S * E])
        before = sr(f"{tag}_before", [P, P])
        row = sr(f"{tag}_row", [P, K, B])
        late = [sr(f"{tag}_late{j}", [P, D]) for j in range(2)]
        bank = core.banks_in(ctx, tag)
        y_dram = nc.dram_tensor(f"{tag}_y_sorted", (S * P, D), F32, kind="Internal").ap()
        s = core.sems_in(f"{tag}r", NORM_SEMS + ["router", "xn", "T", "T_out", "logits", "logits_out", "w_up",
                                                 "extra", "consts", "filled"])
        phases = Phases(nc)

        block = phases.open()

        @block.sync
        def _(sp):
            for k in range(KT):
                sp.dma_start(router[:, k, :], ins[spec["router"]][:, k * P:(k + 1) * P].rearrange("e p -> p e"),
                             allow_slow_non_contiguous=True).then_inc(s["router"], 16)
            if gated:
                sp.dma_start(bias[:, :], ins["L2_ffn_bias"].rearrange("(a n) -> a n", a=1).to_broadcast([P, E])
                             ).then_inc(s["router"], 16)
                for u, name in enumerate(("L2_ffn_sh_gate_w", "L2_ffn_sh_up_w")):
                    sp.dma_start(sh_gu[:, u, :, :], ins[name].rearrange("(k p) f -> p k f", p=P)
                                 ).then_inc(s["extra"], 16)
                sp.dma_start(sh_down[:, :, :], ins["L2_ffn_sh_down_w"].rearrange("(m p) d -> p m d", p=P)
                             ).then_inc(s["extra"], 16)
            if gated:
                up4 = w_up[:, :].rearrange("p (e k u f) -> p e k u f", e=E, k=KT, u=2)
                for u, name in enumerate(("L2_ffn_gate_w", "L2_ffn_up_w")):
                    for k in range(KT):
                        sp.dma_start(up4[:, :, k, u, :], ins[name][:, k * P:(k + 1) * P, :].rearrange("e p f -> p e f")
                                     ).then_inc(s["w_up"], 16)
            else:
                sp.dma_start(b2[:, :], ins["L1_ffn_b2"].rearrange("(a e) d -> a (e d)", a=1).to_broadcast([P, E * D])
                             ).then_inc(s["extra"], 16)
                sp.dma_start(b1[:, :], ins["L1_ffn_b1"].rearrange("e (m p) -> p (e m)", p=P),
                             allow_slow_non_contiguous=True).then_inc(s["extra"], 16)
        n_extra = 3 if gated else 2

        @block.gpsimd
        def _(pool):
            nc.gpsimd.iota(countdown[:, :], [[-1, E]], E, 0, allow_small_or_imprecise_dtypes=True
                           ).then_inc(s["consts"], 1)
            nc.gpsimd.iota(tile_no[:, :], [[1, S]], 0, 0, allow_small_or_imprecise_dtypes=True
                           ).then_inc(s["consts"], 1)
            for t in (restart_b, restart_e, before):
                nc.gpsimd.memset(t[:, :], 1.0).then_inc(s["filled"], 1)
            pool.wait_ge(s["filled"], 3)
            nc.gpsimd.memset(restart_b[:, :].rearrange("p (e b) -> p e b", e=E)[:, :, 0], 0.0).then_inc(s["consts"], 1)
            nc.gpsimd.memset(restart_e[:, :].rearrange("p (b e) -> p b e", e=E)[:, :, 0], 0.0).then_inc(s["consts"], 1)
            nc.gpsimd.affine_select(out=before[:, :], in_=before[:, :], compare_op=ALU.is_gt, fill=0.0, base=0,
                                    pattern=[[1, P]], channel_multiplier=-1).then_inc(s["consts"], 1)

        @block.tensor
        def _(pe):
            def transposed(j, b):
                pe.wait_ge(s["xn"], b + 1)
                after(pe, s["T_out"], b - 1)
                for k in range(KT):
                    t = nc.tensor.transpose(bank[j][:, k * P:(k + 1) * P], xn[j][:, k * P:(k + 1) * P],
                                            core.ident[:, :])
                t.then_inc(s["T"], 1)

            def body(j, b, first, last):
                if not last:
                    transposed(1 - j, b + 1)
                pe.wait_ge(s["T_out"], b + 1)
                after(pe, s["logits_out"], b - 1)
                for k in range(KT):
                    t = nc.tensor.matmul(bank[2 + j][:, 0:E], xT[j][:, k * P:(k + 1) * P], router[:, k, :],
                                         start=(k == 0), stop=(k == KT - 1))
                t.then_inc(s["logits"], 1)

            pe.wait_ge(s["router"], 48 if gated else 32)
            transposed(0, 0)
            over_batches(pe, body)

        @block.scalar
        def _(act):
            def body(j, b, first, last):
                act.wait_ge(s["T"], b + 1)
                after(act, s["logits"], b - 1)
                nc.scalar.copy(xT[j][:, :], bank[j][:, 0:D]).then_inc(s["T_out"], 1)

            finish_norm_scalar(core, act, s, temps)
            over_batches(act, body)

        @block.vector
        def _(dve):
            def norm(j, b):
                after(dve, s["T"], b - 1)
                normalise(core, xn[j][:, :], b).then_inc(s["xn"], 1)

            def body(j, b, first, last):
                if not two_left(b):
                    norm(j, b + 2)
                dve.wait_ge(s["logits"], b + 1)
                nc.vector.tensor_copy(cols(logits, b * E, E), bank[2 + j][:, 0:E]).then_inc(s["logits_out"], 1)

            finish_norm_vector(core, dve, s, temps)
            norm(0, 0)
            norm(1, 1)
            over_batches(dve, body)

        m = core.sems_in(f"{tag}m", ["for_act", "from_act", "chosen", "counted", "step"])
        block = phases.open()

        @block.scalar
        def _(act):
            if gated:
                nc.scalar.activation(abc[1][:, :], logits[:, :], ACT.Sigmoid).then_inc(m["from_act"], 1)
            else:
                act.wait_ge(m["for_act"], 1)
                nc.scalar.activation(abc[1][:, :], abc[0][:, :], ACT.Exp).then_inc(m["from_act"], 1)

        @block.tensor
        def _(pe):
            pe.wait_ge(m["chosen"], 1)
            nc.tensor.matmul(bank[0][:, 0:N], before[:, :], chosen[:, :], start=True, stop=True)
            nc.tensor.matmul(bank[1][:, 0:N], core.ones[:, :], chosen[:, :], start=True, stop=True
                             ).then_inc(m["counted"], 1)

        @block.vector
        def _(dve):
            link = chain(dve, m["step"], 0)

            def be(t):
                return t[:, :].rearrange("p (b e) -> p b e", e=E)

            def eb(t):
                return t[:, :].rearrange("p (e b) -> p e b", e=E)

            views = dict(a=be(abc[0]), b=be(abc[1]), c=be(abc[2]), a2=abc[0][:, :], c2=abc[2][:, :],
                         chosen=be(chosen), share=be(share), countdown=countdown[:, :],
                         col=[small[:, i, :] for i in range(3)], restart_e2=restart_e[:, :])
            if gated:
                views.update(group=[group[:, i, :] for i in range(3)], sorted=best8[:, :], bias=bias[:, :])
            (choose_in_groups if gated else choose_best)(core, dve, link, m, views, be(logits))
            dve.sem_inc(m["chosen"], 1)
            dve.wait_ge(m["counted"], 1)
            total, cum = abc[0], abc[1]
            link(nc.vector.tensor_copy(eb(total), bank[1][:, 0:N].rearrange("p (b e) -> p e b", e=E)))
            link(nc.vector.tensor_tensor_scan(cum[:, :], restart_b[:, :], total[:, :], 0.0, ALU.mult, ALU.add))
            count, tiles, end, first = (per_e[:, i, :] for i in range(4))
            link(nc.vector.tensor_scalar(tiles, eb(cum)[:, :, B - 1], 1.0 / P, 63.5 / P, ALU.mult, ALU.add))
            link(nc.vector.tensor_scalar(tiles, tiles, MAGIC, None, ALU.add))
            link(nc.vector.tensor_scalar(tiles, tiles, -MAGIC, None, ALU.add))
            link(nc.vector.tensor_tensor_scan(end, core.ones[:, 0:E], tiles, 0.0, ALU.mult, ALU.add))
            link(nc.vector.tensor_tensor(first, end, tiles, ALU.subtract))
            link(nc.vector.tensor_scalar(first, first, float(P), None, ALU.mult))
            link(nc.vector.tensor_tensor(cum[:, :], cum[:, :], total[:, :], ALU.subtract))
            link(nc.vector.tensor_tensor(eb(cum), eb(cum), first[:, :, None].to_broadcast([P, E, B]), ALU.add))
            link(nc.vector.tensor_tensor(be(total), cum[:, :].rearrange("p (e b) -> p b e", e=E),
                                         bank[0][:, 0:N].rearrange("p (b e) -> p b e", e=E), ALU.add))
            place = total
            if K > 1:
                order, one_pick = abc[1], abc[2]
                link(nc.vector.tensor_tensor_scan(order[:, :], restart_e[:, :], chosen[:, :], 0.0, ALU.mult, ALU.add))
            for k in range(K):
                if K > 1:
                    link(nc.vector.scalar_tensor_tensor(one_pick[:, :], order[:, :], float(k + 1), chosen[:, :],
                                                        ALU.is_equal, ALU.mult))
                else:
                    one_pick = chosen
                link(nc.vector.tensor_tensor(logits[:, :], one_pick[:, :], place[:, :], ALU.mult))
                link(nc.vector.tensor_reduce(row[:, k, :], be(logits), AX.X, ALU.add))
                link(nc.vector.tensor_tensor(logits[:, :], one_pick[:, :], share[:, :], ALU.mult))
                link(nc.vector.tensor_reduce(pick_share[:, k * B:(k + 1) * B], be(logits), AX.X, ALU.add))
            nc.vector.tensor_copy(row_int[:, :], row[:, :, :].rearrange("p k b -> p (k b)"))
            link(nc.vector.tensor_tensor(tile_cmp[:, :].rearrange("p (t e) -> p t e", e=E),
                                         tile_no[:, :, None].to_broadcast([P, S, E]),
                                         end[:, None, :].to_broadcast([P, S, E]), ALU.is_ge))
            link(nc.vector.tensor_reduce(tile_e[:, :], tile_cmp[:, :].rearrange("p (t e) -> p t e", e=E), AX.X, ALU.add))
            nc.vector.tensor_scalar(tile_expert[:, :], tile_e[:, :], float(E - 1), None, ALU.min)

        def shared_expert(block, c):

            @block.tensor
            def _(pe):
                def front(j, i):
                    pe.wait_ge(c["xn"], i + 1)
                    after(pe, c["T_out"], i)
                    for k in range(KT):
                        t = nc.tensor.transpose(bank[0][:, k * P:(k + 1) * P], xn[j][:, k * P:(k + 1) * P],
                                                core.ident[:, :])
                    t.then_inc(c["T"], 1)
                    pe.wait_ge(c["T_out"], i + 1)
                    after(pe, c["h"], i - 1)
                    for u in range(2):
                        for m in range(SH // P):
                            for k in range(KT):
                                t = nc.tensor.matmul(bank[2 + 2 * j + u][:, m * P:(m + 1) * P],
                                                     sh_gu[:, u, k, m * P:(m + 1) * P], xT[j][:, k * P:(k + 1) * P],
                                                     start=(k == 0), stop=(k == KT - 1))
                    t.then_inc(c["up"], 1)

                def body(j, i, first, last):
                    if not last:
                        front(1 - j, i + 1)
                    pe.wait_ge(c["h"], i + 1)
                    after(pe, c["updated"], i - 1)
                    for k in range(SH // P):
                        t = nc.tensor.matmul(bank[6 + j][:, 0:D], hT[j][:, k * P:(k + 1) * P], sh_down[:, k, :],
                                             start=(k == 0), stop=(k == SH // P - 1))
                    t.then_inc(c["down"], 1)

                pe.wait_ge(s["extra"], 16 * n_extra)
                front(0, 0)
                over_batches(pe, body, HALF)

            @block.scalar
            def _(act):
                def front(j, i):
                    act.wait_ge(c["T"], i + 1)
                    after(act, c["up"], i - 1)
                    nc.scalar.copy(xT[j][:, :], bank[0][:, 0:D]).then_inc(c["T_out"], 1)
                    act.wait_ge(c["up"], i + 1)
                    after(act, c["h"], i - 1)
                    nc.scalar.activation(gate_h[j][:, :], bank[2 + 2 * j][:, :], ACT.Silu).then_inc(c["silu"], 1)

                def body(j, i, first, last):
                    if not last:
                        front(1 - j, i + 1)

                front(0, 0)
                over_batches(act, body, HALF)

        def shared_gated(dve, c, j, i):
            dve.wait_ge(c["silu"], i + 1)
            after(dve, c["down"], i - 1)
            nc.vector.tensor_tensor(hT[j][:, :], gate_h[j][:, :], bank[3 + 2 * j][:, :], ALU.mult
                                    ).then_inc(c["h"], 1)

        def shared_update(dve, c, j, i, b):
            dve.wait_ge(c["down"], i + 1)
            nc.vector.scalar_tensor_tensor(cols(core.x, b * D, D), bank[6 + j][:, 0:D],
                                           core.gate(spec["layer"], 1), cols(core.x, b * D, D),
                                           ALU.mult, ALU.add).then_inc(c["updated"], 1)

        HALF = B // 2
        SHARED_SEMS = ["xn", "T", "T_out", "up", "silu", "h", "down", "updated"]
        c = core.sems_in(f"{tag}c", SHARED_SEMS + ["late", "sent0", "sent1", "late_sent0", "late_sent1"])
        block = phases.open()

        @block.gpsimd
        def _(pool):
            def send(b, src, sem):
                for k in range(K):
                    pool.indirect_dma_start(
                        out=sorted_dram[:, :],
                        out_offset=bass.IndirectOffsetOnAxis(ap=row_int[:, k * B + b:k * B + b + 1], axis=0),
                        in_=src[:, :], in_offset=None).then_inc(sem, 16)

            for i in range(HALF):
                pool.wait_ge(c["xn"], i + 1)
                send(i, xn[i % 2], c[f"sent{i % 2}"])
                pool.wait_ge(c["late"], i + 1)
                send(HALF + i, late[i % 2], c[f"late_sent{i % 2}"])
            for j in range(2):
                pool.wait_ge(c[f"sent{j}"], 16 * K * HALF // 2)
                pool.wait_ge(c[f"late_sent{j}"], 16 * K * HALF // 2)

        if gated:
            shared_expert(block, c)

        @block.vector
        def _(dve):
            def sent(name, j, i):
                if not (isinstance(i, int) and i < 2):
                    dve.wait_ge(c[f"{name}{j}"], (i - j) * (8 * K))

            def front(j, i):
                sent("sent", j, i)
                if gated:
                    after(dve, c["T"], i - 1)
                normalise(core, xn[j][:, :], i).then_inc(c["xn"], 1)
                sent("late_sent", j, i)
                normalise(core, late[j][:, :], i + HALF).then_inc(c["late"], 1)
                if gated:
                    shared_gated(dve, c, j, i)

            def body(j, i, first, last):
                if not last:
                    front(1 - j, i + 1)
                if gated:
                    shared_update(dve, c, j, i, i)

            front(0, 0)
            over_batches(dve, body, HALF)

        phases.close()
        routing.close()
        rows = [sb(f"{tag}_rows{j}", [P, D]) for j in range(2)]
        if gated:
            y = [sb(f"{tag}_y{j}", [P, D]) for j in range(2)]
        else:
            hT = [sb(f"{tag}_hT{j}", [P, F]) for j in range(2)]
            y = xn
        w_tile = [sb(f"{tag}_w_tile{j}", [P, KT * UP]) for j in range(2)]
        q = core.sems_in(f"{tag}q", ["rows0", "rows1", "passed", "w_tile", "T", "T_out", "up", "silu", "h",
                                     "h_act", "down", "y", "stored0", "stored1"])
        block = phases.open()

        def dram_rows(ap, t):
            return ap[bass.ds(t * P, P), :]

        @block.sync
        def _(sp):
            def load(j, t):
                sp.dma_start(rows[j][:, :], dram_rows(sorted_dram, t)).then_inc(q[f"rows{j}"], 16)

            def body(j, t, first, last):
                if not (isinstance(t, int) and t + 2 >= S):
                    sp.wait_ge(q["T"], t + 1)
                    settle(sp, q["passed"])
                    load(j, t + 2)
                sp.wait_ge(q["y"], t + 1)
                settle(sp, q["passed"])
                sp.dma_start(dram_rows(y_dram, t), y[j][:, :]).then_inc(q[f"stored{j}"], 16)

            load(0, 0)
            load(1, 1)
            over_batches(sp, body, S)
            for j in range(2):
                sp.wait_ge(q[f"stored{j}"], 16 * S // 2)

        def expert_of(eng, t):
            return eng.value_load(tile_expert[0:1, bass.ds(t, 1)], min_val=0, max_val=E - 1)

        def products(j, m):
            return (bank[2 + j] if gated else bank[2 + 2 * j + m // 4])[:, m % 4 * P:(m % 4 + 1) * P]

        def rectified(eng, ops, j, t, half, sem):
            e = expert_of(eng, t)
            eng.wait_ge(q["up"], t + 1)
            after(eng, q["down"], t - 1)
            for m in range(4 * half, 4 * half + 4):
                dst, bias_col = hT[j][:, m * P:(m + 1) * P], cols(b1, e * FT + m, 1)
                if ops is nc.scalar:
                    x = nc.scalar.activation(dst, products(j, m), ACT.Relu, bias=bias_col)
                else:
                    x = nc.vector.tensor_scalar(dst, products(j, m), bias_col, 0.0, ALU.add, ALU.max)
            x.then_inc(sem, 1)

        @block.tensor
        def _(pe):
            def front(j, t):
                pe.wait_ge(q[f"rows{j}"], loads(t, j))
                after(pe, q["T_out"], t)
                for k in range(KT):
                    x = nc.tensor.transpose(bank[0][:, k * P:(k + 1) * P], rows[j][:, k * P:(k + 1) * P],
                                            core.ident[:, :])
                x.then_inc(q["T"], 1)
                pe.wait_ge(q["T_out"], t + 1)
                pe.wait_ge(q["w_tile"], t + 1)
                after(pe, q["h"], t - 1)
                if not gated:
                    after(pe, q["h_act"], t - 1)
                for m in range(UP // P):
                    for k in range(KT):
                        at = k * UP + m * P
                        x = nc.tensor.matmul(products(j, m), w_tile[j][:, at:at + P], xT[j][:, k * P:(k + 1) * P],
                                             start=(k == 0), stop=(k == KT - 1))
                x.then_inc(q["up"], 1)

            def body(j, t, first, last):
                if not last:
                    front(1 - j, t + 1)
                e = expert_of(pe, t)
                pe.wait_ge(q["h"], t + 1)
                if not gated:
                    pe.wait_ge(q["h_act"], t + 1)
                after(pe, q["y"], t - 1)
                for k in range(FT):
                    x = nc.tensor.matmul(bank[6 + j][:, 0:D], hT[j][:, k * P:(k + 1) * P],
                                         cols(w_down, e * (FT * D) + k * D, D), start=(k == 0), stop=(k == FT - 1))
                x.then_inc(q["down"], 1)

            front(0, 0)
            over_batches(pe, body, S)

        @block.scalar
        def _(act):
            def place_weights(j, t):
                e = expert_of(act, t)
                after(act, q["up"], t - 1)
                nc.scalar.copy(w_tile[j][:, :], cols(w_up, e * (KT * UP), KT * UP)).then_inc(q["w_tile"], 1)

            def front(j, t):
                act.wait_ge(q["T"], t + 1)
                after(act, q["up"], t - 1)
                nc.scalar.copy(xT[j][:, :], bank[0][:, 0:D]).then_inc(q["T_out"], 1)
                if gated:
                    act.wait_ge(q["up"], t + 1)
                    after(act, q["h"], t - 1)
                    nc.scalar.activation(gate_h[j][:, 0:F], bank[2 + j][:, 0:F], ACT.Silu).then_inc(q["silu"], 1)
                else:
                    rectified(act, nc.scalar, j, t, 1, q["h_act"])

            def body(j, t, first, last):
                if not last:
                    front(1 - j, t + 1)
                if not (isinstance(t, int) and t + 2 >= S):
                    place_weights(j, t + 2)

            if gated:
                act.wait_ge(s["w_up"], 16 * 2 * KT)
            act.wait_ge(s["extra"], 16 * n_extra)
            place_weights(0, 0)
            place_weights(1, 1)
            front(0, 0)
            over_batches(act, body, S)

        @block.vector
        def _(dve):
            def front(j, t):
                if gated:
                    dve.wait_ge(q["silu"], t + 1)
                    after(dve, q["down"], t - 1)
                    nc.vector.tensor_tensor(hT[j][:, 0:F], gate_h[j][:, 0:F], bank[2 + j][:, F:2 * F], ALU.mult
                                            ).then_inc(q["h"], 1)
                else:
                    rectified(dve, nc.vector, j, t, 0, q["h"])

            def body(j, t, first, last):
                if not last:
                    front(1 - j, t + 1)
                if not gated:
                    e = expert_of(dve, t)
                dve.wait_ge(q["down"], t + 1)
                if not (isinstance(t, int) and t < 2):
                    dve.wait_ge(q[f"stored{j}"], loads(t, j) - 16)
                if gated:
                    x = nc.vector.tensor_copy(y[j][:, :], bank[6 + j][:, 0:D])
                else:
                    x = nc.vector.tensor_tensor(y[j][:, :], bank[6 + j][:, 0:D], cols(b2, e * D, D), ALU.add)
                x.then_inc(q["y"], 1)

            if not gated:
                dve.wait_ge(s["extra"], 16 * n_extra)
            front(0, 0)
            over_batches(dve, body, S)

        g = core.sems_in(f"{tag}g", (SHARED_SEMS if gated else []) + ["got0", "got1", "got2", "got3", "added"])
        got = [rows[0], rows[1], y[0], y[1]]
        if gated:
            batches = [0] + [b for i in range(HALF - 1) for b in (i + 1, i + HALF)] + [B - 1]
        else:
            batches = [b for i in range(HALF) for b in (i, i + HALF)]
        order = [(b, k) for b in batches for k in range(K)]
        block = phases.open()

        @block.gpsimd
        def _(pool):
            for n, (b, k) in enumerate(order):
                after(pool, g["added"], n - 3)
                pool.indirect_dma_start(
                    out=got[n % 4][:, :], out_offset=None, in_=y_dram[:, :],
                    in_offset=bass.IndirectOffsetOnAxis(ap=row_int[:, k * B + b:k * B + b + 1], axis=0)
                ).then_inc(g[f"got{n % 4}"], 16)

        if gated:
            shared_expert(block, g)

        @block.vector
        def _(dve):
            def add_pairs(b, turn):
                for k in range(K):
                    dve.wait_ge(g[f"got{k}"], turn * 16 + 16)
                    after(dve, g["added"], turn * K + k)
                    nc.vector.scalar_tensor_tensor(cols(core.x, b * D, D), got[k][:, :],
                                                   cols(pick_share, b + k * B, 1), cols(core.x, b * D, D),
                                                   ALU.mult, ALU.add).then_inc(g["added"], 1)
                dve.wait_ge(g["added"], turn * K + K)
                take_stats(core, b)

            def normed(j, i):
                after(dve, g["T"], i - 1)
                normalise(core, xn[j][:, :], i + HALF).then_inc(g["xn"], 1)

            def body(j, i, first, last):
                if not last:
                    normed(1 - j, i + 1)
                    add_pairs(i + 1, i * 2 + 1)
                    shared_gated(dve, g, 1 - j, i + 1)
                shared_update(dve, g, j, i, i + HALF)
                dve.wait_ge(g["updated"], i + 1)
                add_pairs(i + HALF, B - 1 if last else i * 2 + 2)

            if gated:
                normed(0, 0)
                add_pairs(0, 0)
                shared_gated(dve, g, 0, 0)
                over_batches(dve, body, HALF)
            else:
                with dve.Fori(0, HALF // 2) as r:
                    for j in range(2):
                        for half in range(2):
                            dve.wait_ge(g[f"got{2 * j + half}"], r * 16 + 16)
                            b = r * 2 + (j + half * HALF)
                            nc.vector.scalar_tensor_tensor(cols(core.x, b * D, D), got[2 * j + half][:, :],
                                                           cols(pick_share, b, 1), cols(core.x, b * D, D),
                                                           ALU.mult, ALU.add).then_inc(g["added"], 1)
                            dve.wait_ge(g["added"], r * 4 + (2 * j + half + 1))
                            take_stats(core, b)

        phases.close()


def flamingo_stack(nc, ins, out):
    with ExitStack() as ctx:
        core = Core(nc, ins, out, ctx)

        def with_experts(xattn, spec):
            with ExitStack() as pair:
                ahead = ExpertLoads(core, spec, pair)
                xattn(ahead)
                ahead.zeros_scope.close()
                core.give_back_sems()
                routed_experts(core, spec, ahead)
            core.give_back_sems()

        def layer0():
            attention(core, "L0x", 0, 16, "mask_Bx1xSxS2_ik1", L0_MASK, L0_X, False)
            core.give_back_sems()
            depth_routed_block(core)
            core.give_back_sems()

        def layer3():
            with ExitStack() as pair:
                weights = TernaryWeights(core, pair)
                warped_alignment(core, weights)
                core.give_back_sems()
                weights.scratch.close()
                bit_ffn(core, weights)
            core.give_back_sems()

        layers = [
            layer0,
            lambda: with_experts(lambda ahead: bidirectional_attention(core, ahead), L1_EXPERTS),
            lambda: with_experts(lambda ahead: attention(core, "L2x", 2, 64, "mask_BxSxS2_ik0", L2_MASK, L2_X, True,
                                                         ahead), L2_EXPERTS),
            layer3,
        ]
        load_and_prepare(core)
        for layer in layers:
            layer()
        store_result(core)


_INS = ['x', 'ctx_1024', 'mask_Bx1xSxS2_ik1', 'mask_BxSxS2_ik0', 'g_xattn', 'g_ffn',
        'L0_xattn_wq', 'L0_xattn_wk', 'L0_xattn_wv', 'L0_xattn_wo', 'L0_xattn_bo',
        'L0_ffn_attention_mask', 'L0_ffn_position_ids', 'L0_ffn_router_w', 'L0_ffn_router_b',
        'L0_ffn_wq', 'L0_ffn_wk', 'L0_ffn_wv', 'L0_ffn_wo', 'L0_ffn_w1', 'L0_ffn_w2', 'L0_ffn_ln1', 'L0_ffn_ln2',
        'L1_xattn_w_sim', 'L1_xattn_b_sim', 'L1_xattn_W_qv', 'L1_xattn_b_qv',
        'L1_ffn_gate_w', 'L1_ffn_w1', 'L1_ffn_b1', 'L1_ffn_w2', 'L1_ffn_b2',
        'L2_xattn_Wq', 'L2_xattn_bq', 'L2_xattn_Wk', 'L2_xattn_bk', 'L2_xattn_Wv', 'L2_xattn_bv',
        'L2_xattn_Wo', 'L2_xattn_bo',
        'L2_ffn_router_w', 'L2_ffn_bias', 'L2_ffn_gate_w', 'L2_ffn_up_w', 'L2_ffn_down_w',
        'L2_ffn_sh_gate_w', 'L2_ffn_sh_up_w', 'L2_ffn_sh_down_w',
        'L3_ffn_w_gate', 'L3_ffn_w_up', 'L3_ffn_w_down']


def kernel(**inputs):
    import concourse.bacc as bacc
    from concourse.bass_utils import run_bass_kernel_spmd

    nc = bacc.Bacc("TRN2", target_bir_lowering=False, num_devices=1)
    arrays, ins = {}, {}
    for name in _INS:
        a = np.ascontiguousarray(inputs[name])
        arrays[f"in_{name}"] = a
        ins[name] = nc.dram_tensor(f"in_{name}", a.shape, mybir.dt.from_np(a.dtype), kind="ExternalInput").ap()
    out = nc.dram_tensor("out_x", (B, P, D), F32, kind="ExternalOutput").ap()
    flamingo_stack(nc, ins, out)
    r = run_bass_kernel_spmd(nc, [arrays], core_ids=[0])
    return r.results[0]["out_x"]
```
